# Optimizing a Trainium2 kernel written in Bass

```python
import numpy as np
import jax
import jax.numpy as jnp

def _softmax(x, axis=-1):
    return jax.nn.softmax(x, axis=axis)

def _gelu(x):
    return jax.nn.gelu(x, approximate=True)

def _silu(x):
    return jax.nn.silu(x)

def _sigmoid(x):
    return jax.nn.sigmoid(x)

def _layernorm(x, axis=-1, eps=1e-05):
    m = jnp.mean(x, axis=axis, keepdims=True)
    v = jnp.var(x, axis=axis, keepdims=True)
    return (x - m) / jnp.sqrt(v + eps)

def _scatter_add(tgt, idx, src, axis=0):
    return tgt.at[idx].add(src)

def _segment_sum(src, seg, n):
    return jax.ops.segment_sum(src, seg, n)
kernel_name = 'mk_gnn_ffn_d1_gnn_r8_1ae234'

def setup_inputs(seed: int=0):
    np.random.seed(seed)
    _w = jnp.asarray

    def _rec_inputs():
        import jax
        import jax.numpy as jnp
        _gk = jax.random.key(seed)
        x = -6.415e-05 + 1 * jax.random.normal(jax.random.fold_in(_gk, 1), (6250, 512), jnp.float32)
        src = jax.random.randint(jax.random.fold_in(_gk, 2), (100000,), 0, 6250, jnp.int32)
        dst = jnp.minimum((6250 * jax.random.uniform(jax.random.fold_in(_gk, 3), (100000,)) ** 2.0).astype(jnp.int32), 49999)
        _o = jnp.argsort(dst, stable=True)
        src = src[_o]
        dst = dst[_o]
        edge_attr_8 = 0.0012443 + 1.0001 * jax.random.normal(jax.random.fold_in(_gk, 11), (100000, 8), jnp.float32)
        return (x, src, dst, edge_attr_8)
    x, src, dst, edge_attr_8 = _rec_inputs()

    def _L0_gnn_setup():
        import jax, jax.numpy as jnp
        import numpy as np
        N = 2500
        E = 40000
        D = 512
        H = 8
        DK = D // H
        key = jax.random.key(seed)
        ks = jax.random.split(key, 12)
        x = jax.random.normal(ks[0], (N, D), jnp.float32)
        rows = jnp.sort(jax.random.randint(ks[1], (E,), 0, N))
        cols = jax.random.randint(ks[2], (E,), 0, N)
        edge_index = jnp.stack([rows, cols]).astype(jnp.int32)
        att_bias = jax.random.normal(ks[3], (E, H), jnp.float32)
        s = float(1.0 / np.sqrt(D))
        Wq = jax.random.normal(ks[4], (D, D), jnp.float32) * s
        Wk = jax.random.normal(ks[5], (D, D), jnp.float32) * s
        Wv = jax.random.normal(ks[6], (D, D), jnp.float32) * s
        Wo = jax.random.normal(ks[7], (D, D), jnp.float32) * s
        bq = jnp.zeros((D,), jnp.float32)
        bk = jnp.zeros((D,), jnp.float32)
        bv = jnp.zeros((D,), jnp.float32)
        bo = jnp.zeros((D,), jnp.float32)
        return dict(x=x, edge_index=edge_index, att_bias=att_bias, Wq=Wq, bq=bq, Wk=Wk, bk=bk, Wv=Wv, bv=bv, Wo=Wo, bo=bo)
    _L0_gnn_all = _L0_gnn_setup()
    _L0_gnn_in = {k: v for k, v in _L0_gnn_all.items() if k in ('Wq', 'bq', 'Wk', 'bk', 'Wv', 'bv', 'Wo', 'bo')}
    del _L0_gnn_all

    def _L0_ffn_setup():
        import jax, jax.numpy as jnp
        import numpy as np
        MARK_AX, OP_ADD, OP_SUB = (0, 1, 2)
        ALU_LO, ALU_HI = (16, 32)
        AX_CARRY_LO, AX_CARRY_HI = (48, 64)
        OPCODE_BASE = 80
        OUTPUT_LO, OUTPUT_HI, CARRY = (128, 144, 160)
        NIB_A, NIB_B, OP_START = (0, 1, 10)
        RESULT, CARRY_OUT = (100, 101)
        GE_POS, GE_DIM = (8, 160)
        OPC_ADD, OPC_SUB = (25, 26)
        B, S, D = (8, 512, 512)

        def _decode_nibble(x, base):
            return jnp.argmax(x[..., base:base + 16] > 0.5, axis=-1).astype(x.dtype)

        def _pipeline(h, W, b):
            for i in range(3):
                h = jnp.einsum('bspd,od->bspo', h, W[i]) + b[i]
                if i < 2:
                    h = jax.nn.relu(h)
            return h
        key = jax.random.key(seed)
        kx, k1, k2, k3, k4 = jax.random.split(key, 5)
        x_bd = jax.random.uniform(kx, (B, S, D), dtype=jnp.float32)
        Wa = jax.random.normal(k1, (3, GE_DIM, GE_DIM), dtype=jnp.float32) * 0.05
        ba = jax.random.normal(k2, (3, GE_DIM), dtype=jnp.float32) * 0.05
        Ws = jax.random.normal(k3, (3, GE_DIM, GE_DIM), dtype=jnp.float32) * 0.05
        bs = jax.random.normal(k4, (3, GE_DIM), dtype=jnp.float32) * 0.05
        return {'x_bd': x_bd, 'Wa': Wa, 'ba': ba, 'Ws': Ws, 'bs': bs}
    _L0_ffn_all = _L0_ffn_setup()
    _L0_ffn_in = {k: v for k, v in _L0_ffn_all.items() if k in ('Wa', 'ba', 'Ws', 'bs')}
    del _L0_ffn_all
    return {'x': x, 'src': src, 'dst': dst, 'edge_attr_8': edge_attr_8, 'L0_gnn_Wq': _L0_gnn_in['Wq'], 'L0_gnn_bq': _L0_gnn_in['bq'], 'L0_gnn_Wk': _L0_gnn_in['Wk'], 'L0_gnn_bk': _L0_gnn_in['bk'], 'L0_gnn_Wv': _L0_gnn_in['Wv'], 'L0_gnn_bv': _L0_gnn_in['bv'], 'L0_gnn_Wo': _L0_gnn_in['Wo'], 'L0_gnn_bo': _L0_gnn_in['bo'], 'L0_ffn_Wa': _L0_ffn_in['Wa'], 'L0_ffn_ba': _L0_ffn_in['ba'], 'L0_ffn_Ws': _L0_ffn_in['Ws'], 'L0_ffn_bs': _L0_ffn_in['bs']}

def reference(x, src, dst, edge_attr_8, L0_gnn_Wq, L0_gnn_bq, L0_gnn_Wk, L0_gnn_bk, L0_gnn_Wv, L0_gnn_bv, L0_gnn_Wo, L0_gnn_bo, L0_ffn_Wa, L0_ffn_ba, L0_ffn_Ws, L0_ffn_bs):
    import jax
    import jax.numpy as jnp

    def _L0_gnn_ref(x, edge_index, att_bias, Wq, bq, Wk, bk, Wv, bv, Wo, bo):
        import jax, jax.numpy as jnp
        import numpy as np
        N = 2500
        E = 40000
        D = 512
        H = 8
        DK = D // H
        n = x.shape[0]
        rows, cols = (edge_index[0], edge_index[1])
        q = (x @ Wq + bq).reshape(n, H, DK)
        k = (x @ Wk + bk).reshape(n, H, DK)
        v = (x @ Wv + bv).reshape(n, H, DK)
        scale = 1.0 / jnp.sqrt(jnp.asarray(DK, x.dtype))
        logits = jnp.einsum('ehd,ehd->eh', q[rows] * scale, k[cols]) + att_bias
        row_max = jax.ops.segment_max(logits, rows, num_segments=n)
        p = jnp.exp(logits - row_max[rows])
        denom = jax.ops.segment_sum(p, rows, num_segments=n)
        att = p / denom[rows]
        y = jax.ops.segment_sum(att[:, :, None] * v[cols], rows, num_segments=n)
        out = y.reshape(n, H * DK) @ Wo + bo
        return out

    def _L0_ffn_ref(x_bd, Wa, ba, Ws, bs):
        import jax, jax.numpy as jnp
        import numpy as np
        MARK_AX, OP_ADD, OP_SUB = (0, 1, 2)
        ALU_LO, ALU_HI = (16, 32)
        AX_CARRY_LO, AX_CARRY_HI = (48, 64)
        OPCODE_BASE = 80
        OUTPUT_LO, OUTPUT_HI, CARRY = (128, 144, 160)
        NIB_A, NIB_B, OP_START = (0, 1, 10)
        RESULT, CARRY_OUT = (100, 101)
        GE_POS, GE_DIM = (8, 160)
        OPC_ADD, OPC_SUB = (25, 26)
        B, S, D = (8, 512, 512)

        def _decode_nibble(x, base):
            return jnp.argmax(x[..., base:base + 16] > 0.5, axis=-1).astype(x.dtype)

        def _pipeline(h, W, b):
            for i in range(3):
                h = jnp.einsum('bspd,od->bspo', h, W[i]) + b[i]
                if i < 2:
                    h = jax.nn.relu(h)
            return h
        x = x_bd
        Bsz, seq, _ = x.shape
        x_ge = jnp.zeros((Bsz, seq, GE_POS, GE_DIM), dtype=x.dtype)
        x_ge = x_ge.at[..., 0, NIB_A].set(_decode_nibble(x, ALU_LO))
        x_ge = x_ge.at[..., 1, NIB_A].set(_decode_nibble(x, ALU_HI))
        x_ge = x_ge.at[..., 0, NIB_B].set(_decode_nibble(x, AX_CARRY_LO))
        x_ge = x_ge.at[..., 1, NIB_B].set(_decode_nibble(x, AX_CARRY_HI))
        x_ge = x_ge.at[..., :, OP_START + OPC_ADD].set(x[..., OPCODE_BASE + OPC_ADD][..., None])
        x_ge = x_ge.at[..., :, OP_START + OPC_SUB].set(x[..., OPCODE_BASE + OPC_SUB][..., None])
        mark = x[..., MARK_AX] > 0.5
        m_add = mark & (x[..., OP_ADD] > 0.5)
        m_sub = mark & ~(x[..., OP_ADD] > 0.5) & (x[..., OP_SUB] > 0.5)
        active = (m_add | m_sub).astype(x.dtype)
        y_add = _pipeline(x_ge, Wa, ba)
        y_sub = _pipeline(x_ge, Ws, bs)
        y = jnp.where(m_add[..., None, None], y_add, jnp.where(m_sub[..., None, None], y_sub, x_ge))
        res_lo = jnp.clip(jnp.round(y[..., 0, RESULT]), 0, 15).astype(jnp.int32)
        res_hi = jnp.clip(jnp.round(y[..., 1, RESULT]), 0, 15).astype(jnp.int32)
        oh_lo = jax.nn.one_hot(res_lo, 16, dtype=x.dtype) * active[..., None]
        oh_hi = jax.nn.one_hot(res_hi, 16, dtype=x.dtype) * active[..., None]
        carry = (jnp.round(y[..., 1, CARRY_OUT]) > 0.5).astype(x.dtype) * active
        out = x
        out = out.at[..., OUTPUT_LO:OUTPUT_LO + 16].add(2.0 * oh_lo)
        out = out.at[..., OUTPUT_HI:OUTPUT_HI + 16].add(2.0 * oh_hi)
        out = out.at[..., CARRY].add(carry)
        return out
    edge_index = jnp.stack([src, dst])
    x = x + _L0_gnn_ref(_layernorm(x, axis=-1), edge_index, edge_attr_8, L0_gnn_Wq, L0_gnn_bq, L0_gnn_Wk, L0_gnn_bk, L0_gnn_Wv, L0_gnn_bv, L0_gnn_Wo, L0_gnn_bo)
    x = x + _L0_ffn_ref(_layernorm(x, axis=-1)[None], L0_ffn_Wa, L0_ffn_ba, L0_ffn_Ws, L0_ffn_bs)[0]
    return x

_drawn_inputs = setup_inputs


def setup_inputs(seed=0):
    import zlib

    import numpy as np

    out = dict(_drawn_inputs(seed))
    spreads = {'L0_gnn_bq': (0.0, 0.1),
     'L0_gnn_bk': (0.0, 0.1),
     'L0_gnn_bv': (0.0, 0.1),
     'L0_gnn_bo': (0.0, 0.1)}
    factors = {}
    for name, (base, spread) in spreads.items():
        noise = np.random.default_rng([zlib.crc32(name.encode()), seed]).standard_normal(out[name].shape)
        drawn = base * np.exp(spread * noise) if base else spread * noise
        out[name] = jnp.asarray(drawn.astype(out[name].dtype))
    for name, factor in factors.items():
        out[name] = (out[name] * factor).astype(out[name].dtype)
    return out
```

```python
import concourse.bass as bass
from concourse import mybir
from contextlib import ExitStack


class Program:

    def __init__(self, nc, ctx):
        self.nc, self.ctx = nc, ctx
        self.queues = {e: [] for e in ("sync", "gpsimd", "scalar", "vector", "tensor")}
        self.sems, self.counts = {}, {}

    def token(self, stream, n):
        if stream not in self.sems:
            self.sems[stream] = self.ctx.enter_context(self.nc.semaphore("s_" + stream))
            self.counts[stream] = 0
        self.counts[stream] += n
        return (stream, self.counts[stream])

    def op(self, eng, stream, fn, *waits):
        tok = self.token(stream, 1)
        self.queues[eng].append((fn, waits, stream, 1))
        return tok

    def dma(self, eng, stream, fn, *waits):
        tok = self.token(stream, 16)
        self.queues[eng].append((fn, waits, stream, 16))
        return tok

    def plain(self, eng, fn, *waits):
        self.queues[eng].append((fn, waits, None, 0))

    def emit(self, name, eng):
        seen = {}

        def flat(ws):
            for w in ws:
                if isinstance(w, list):
                    yield from flat(w)
                elif w is not None:
                    yield w

        for fn, waits, stream, n in self.queues[name]:
            need = {}
            for s, v in flat(waits):
                need[s] = max(need.get(s, 0), v)
            for s, v in need.items():
                if seen.get(s, 0) < v:
                    eng.wait_ge(self.sems[s], v)
                    seen[s] = v
            if fn is None:
                continue
            ins = fn(eng)
            if stream is not None:
                ins.then_inc(self.sems[stream], n)


def build(nc, x, src, dst, attr, wq, bq, wk, bk, wv, bv, wo, bo, waT, ba, wsT, bs, out):
    f32, i32 = mybir.dt.float32, mybir.dt.int32
    bf16, u16 = mybir.dt.bfloat16, mybir.dt.uint16
    ALU, ACT, AX = mybir.AluOpType, mybir.ActivationFunctionType, mybir.AxisListType
    N, E, D, H = 6250, 100000, 512, 8
    W = 49
    TS = 782
    T = 832
    NB = T // 16
    REC = 10
    YW = 520
    BIG = 1.0e30
    rows_of = [min(128, N - 128 * w) for w in range(W)]

    ctx = ExitStack()
    with ctx:
        P = Program(nc, ctx)
        op, dma = P.op, P.dma

        def sb(name, shape, dt):
            return ctx.enter_context(nc.sbuf_tensor(name, shape, dt))

        def dram(name, shape, dt):
            return nc.dram_tensor(name, shape, dt, kind="Internal").ap()

        Qd = dram("q_scratch", (W * 128, D), f32)
        Kd = dram("k_scratch", (N, D), f32)
        Vd = dram("v_scratch", (N, D), f32)
        recd = dram("rec_scratch", (128 * T, REC), f32)
        loTd = dram("lo_rows", (TS * 128,), bf16)
        srcTd = dram("src_rows", (TS * 128,), u16)
        loSd = dram("lo_sorted", (T * 128,), bf16)
        sfd = dram("seg_flags", (T * 128,), bf16)
        widd = dram("tile_window", (896,), i32)

        R1 = sb("R1", [128, W * YW], f32)
        R2 = sb("R2", [128, T * REC], f32)
        R3 = sb("R3", [128, TS * REC], f32)
        rowR = sb("rowR", [128, 2, 2048], bf16)
        ident = sb("ident", [128, 128], f32)
        iotaF = sb("iotaF", [128, 128], f32)
        pidx = sb("pidx", [128, 1], f32)
        loS = sb("loS", [128, T], f32)
        dstS = sb("dstS", [128, T], i32)
        loEnd = sb("loEnd", [128, T], f32)
        widr = sb("widr", [1, T], i32)
        Mall = sb("Mall", [128, W, 8], f32)
        small = sb("small", [128, 1536], f32)
        ones = sb("ones", [1, 128], f32)
        BK = [ctx.enter_context(nc.psum_tensor(f"bk{i}", [128, 512], f32)) for i in range(8)]

        def carve(base, start=0):
            at = [start]

            def take(n, dt=f32):
                words = n if dt in (f32, i32) else (n + 1) // 2
                v = base[:, at[0]:at[0] + words]
                at[0] += words
                assert at[0] <= base.shape[1], (base.name, at[0])
                return v if dt == f32 else v.bitcast(dt)
            return take

        a = carve(R1)
        iotaI = a(128).bitcast(i32)
        pI = a(1).bitcast(i32)
        a(3)
        low = a(128)
        upp = a(128)
        onesf = a(128)
        W3 = [a(2048).rearrange("p (c n) -> p c n", c=4) for _ in range(3)]
        B3 = a(1536)
        k1 = op("gpsimd", "cst", lambda e: e.iota(iotaI, pattern=[[1, 128]], base=0, channel_multiplier=0))
        k2 = op("gpsimd", "cst", lambda e: e.iota(pI, pattern=[[0, 1]], base=0, channel_multiplier=1))
        c_iota = op("vector", "cv", lambda e: e.tensor_copy(iotaF[:, :], iotaI), k1)
        c_pidx = op("vector", "cv", lambda e: e.tensor_copy(pidx[:, :], pI), k2)
        c_id = op("vector", "cv", lambda e: e.tensor_scalar(ident[:, :], iotaF[:, :], pidx[:, 0:1], None, ALU.is_equal), c_pidx)
        c_low = op("vector", "cv", lambda e: e.tensor_scalar(low, iotaF[:, :], pidx[:, 0:1], None, ALU.is_lt))
        c_upp = op("vector", "cv", lambda e: e.tensor_scalar(upp, iotaF[:, :], pidx[:, 0:1], None, ALU.is_gt))
        c_onesf = op("vector", "cv", lambda e: e.memset(onesf, 1.0))
        c_ones = op("vector", "cv", lambda e: e.memset(ones[:, :], 1.0))

        wl = [dma("sync", f"w{n}", lambda e, n=n, w_=w_: e.dma_start(W3[n], w_.rearrange("(c p) n -> p c n", p=128)))
              for n, w_ in enumerate((wq, wk, wv))]
        srcI = a(TS).bitcast(i32)
        dstI = a(TS).bitcast(i32)
        tI = a(TS).bitcast(i32)
        srcF = a(TS)
        hiF = a(TS)
        inv = a(TS)
        rec = R3[:, :].rearrange("p (t r) -> p t r", r=REC)
        FULL = 127 * TS
        TAIL = E - FULL
        def2 = R2[:, :].rearrange("p (t r) -> p t r", r=REC)
        z1 = op("vector", "v", lambda e: e.memset(srcI[:, TAIL:TS], 8191))
        z2 = op("vector", "v", lambda e: e.memset(dstI[:, TAIL:TS], 0))
        d1 = op("gpsimd", "g", lambda e: e.memset(R2[:, :], 0.0))
        d2 = op("gpsimd", "g", lambda e: e.memset(def2[:, :, 8:9], -1.0), d1)
        t_def = dma("sync", "def", lambda e: e.dma_start(recd.rearrange("(p t) r -> p (t r)", p=128), R2[:, :]), d2)
        ls = []
        for name, t_, v_ in (("ls", srcI, src), ("ld", dstI, dst)):
            zt = z1 if name == "ls" else z2
            ls.append([dma("sync", name, lambda e, t_=t_, v_=v_: e.dma_start(t_[0:127, :], v_[0:FULL].rearrange("(p t) -> p t", t=TS)), zt),
                       dma("sync", name, lambda e, t_=t_, v_=v_: e.dma_start(t_[127:128, 0:TAIL], v_[FULL:E].rearrange("(p t) -> p t", p=1)), zt)])
        at8 = R2[:, 0:TS * 8]
        d3 = op("gpsimd", "g", lambda e: e.memset(R2[:, TAIL * 8:TS * 8], 0.0), t_def)
        la = [dma("sync", "la", lambda e: e.dma_start(at8[0:127, :], attr[0:FULL, :].rearrange("(p t) h -> p (t h)", t=TS)), d3, t_def),
              dma("sync", "la", lambda e: e.dma_start(at8[127:128, 0:TAIL * 8], attr[FULL:E, :].rearrange("(p t) h -> p (t h)", p=1)), d3, t_def)]
        r1 = op("scalar", "a", lambda e: e.copy(rec[:, :, 0:8], at8.rearrange("p (t h) -> p t h", h=8)), la)
        r2 = op("vector", "v", lambda e: e.tensor_copy(rec[:, :, 9:10].bitcast(i32), dstI.rearrange("p (t a) -> p t a", a=1)), ls[1])
        r3 = op("vector", "v", lambda e: e.tensor_copy(srcF, srcI), ls[0])
        r4 = op("vector", "v", lambda e: e.tensor_scalar(tI, srcI, 7, None, ALU.logical_shift_right))
        r5 = op("vector", "v", lambda e: e.tensor_copy(hiF, tI), r4)
        r6 = op("vector", "v", lambda e: e.scalar_tensor_tensor(rec[:, :, 8:9].rearrange("p t a -> p (t a)"), hiF, -128.0, srcF, ALU.mult, ALU.add), r5)
        r7 = op("vector", "v", lambda e: e.tensor_scalar(inv, hiF, 48.5, 1048576.0, ALU.is_gt, ALU.mult), r5)
        loF = rec[:, :, 8]

        tr = []
        stl = a(7 * 128, bf16).rearrange("p (c n) -> p c n", c=7)
        stu = a(7 * 128, u16).rearrange("p (c n) -> p c n", c=7)
        for c in range(7):
            n = min(128, TS - 128 * c)
            m1 = op("tensor", "tr", lambda e, c=c, n=n: e.transpose(BK[c % 2][0:n, 0:128], loF[:, 128 * c:128 * c + n], ident[:, :]), r6, c_id,
                    tr[-2] if c >= 2 else None)
            m2 = op("tensor", "tr", lambda e, c=c, n=n: e.transpose(BK[c % 2][0:n, 128:256], srcF[:, 128 * c:128 * c + n], ident[:, :]), r3)
            v1 = op("vector", "v", lambda e, c=c, n=n: e.tensor_copy(stl[0:n, c, :], BK[c % 2][0:n, 0:128]), m1, m2)
            v2 = op("vector", "v", lambda e, c=c, n=n: e.tensor_copy(stu[0:n, c, :], BK[c % 2][0:n, 128:256]), m2)
            tr.append(v2)
        t_rows = []
        for st, dd in ((stl, loTd), (stu, srcTd)):
            t_rows.append(dma("sync", "rw", lambda e, st=st, dd=dd: e.dma_start(dd[0:768 * 128].rearrange("(c p n) -> p c n", p=128, n=128), st[:, 0:6, :]), tr[-1]))
            t_rows.append(dma("sync", "rw", lambda e, st=st, dd=dd: e.dma_start(dd[768 * 128:TS * 128].rearrange("(p n) -> p n", n=128), st[0:14, 6, :]), tr[-1]))

        a2 = carve(R1, 6144 + 1536 + 4 + 512 + 6 * TS + 2 * 448)
        Abf = [a2(8 * 128, bf16).rearrange("p (t n) -> p t n", n=128) for _ in range(2)]
        Bbf = [a2(8 * W, bf16).rearrange("p (t n) -> p t n", n=W) for _ in range(3)]
        AT = [a2(8 * 128).rearrange("p (t n) -> p t n", n=128) for _ in range(2)]
        Cs = a2(17 * W).rearrange("p (t n) -> p t n", n=W)
        GB = a2(8 * W).rearrange("p (t n) -> p t n", n=W)
        rank = a2(2 * 8).rearrange("p (a t) -> p a t", a=2)
        psel = a2(2 * 8).rearrange("p (a t) -> p a t", a=2)
        sm = [a2(8) for _ in range(6)]
        ridx = a2(4 * 8).bitcast(i32).rearrange("p (a t) -> p a t", a=4)
        scr = a2(128)
        xin = [a2(512) for _ in range(3)]
        xT = [a2(512).rearrange("p (c n) -> p c n", c=4) for _ in range(2)]
        stg = [a2(512) for _ in range(3)]
        rowsS = [a2(1024, u16) for _ in range(3)]
        rowsL = [rowR[:, 0, 0:1024], rowR[:, 0, 1024:2048], rowR[:, 1, 0:1024]]
        NCH = (TS + 7) // 8
        chn = [min(8, TS - 8 * c) for c in range(NCH)]

        def bcast_last(ap, n, m):
            return ap.rearrange("p (t a) -> p t a", a=1).broadcast_to([128, n, m])

        def build_AB(c, slot_wait):
            n = chn[c]
            lo_c = rec[:, 8 * c:8 * c + n, 8:9].broadcast_to([128, n, 128])
            io = iotaF[:, :].rearrange("p (a n) -> p a n", a=1).broadcast_to([128, n, 128])
            ta = op("vector", "ab", lambda e: e.tensor_tensor(Abf[c % 2][:, 0:n, :], lo_c, io, ALU.is_equal), r6, c_iota, slot_wait)
            hi_c = bcast_last(hiF[:, 8 * c:8 * c + n], n, W)
            io2 = iotaF[:, 0:W].rearrange("p (a n) -> p a n", a=1).broadcast_to([128, n, W])
            tb = op("vector", "ab", lambda e: e.tensor_tensor(Bbf[c % 3][:, 0:n, :], hi_c, io2, ALU.is_equal), r5)
            return tb

        hist = []
        for c in range(NCH):
            t_ab = build_AB(c, hist[c - 2] if c >= 2 else None)
            for j in range(chn[c]):
                last = op("tensor", "hi", lambda e, c=c, j=j: e.matmul(BK[0][:, 0:W], Abf[c % 2][:, j, :], Bbf[c % 3][:, j, :],
                          start=(c == 0 and j == 0), stop=(c == NCH - 1 and j == chn[c] - 1)), t_ab, tr[-1])
            hist.append(last)
        sHt = a2(W)
        sC = a2(W)
        sTi = a2(W).bitcast(i32)
        sTf = a2(W)
        sInc = a2(W)
        z0 = a2(W)
        q1 = op("vector", "v", lambda e: e.tensor_copy(sHt, BK[0][:, 0:W]), hist[-1])
        q0 = op("vector", "v", lambda e: e.memset(z0, 0.0))
        m1 = op("tensor", "hb", lambda e: e.matmul(BK[1][:, 0:W], upp, sHt, start=True, stop=True), q1, c_upp)
        m2 = op("tensor", "hb", lambda e: e.matmul(BK[1][:, 64:64 + W], onesf, sHt, start=True, stop=True), q1, c_onesf)
        q2 = op("vector", "v", lambda e: e.tensor_scalar(sC, BK[1][:, 64:64 + W], 127.0, None, ALU.add), m2)
        q3 = op("vector", "v", lambda e: e.tensor_copy(sTi, sC), q2)
        q4 = op("vector", "v", lambda e: e.tensor_scalar(sTi, sTi, 7, None, ALU.logical_shift_right), q3)
        q5 = op("vector", "v", lambda e: e.tensor_copy(sTf, sTi), q4)
        q6 = op("vector", "v", lambda e: e.tensor_tensor_scan(sInc, z0, sTf, 0.0, ALU.add, ALU.add), q5, q0)
        q7 = op("vector", "v", lambda e: e.tensor_tensor(sC, sInc, sTf, ALU.subtract), q6)
        t_base = op("vector", "v", lambda e: e.scalar_tensor_tensor(Cs[:, 0, :], sC, 128.0, BK[1][:, 0:W], ALU.mult, ALU.add), q7, m1)
        wI = a2(7).bitcast(i32)
        wF = a2(7)
        wC = a2(7 * W).rearrange("p (c n) -> p c n", n=W)
        g1 = op("gpsimd", "g", lambda e: e.iota(wI, pattern=[[128, 7]], base=0, channel_multiplier=1))
        q8 = op("vector", "v", lambda e: e.tensor_copy(wF, wI), g1)
        q9 = op("vector", "v", lambda e: e.tensor_tensor(wC, sInc.rearrange("p (a n) -> p a n", a=1).broadcast_to([128, 7, W]),
                bcast_last(wF, 7, W), ALU.is_le), q8, q6)
        q10 = op("vector", "v", lambda e: e.tensor_reduce(wF, wC, AX.X, ALU.add), q9)
        q11 = op("vector", "v", lambda e: e.tensor_scalar(wI, wF, 48.0, None, ALU.min), q10)
        t_wd = dma("sync", "wid", lambda e: e.dma_start(widd.rearrange("(c p) -> p c", p=128), wI, allow_slow_non_contiguous=True), q11)
        t_wid = dma("sync", "wid", lambda e: e.dma_start(widr[:, :], widd[0:T].rearrange("(a t) -> a t", a=1)), t_wd)

        c_b3 = [dma("sync", f"b3{n}", lambda e, n=n, b_=b_: e.dma_start(B3[0:1, 512 * n:512 * n + 512], b_.rearrange("(a n) -> a n", a=1)))
                for n, b_ in enumerate((bq, bk, bv))]
        st6 = small[:, 0:12].rearrange("p (a n) -> p a n", a=2)
        mv = small[:, 12:16].rearrange("p (a n) -> p a n", a=2)
        rs = small[:, 16:20].rearrange("p (a n) -> p a n", a=2)
        xl, xTt, pj, stv, lnd = {}, {}, {}, {}, {}
        stored = {}
        OUTS = (Qd, Kd, Vd)

        def load_x(w):
            n = rows_of[w]
            xl[w] = dma("sync", f"x{w % 3}", lambda e: e.dma_start(xin[w % 3][0:n, :], x[128 * w:128 * w + n, :]), xTt.get((w - 3, "T")))

        def ln_stats(w, xt, n, wait, tag, slot):
            b1 = op("vector", tag, lambda e: e.bn_stats(st6[0:n, slot, :], xt), wait)
            b2 = op("vector", tag, lambda e: e.bn_aggr(mv[0:n, slot, :], st6[0:n, slot, :]), b1)
            b3 = op("vector", tag, lambda e: e.tensor_scalar(rs[0:n, slot, 0:1], mv[0:n, slot, 1:2], 1e-5, None, ALU.add), b2)
            b4 = op("scalar", tag + "a", lambda e: e.activation(rs[0:n, slot, 1:2], rs[0:n, slot, 0:1], ACT.Sqrt), b3)
            b5 = op("vector", tag, lambda e: e.reciprocal(rs[0:n, slot, 0:1], rs[0:n, slot, 1:2]), b4)
            return b5

        def proj_ln(w):
            n, xt = rows_of[w], xin[w % 3]
            b5 = ln_stats(w, xt[0:n, :], n, xl[w], "ln", w % 2)
            lnd[w] = op("vector", "ln", lambda e: e.tensor_scalar(xt[0:n, :], xt[0:n, :], mv[0:n, w % 2, 0:1], rs[0:n, w % 2, 0:1],
                        ALU.subtract, ALU.mult), b5)

        def proj_T(w):
            n, xt = rows_of[w], xin[w % 3]
            for c in range(4):
                last = op("tensor", "pt", lambda e, c=c: e.transpose(BK[3][:, 128 * c:128 * c + n], xt[0:n, 128 * c:128 * c + 128],
                          ident[0:n, 0:n]), lnd[w], xTt.get(w - 1))
            xTt[(w, "T")] = last
            xTt[w] = op("scalar", "px", lambda e: e.copy(xT[w % 2][:, :, 0:n], BK[3][:, :].rearrange("p (c n) -> p c n", c=4)[:, :, 0:n]),
                        last, pj.get((w - 2, 2)))

        def proj_M(w, m):
            n = rows_of[w]
            i = 3 * w + m
            bank = BK[4 + i % 3]
            for c in range(4):
                op("tensor", "pj", lambda e, c=c: e.matmul(bank[0:n, :], xT[w % 2][:, c, 0:n], W3[m][:, c, :], start=(c == 0), stop=False),
                   xTt[w], wl[m], stv.get(i - 3))
            pj[(w, m)] = op("tensor", "pj", lambda e: e.matmul(bank[0:n, :], ones[0:1, 0:n], B3[0:1, 512 * m:512 * m + 512], start=False, stop=True),
                            c_ones, c_b3[m])
            stv[i] = op("scalar", "ps", lambda e: e.activation(stg[i % 3][0:n, :], bank[0:n, :], ACT.Copy, scale=0.125 if m == 0 else 1.0),
                        pj[(w, m)], stored.get(i - 3))
            stored[i] = dma("sync", f"st{i % 3}", lambda e: e.dma_start(OUTS[m][128 * w:128 * w + n, :], stg[i % 3][0:n, :]), stv[i])

        proj = []
        for w in range(W):
            proj += [[lambda w=w: (proj_T(w), proj_ln(w + 1) if w + 1 < W else None, proj_M(w, 0), load_x(w + 3) if w + 3 < W else None)],
                     [lambda w=w: (proj_M(w, 1), proj_M(w, 2))]]
        for w in range(3):
            load_x(w)
        proj_ln(0)

        rowt, gsum, rk, scat, ATt, Gt, Ht, Cst = {}, {}, {}, {}, {}, {}, {}, {}
        Cst[0] = t_base
        abt = {}

        def s_rows(c):
            n = chn[c]
            rowt[c] = [dma("sync", f"rl{c % 3}", lambda e: e.dma_start(rowsL[c % 3][:, 0:128 * n], loTd[1024 * c:1024 * c + 128 * n]
                           .rearrange("(a n) -> a n", a=1).broadcast_to([128, 128 * n])), t_rows, ATt.get(c - 3)),
                       dma("sync", f"rs{c % 3}", lambda e: e.dma_start(rowsS[c % 3][:, 0:128 * n], srcTd[1024 * c:1024 * c + 128 * n]
                           .rearrange("(a n) -> a n", a=1).broadcast_to([128, 128 * n])), t_rows, rk.get(c - 3))]

        def s_front(c):
            n = chn[c]
            abt[c] = build_AB(c, [Ht.get(c - 2), hist[-1], gsum.get(c - 3)])
            for j in range(n):
                last = op("tensor", "sh", lambda e, j=j: e.matmul(BK[0][:, j * W:(j + 1) * W], Abf[c % 2][:, j, :], Bbf[c % 3][:, j, :], start=True, stop=True),
                          abt[c], q1, Cst.get(8 * c))
            Ht[c] = last
            ATt[c] = op("vector", "at", lambda e: e.tensor_scalar(AT[c % 2][:, 0:n, :], rowsL[c % 3][:, 0:128 * n].rearrange("p (t n) -> p t n", n=128),
                        pidx[:, 0:1], None, ALU.is_equal), rowt[c][0], Gt.get(c - 2), c_pidx)
            for j in range(n):
                t = 8 * c + j
                Cst[t + 1] = op("vector", "cs", lambda e, t=t, j=j: e.tensor_tensor(Cs[:, (t + 1) % 17, :], Cs[:, t % 17, :], BK[0][:, j * W:(j + 1) * W], ALU.add),
                                Ht[c], Cst[t], Gt.get(c - 2))
            for j in range(n):
                t = 8 * c + j
                Gt[c] = op("tensor", "sg", lambda e, t=t, j=j: e.matmul(BK[1 + c % 2][:, j * W:(j + 1) * W], AT[c % 2][:, j, :], Cs[:, t % 17, :], start=True, stop=True),
                           ATt[c], Cst[8 * c + n - 1] if n > 1 else Cst[8 * c], gsum.get(c - 2), q11)

        def s_back(c):
            n, k = chn[c], c % 2
            for j in range(n):
                t = 8 * c + j
                rk[c] = op("vector", "rk", lambda e, t=t, j=j: e.scalar_tensor_tensor(scr, rowsS[c % 3][:, 128 * j:128 * j + 128], srcF[:, t:t + 1], low,
                           ALU.is_equal, ALU.mult, accum_out=rank[:, k, j:j + 1]), rowt[c][1], c_low, rk.get(c if j else c - 1))
            gb = op("vector", "sv", lambda e: e.tensor_tensor(GB[:, 0:n, :], BK[1 + k][:, 0:n * W].rearrange("p (t n) -> p t n", n=W), Bbf[c % 3][:, 0:n, :], ALU.mult),
                    Gt[c], gsum.get(c - 1))
            gsum[c] = op("vector", "sv", lambda e: e.tensor_reduce(psel[:, k, 0:n], GB[:, 0:n, :], AX.X, ALU.add), gb)
            pf, pi, af, bf_, av = sm[0][:, 0:n], sm[1].bitcast(i32)[:, 0:n], sm[2][:, 0:n], sm[3][:, 0:n], sm[4][:, 0:n]
            u1 = op("vector", "sv", lambda e: e.tensor_tensor(pf, psel[:, k, 0:n], rank[:, k, 0:n], ALU.add), gsum[c], rk[c])
            u2 = op("vector", "sv", lambda e: e.tensor_copy(pi, pf), u1)
            u3 = op("vector", "sv", lambda e: e.tensor_scalar(pi, pi, 7, None, ALU.logical_shift_right), u2)
            u4 = op("vector", "sv", lambda e: e.tensor_copy(af, pi), u3)
            u5 = op("vector", "sv", lambda e: e.scalar_tensor_tensor(bf_, af, -128.0, pf, ALU.mult, ALU.add), u4)
            u6 = op("vector", "sv", lambda e: e.tensor_tensor(av, af, inv[:, 8 * c:8 * c + n], ALU.add), u4, r7)
            u7 = op("vector", "sv", lambda e: e.scalar_tensor_tensor(ridx[:, c % 4, 0:n], bf_, float(T), av, ALU.mult, ALU.add), u5, u6, scat.get(c - 4))
            for j in range(n):
                t = 8 * c + j
                scat[c] = dma("gpsimd", f"sc{c % 4}", lambda e, t=t, j=j: e.indirect_dma_start(
                    recd, bass.IndirectOffsetOnAxis(ap=ridx[:, c % 4, j:j + 1], axis=0), rec[:, t, :], None,
                    bounds_check=128 * T - 1, oob_is_err=False), u7, r1, r2, r6, t_def)

        s_rows(0)
        s_rows(1)
        s_front(0)
        for c in range(NCH):
            if c + 2 < NCH:
                s_rows(c + 2)
            if c + 1 < NCH:
                s_front(c + 1)
            s_back(c)
            for f in proj[c]:
                f()
        scat_all = [scat[c] for c in range(NCH - 4, NCH)]
        proj_all = [stored[i] for i in range(3 * W - 3, 3 * W)]
        phaseA = [pj[(W - 1, 2)], stv[3 * W - 1], gsum[NCH - 1], rk[NCH - 1]]

        Qall = R1[:, 0:W * 512].rearrange("p (w n) -> p w n", n=512)
        t_q = dma("sync", "q", lambda e: e.dma_start(Qall[:, 0:W - 1, :], Qd[0:(W - 1) * 128, :].rearrange("(w p) n -> p w n", p=128)),
                  phaseA, proj_all, scat_all)
        z3 = op("vector", "v", lambda e: e.memset(Qall[:, W - 1, :], 0.0), phaseA, proj_all, scat_all)
        t_q2 = dma("sync", "q", lambda e: e.dma_start(Qall[0:106, W - 1, :], Qd[(W - 1) * 128:N, :]), z3, phaseA, proj_all)
        t_rec = dma("sync", "rec", lambda e: e.dma_start(R2[:, :], recd.rearrange("(p t) r -> p (t r)", p=128)), scat_all, phaseA)
        L = R3[:, 0:T * 8].rearrange("p (b h t) -> p b h t", h=8, t=16)
        recS = R2[:, :].rearrange("p (b t r) -> p b t r", t=16, r=REC)
        s1 = op("vector", "v", lambda e: e.tensor_copy(loS[:, :], R2[:, :].rearrange("p (t r) -> p t r", r=REC)[:, :, 8]), t_rec)
        s2 = op("vector", "v", lambda e: e.tensor_copy(dstS[:, :], R2[:, :].rearrange("p (t r) -> p t r", r=REC)[:, :, 9].bitcast(i32)))
        s3 = op("scalar", "a", lambda e: e.copy(L.rearrange("p b h t -> p b t h"), recS[:, :, :, 0:8]), t_rec, scat_all)
        s4 = op("vector", "v", lambda e: e.memset(Mall[:, :, :], -BIG))
        loT = R3[:, T * 8:T * 8 + 896].rearrange("p (c n) -> p c n", n=128)
        loTb = small[:, 0:448].bitcast(bf16).rearrange("p (c n) -> p c n", n=128)
        sfb = small[:, 448:896].bitcast(bf16).rearrange("p (c n) -> p c n", n=128)
        en = small[:, 896:1024]
        te = []
        for c in range(7):
            n = min(128, T - 128 * c)
            m1 = op("tensor", "u", lambda e, c=c, n=n: e.transpose(BK[c % 2][0:n, 0:128], loS[:, 128 * c:128 * c + n], ident[:, :]), s1, te[c - 2] if c >= 2 else None,
                    phaseA)
            v1 = op("vector", "u2", lambda e, c=c, n=n: e.tensor_copy(loT[0:n, c, :], BK[c % 2][0:n, 0:128]), m1, s3)
            v2 = op("vector", "u2", lambda e, c=c, n=n: e.tensor_copy(loTb[0:n, c, :], loT[0:n, c, :]), v1)
            v3 = op("vector", "u2", lambda e, c=c, n=n: e.tensor_tensor(sfb[0:n, c, 1:128], loT[0:n, c, 1:128], loT[0:n, c, 0:127], ALU.is_equal), v1)
            v4 = op("vector", "u2", lambda e, c=c, n=n: e.memset(sfb[0:n, c, 0:1], 0.0))
            v5 = op("vector", "u2", lambda e, c=c, n=n: e.tensor_scalar(en[0:n, 0:127], sfb[0:n, c, 1:128], -1.0, 1.0, ALU.mult, ALU.add), v3, te[-1] if te else None)
            v6 = op("vector", "u2", lambda e, c=c, n=n: e.memset(en[0:n, 127:128], 1.0))
            v7 = op("vector", "u2", lambda e, c=c, n=n: e.scalar_tensor_tensor(en[0:n, :], loT[0:n, c, :], 1.0, en[0:n, :], ALU.add, ALU.mult), v5, v6)
            v8 = op("vector", "u2", lambda e, c=c, n=n: e.tensor_scalar(en[0:n, :], en[0:n, :], -1.0, None, ALU.add), v7)
            v9 = op("vector", "u2", lambda e, c=c, n=n: e.tensor_scalar(sfb[0:n, c, :], sfb[0:n, c, :], -1.0, BIG, ALU.add, ALU.mult), v5, v4)
            m2 = op("tensor", "u", lambda e, c=c, n=n: e.transpose(BK[c % 2][:, 128:128 + n], en[0:n, :], ident[0:n, 0:n]), v8)
            te.append(op("vector", "u2", lambda e, c=c, n=n: e.tensor_copy(loEnd[:, 128 * c:128 * c + n], BK[c % 2][:, 128:128 + n]), m2))
        t_ss = []
        for st, dd in ((loTb, loSd), (sfb, sfd)):
            t_ss.append(dma("sync", "rx", lambda e, st=st, dd=dd: e.dma_start(dd[0:768 * 128].rearrange("(c p n) -> p c n", p=128, n=128), st[:, 0:6, :]), te[-1]))
            t_ss.append(dma("sync", "rx", lambda e, st=st, dd=dd: e.dma_start(dd[768 * 128:T * 128].rearrange("(p n) -> p n", n=128), st[0:64, 6, :]), te[-1]))

        b = carve(R2)
        KR = 8
        Kr = [b(512) for _ in range(KR)]
        prod = [b(512) for _ in range(2)]
        ohT = [b(8 * 128).rearrange("p (t n) -> p t n", n=128) for _ in range(2)]
        c3 = carve(small, 0)
        sfr = [c3(128, bf16) for _ in range(2)]
        Lr = [c3(128).rearrange("p (h t) -> p h t", h=8) for _ in range(2)]
        Fs = c3(128)
        Fe = [c3(9 * 16).rearrange("p (h t) -> p h t", h=9) for _ in range(2)]
        eo = [c3(128) for _ in range(4)]
        pen = c3(16)
        fe1 = op("vector", "v", lambda e: (e.memset(Fe[0][:, 8, :], 1.0)), t_ss)
        fe2 = op("vector", "v", lambda e: (e.memset(Fe[1][:, 8, :], 1.0)))
        rt, oht, kt, qt, prt, redt, sft, lb = {}, {}, {}, {}, {}, {}, {}, {}
        clr = [s1, s2, s3]

        def regs(eng_name, tag):
            return {"r": None, "tag": tag, "eng": eng_name}

        def load_regs(st, b_, wait):
            def f(e):
                if st["r"] is None:
                    st["r"] = [e.alloc_register(f"{st['tag']}{j}") for j in range(16)]
                return e.reg_load(st["r"], widr[0:1, 16 * b_:16 * b_ + 16])
            P.plain(st["eng"], f, wait)

        def win(e, st, t):
            return e.snap(st["r"][t % 16], min_val=0, max_val=W - 1)

        def rows2(b_, store, tag, wait):
            store[b_] = dma("sync", f"{tag}{b_ % 2}", lambda e: e.dma_start(rowR[:, b_ % 2, :], loSd[2048 * b_:2048 * b_ + 2048]
                            .rearrange("(a n) -> a n", a=1).broadcast_to([128, 2048])), wait)

        def mk_ohT(h_, rtok, store, free, eng_stream):
            b_ = h_ // 2
            store[h_] = op("vector", eng_stream, lambda e: e.tensor_scalar(ohT[h_ % 2], rowR[:, b_ % 2, 1024 * (h_ % 2):1024 * (h_ % 2) + 1024]
                           .rearrange("p (t n) -> p t n", n=128), pidx[:, 0:1], None, ALU.is_equal), rtok[b_], free)

        def gather_k(t):
            kt[t] = dma("gpsimd", f"k{t % KR}", lambda e: e.indirect_dma_start(Kr[t % KR], None, Kd, bass.IndirectOffsetOnAxis(ap=dstS[:, t:t + 1], axis=0),
                        bounds_check=N - 1, oob_is_err=False), prt.get(t - KR), clr, proj_all, phaseA)

        pe1 = regs("tensor", "pw")
        dv1 = regs("vector", "dw")

        def p1_q(t):
            qt[t] = op("tensor", "q1", lambda e: e.matmul(BK[t % 3][:, :], ohT[(t // 8) % 2][:, t % 8, :], Qall[:, bass.ds(win(e, pe1, t), 1), :],
                       start=True, stop=True), oht[t // 8], prt.get(t - 3), t_q, t_q2, te[-1])

        def p1_l(t):
            b_, k = t // 16, t // 16 % 2
            prt[t] = op("vector", "pr", lambda e: e.tensor_tensor(prod[t % 2], BK[t % 3][:, :], Kr[t % KR], ALU.mult), qt[t], kt[t], redt.get(t - 2))
            redt[t] = op("vector", "rd", lambda e: e.tensor_reduce(Lr[k][:, :, t % 16], prod[t % 2].rearrange("p (h d) -> p h d", h=8), AX.X, ALU.add),
                         prt[t], lb.get(b_ - 2), t_ss)

        fet, eot, mt, mu = {}, {}, {}, {}

        def p1_b1(b_):
            k = b_ % 2
            lb[b_] = op("vector", "lb", lambda e: e.tensor_tensor(L[:, b_, :, :], L[:, b_, :, :], Lr[k], ALU.add), redt[16 * b_ + 15], s3)
            sft[b_] = dma("sync", f"sf{k}", lambda e: e.dma_start(sfr[k], sfd[2048 * b_:2048 * b_ + 2048].rearrange("(a t n) -> a t n", a=1, n=128)
                          .broadcast_to([8, 16, 128])), t_ss, fet.get((b_ - 2, "s")))
            m1 = op("tensor", "lt", lambda e: e.transpose(BK[3][:, 0:128], L[:, b_, :, :].rearrange("p h t -> p (h t)"), ident[:, :]), lb[b_],
                    fet.get(b_ - 1))
            v1 = op("vector", "sc", lambda e: e.tensor_tensor_scan(Fs, sfr[k], BK[3][:, 0:128], -BIG, ALU.add, ALU.max), m1, sft[b_], fet.get((b_ - 1, "p")))
            fet[(b_, "s")] = v1
            m2 = op("tensor", "lt", lambda e: e.transpose(BK[3][:, 128:256], Fs, ident[:, :]), v1)
            fet[(b_, "p")] = m2
            fet[b_] = op("scalar", "fe", lambda e: e.copy(Fe[k][:, 0:8, :], BK[3][:, 128:256].rearrange("p (h t) -> p h t", h=8)), m2, mt.get(16 * (b_ - 2) + 15), fe2)

        def p1_b2(b_):
            k = b_ % 2
            load_regs(dv1, b_, t_wid)
            for j in range(16):
                t = 16 * b_ + j
                eot[t] = op("vector", "eo", lambda e, t=t: e.tensor_scalar(eo[t % 4], iotaF[:, :], loEnd[:, t:t + 1], None, ALU.is_equal),
                            mt.get(t - 4), te[-1])
                mt[t] = op("tensor", "mt", lambda e, t=t, j=j: e.matmul(BK[4 + k][:, 16 * j:16 * j + 9], eo[t % 4], Fe[k][:, :, j], start=True, stop=True),
                           eot[t], fet[b_], mu.get(16 * (b_ - 2) + 15))
            v1 = op("vector", "mu", lambda e: e.tensor_scalar(pen, BK[4 + k][:, 0:256].rearrange("p (t n) -> p t n", n=16)[:, :, 8], -1.0, BIG, ALU.add, ALU.mult),
                    mt[16 * b_ + 15], mu.get(16 * b_ - 1))
            for j in range(16):
                t = 16 * b_ + j

                def f(e, t=t, j=j):
                    r = win(e, dv1, t)
                    mw = Mall[:, bass.ds(r, 1), :].rearrange("p a n -> p (a n)")
                    return e.scalar_tensor_tensor(mw, BK[4 + k][:, 16 * j:16 * j + 8], pen[:, j:j + 1], mw, ALU.add, ALU.max)
                mu[t] = op("vector", "mu", f, v1, mu.get(t - 1), s4)

        rows2(0, rt, "r", [t_ss, ATt[NCH - 1]])
        for t in range(KR):
            gather_k(t)
        for b_ in range(NB):
            if b_ + 1 < NB:
                rows2(b_ + 1, rt, "r", [t_ss, oht.get(2 * b_ - 1), ATt[NCH - 1]])
            load_regs(pe1, b_, t_wid)
            for t in range(16 * b_, 16 * b_ + 16):
                if t % 8 == 0:
                    mk_ohT(t // 8, rt, oht, [qt.get(t - 9), clr], "oh")
                p1_q(t)
                p1_l(t)
                if t + KR < T:
                    gather_k(t + KR)
            p1_b1(b_)
            if b_:
                p1_b2(b_ - 1)
        p1_b2(NB - 1)
        mx_all = mu[T - 1]
        pass1 = [mu[T - 1], qt[T - 1], redt[T - 1], lb[NB - 1]]

        Yall = R1[:, :].rearrange("p (w n) -> p w n", n=YW)
        y0 = op("vector", "v", lambda e: e.memset(R1[:, :], 0.0), pass1)
        b2 = carve(R2)
        Vr = [b2(512) for _ in range(KR)]
        assert KR * 512 + 1024 <= T * REC
        pv = prod
        c4 = carve(small, 0)
        oh = [c4(128) for _ in range(4)]
        rt2, oht2, vt, mgt, pt, pvt, yt, ya, oh2, lst = {}, {}, {}, {}, {}, {}, {}, {}, {}, {}

        def gather_v(t):
            vt[t] = dma("gpsimd", f"k{t % KR}", lambda e: e.indirect_dma_start(Vr[t % KR], None, Vd, bass.IndirectOffsetOnAxis(ap=dstS[:, t:t + 1], axis=0),
                        bounds_check=N - 1, oob_is_err=False), prt[T - KR + t % KR] if t < KR else pvt[t - KR])

        def p2_m(b_):
            k = b_ % 2
            load_regs(pe1, b_, t_wid)
            for j in range(16):
                t = 16 * b_ + j
                if t % 8 == 0:
                    h_ = t // 8
                    mk_ohT(h_, rt2, oht2, [mgt.get(t - 9), qt[T - 1]], "oh")
                mgt[t] = op("tensor", "mg", lambda e, t=t, j=j: e.matmul(BK[4 + k][:, 8 * j:8 * j + 8], ohT[(t // 8) % 2][:, t % 8, :],
                            Mall[:, bass.ds(win(e, pe1, t), 1), :], start=True, stop=True), oht2[t // 8], lst.get(b_ - 2), mx_all)
            v = op("vector", "lp", lambda e: e.tensor_tensor(L[:, b_, :, :], L[:, b_, :, :], BK[4 + k][:, 0:128].rearrange("p (t h) -> p h t", h=8), ALU.subtract),
                   mgt[16 * b_ + 15], mx_all)
            lst[b_] = v
            pt[b_] = op("scalar", "ex", lambda e: e.activation(L[:, b_, :, :], L[:, b_, :, :], ACT.Exp), v)

        def p2_v(t):
            b_ = t // 16
            ph = L[:, b_, :, t % 16]
            oh2[t] = op("vector", "oe", lambda e: e.tensor_scalar(oh[t % 4], iotaF[:, :], loS[:, t:t + 1], None, ALU.is_equal), yt.get(t - 4), pass1)
            pvt[t] = op("vector", "pv", lambda e: e.tensor_tensor(pv[t % 2].rearrange("p (h d) -> p h d", h=8), Vr[t % KR].rearrange("p (h d) -> p h d", h=8),
                        ph.rearrange("p (h a) -> p h a", a=1).broadcast_to([128, 8, 64]), ALU.mult), vt[t], pt[b_], yt.get(t - 2))
            op("tensor", "yt", lambda e: e.matmul(BK[2 * (t % 2)][:, :], oh[t % 4], pv[t % 2], start=True, stop=True), pvt[t], oh2[t], ya.get(t - 2))
            yt[t] = op("tensor", "yt", lambda e: e.matmul(BK[2 * (t % 2) + 1][:, 0:8], oh[t % 4], ph, start=True, stop=True))

        def p2_y(t):
            def f(e):
                st["w"] = win(e, dv1, t)
                yw = Yall[:, bass.ds(st["w"], 1), 0:512].rearrange("p a n -> p (a n)")
                return e.tensor_tensor(yw, yw, BK[2 * (t % 2)][:, :], ALU.add)

            def g(e):
                dw = Yall[:, bass.ds(st["w"], 1), 512:520].rearrange("p a n -> p (a n)")
                return e.tensor_tensor(dw, dw, BK[2 * (t % 2) + 1][:, 0:8], ALU.add)
            st = {}
            op("vector", "ya", f, yt[t], ya.get(t - 1), y0)
            ya[t] = op("vector", "ya", g)

        rows2(0, rt2, "r", [oht[2 * NB - 1]])
        rows2(1, rt2, "r", [oht[2 * NB - 1]])
        for t in range(KR):
            gather_v(t)
        p2_m(0)
        for b_ in range(NB):
            if b_ + 2 < NB:
                rows2(b_ + 2, rt2, "r", [oht2[2 * b_ + 1]])
            if b_ + 1 < NB:
                p2_m(b_ + 1)
            for t in range(16 * b_, 16 * b_ + 16):
                if t >= 1:
                    if (t - 1) % 16 == 0:
                        load_regs(dv1, (t - 1) // 16, t_wid)
                p2_v(t)
                if t >= 1:
                    p2_y(t - 1)
                if t + KR < T:
                    gather_v(t + KR)
        p2_y(T - 1)
        pass2 = [ya[T - 1], yt[T - 1]]

        d = carve(R2)
        e_ = carve(R3)
        WoS = d(2048).rearrange("p (c n) -> p c n", c=4)
        xr = [d(512) for _ in range(4)]
        yn = [d(512) for _ in range(2)]
        yT = [d(512).rearrange("p (c n) -> p c n", c=4) for _ in range(2)]
        xn = [d(512) for _ in range(4)]
        h1 = [e_(512) for _ in range(3)]
        h2 = [e_(512) for _ in range(3)]
        FT = e_(512)
        W0 = e_(320)
        W1a = e_(192)
        W1s = e_(192)
        W1b = e_(320)
        W2t = e_(12)
        b01 = e_(6)
        b2r = e_(4)
        boS = e_(512)
        DF = 6
        sc = [e_(160) for _ in range(4)]
        ini = [op("vector", "w", lambda e, t_=t_: e.memset(t_, 0.0), pass2) for t_ in (W1a, W1s, W1b, W2t, b01, b2r)]
        ft0 = op("vector", "w", lambda e: e.memset(FT, 0.0))
        wt = []

        def wload(dst_, src_):
            wt.append(dma("sync", "wt", lambda e: e.dma_start(dst_, src_, allow_slow_non_contiguous=True), ini, pass2))

        wload(WoS, wo.rearrange("(c p) n -> p c n", p=128))
        wload(boS[0:1, :], bo.rearrange("(a n) -> a n", a=1))
        for pi_, (wT, bb) in enumerate(((waT, ba), (wsT, bs))):
            o = 160 * pi_
            for k_, r_ in enumerate((0, 1, 35, 36)):
                wload(W0[k_:k_ + 1, 128 * pi_:128 * pi_ + 128], wT[0, r_:r_ + 1, 0:128])
                wload(W0[k_:k_ + 1, 256 + 32 * pi_:288 + 32 * pi_], wT[0, r_:r_ + 1, 128:160])
            W1 = (W1a, W1s)[pi_]
            wload(W1[:, 0:128], wT[1, 0:128, 0:128])
            wload(W1[:, 128 + 32 * pi_:160 + 32 * pi_], wT[1, 0:128, 128:160])
            wload(W1b[32 * pi_:32 * pi_ + 32, 128 * pi_:128 * pi_ + 128], wT[1, 128:160, 0:128])
            wload(W1b[32 * pi_:32 * pi_ + 32, 256 + 32 * pi_:288 + 32 * pi_], wT[1, 128:160, 128:160])
            wload(W2t[:, 4 * pi_ + 2 * pi_:4 * pi_ + 2 * pi_ + 2], wT[2, 0:128, 100:102])
            wload(W2t[32 * pi_:32 * pi_ + 32, 8 + 2 * pi_:10 + 2 * pi_], wT[2, 128:160, 100:102])
            for l in range(2):
                wload(b01[:, 3 * l + pi_:3 * l + pi_ + 1], bb[l, 0:128].rearrange("(p a) -> p a", a=1))
                wload(b01[32 * pi_:32 * pi_ + 32, 3 * l + 2:3 * l + 3], bb[l, 128:160].rearrange("(p a) -> p a", a=1))
            wload(b2r[:, 2 * pi_:2 * pi_ + 2], bb[2:3, 100:102].broadcast_to([128, 2]))
        w16 = small[:, 1024:1088].rearrange("p (a n) -> p a n", a=4)
        iw = op("vector", "w", lambda e: e.tensor_scalar(w16, iotaF[:, 0:16].rearrange("p (a n) -> p a n", a=1).broadcast_to([128, 4, 16]), -1.0, 16.0, ALU.mult, ALU.add))

        xt3, ynt, yTt, ot, x1t, xnt, outt, pst = {}, {}, {}, {}, {}, {}, {}, {}
        o_all = []
        res = {}

        def f_load(w):
            n = rows_of[w]
            xt3[w] = dma("sync", f"x{w % 4}" if w % 4 < 3 else "x3", lambda e: e.dma_start(xr[w % 4][0:n, :], x[128 * w:128 * w + n, :]), outt.get(w - 4), pass2)

        def f_y(w):
            n, k = rows_of[w], w % 2
            s = sc[w % 4]
            y = Yall[0:n, w, 0:512]
            u = op("vector", "fy", lambda e: e.tensor_scalar(s[0:n, 0:8], Yall[0:n, w, 512:520], 1e-30, None, ALU.max), pass2, res.get(w - 4))
            u = op("vector", "fy", lambda e: e.reciprocal(s[0:n, 8:16], s[0:n, 0:8]), u)
            ynt[w] = op("vector", "fy", lambda e: e.tensor_tensor(yn[k][0:n, :].rearrange("p (h d) -> p h d", h=8), y.rearrange("p (h d) -> p h d", h=8),
                        s[0:n, 8:16].rearrange("p (h a) -> p h a", a=1).broadcast_to([n, 8, 64]), ALU.mult), u, yTt.get((w - 2, "T")))
            for c in range(4):
                last = op("tensor", "ft", lambda e, c=c: e.transpose(BK[0][:, 128 * c:128 * c + n], yn[k][0:n, 128 * c:128 * c + 128], ident[0:n, 0:n]),
                          ynt[w], yTt.get(w - 1), pass2)
            yTt[(w, "T")] = last
            yTt[w] = op("scalar", "fa", lambda e: e.copy(yT[k][:, :, 0:n], BK[0][:, :].rearrange("p (c n) -> p c n", c=4)[:, :, 0:n]), last, ot.get(w - 2))
            for c in range(4):
                op("tensor", "fo", lambda e, c=c: e.matmul(BK[1 + k][0:n, :], yT[k][:, c, 0:n], WoS[:, c, :], start=(c == 0), stop=False), yTt[w], wt, x1t.get(w - 2))
            ot[w] = op("tensor", "fo", lambda e: e.matmul(BK[1 + k][0:n, :], ones[0:1, 0:n], boS[0:1, :], start=False, stop=True))

        def f_ln(w):
            n, k = rows_of[w], w % 2
            xx, xo, s = xr[w % 4], xn[w % 4], sc[w % 4]
            x1t[w] = op("vector", "fl", lambda e: e.tensor_tensor(xx[0:n, :], xx[0:n, :], BK[1 + k][0:n, :], ALU.add), ot[w], xt3[w])
            b5 = ln_stats(w, xx[0:n, :], n, x1t[w], "l2", w % 2)
            v = op("vector", "fl", lambda e: e.tensor_scalar(xo[0:n, :], xx[0:n, :], mv[0:n, k, 0:1], rs[0:n, k, 0:1], ALU.subtract, ALU.mult), b5, res.get(w - 4))
            xs = op("gpsimd", "fg", lambda e: e.tensor_tensor(xx[0:n, :], xx[0:n, :], xo[0:n, :], ALU.add), v)
            xnt[(w, "s")] = xs
            v1 = op("vector", "fl", lambda e: e.scalar_tensor_tensor(s[0:n, 32:96].rearrange("p (a n) -> p a n", a=4), xo[0:n, 16:80].rearrange("p (a n) -> p a n", a=4), 0.5,
                    w16[0:n, :, :], ALU.is_gt, ALU.mult), v, iw)
            v2 = op("vector", "fl", lambda e: e.tensor_reduce(s[0:n, 96:100], s[0:n, 32:96].rearrange("p (a n) -> p a n", a=4), AX.X, ALU.max), v1)
            v3 = op("vector", "fl", lambda e: e.tensor_scalar(s[0:n, 100:104], s[0:n, 96:100], -1.0, 16.0, ALU.mult, ALU.add), v2)
            fv = s[0:n, 104:112].rearrange("p (q f) -> p q f", q=2)
            v4 = op("vector", "fl", lambda e: e.scalar_tensor_tensor(fv[:, :, 0:2].rearrange("p q f -> p f q"), s[0:n, 96:100].rearrange("p (f q) -> p f q", f=2), 0.0,
                    s[0:n, 100:104].rearrange("p (f q) -> p f q", f=2), ALU.is_gt, ALU.mult), v3)
            v5 = op("vector", "fl", lambda e: e.tensor_copy(fv[:, :, 2:4], xo[0:n, 105:107].rearrange("p (a f) -> p a f", a=1).broadcast_to([n, 2, 2])), v)
            v6 = op("vector", "fl", lambda e: e.tensor_scalar(s[0:n, 112:115], xo[0:n, 0:3], 0.5, None, ALU.is_gt), v)
            xnt[w] = [v4, v5, v6]

        def f_masks(w):
            n, s = rows_of[w], sc[w % 4]
            mk, ad, su = s[0:n, 112:113], s[0:n, 113:114], s[0:n, 114:115]
            u1 = op("vector", "fm", lambda e: e.tensor_tensor(s[0:n, 115:116], mk, ad, ALU.mult), xnt[w])
            u2 = op("vector", "fm", lambda e: e.tensor_tensor(s[0:n, 116:117], mk, su, ALU.mult), u1)
            u3 = op("vector", "fm", lambda e: e.tensor_scalar(s[0:n, 119:120], ad, -1.0, 1.0, ALU.mult, ALU.add), u1)
            u4 = op("vector", "fm", lambda e: e.tensor_tensor(s[0:n, 116:117], s[0:n, 116:117], s[0:n, 119:120], ALU.mult), u3, u2)
            u5 = op("vector", "fm", lambda e: e.tensor_tensor(s[0:n, 117:118], s[0:n, 115:116], s[0:n, 116:117], ALU.add), u4)
            u6 = op("vector", "fm", lambda e: e.tensor_scalar(s[0:n, 118:119], s[0:n, 117:118], 2.0, None, ALU.mult), u5)
            return u6

        ftt, h1t, h2t, l3 = {}, {}, {}, {}

        def f_ffn(g):
            ws = [w for w in (2 * g, 2 * g + 1) if w < W]
            last = None
            for i, w in enumerate(ws):
                n, s = rows_of[w], sc[w % 4]
                for q in range(2):
                    last = op("tensor", "fq", lambda e, i=i, q=q, n=n, s=s: e.transpose(BK[3][0:4, 256 * i + 128 * q:256 * i + 128 * q + n], s[0:n, 104 + 4 * q:108 + 4 * q],
                              ident[0:n, 0:n]), xnt[w], h1t.get((g - 1, "f")))
            evs = []
            for i, w in enumerate(ws):
                n = rows_of[w]
                v = BK[3][0:4, 256 * i:256 * i + 256].rearrange("p (q n) -> p q n", q=2)[:, :, 0:n]
                o = FT[0:4, 256 * i:256 * i + 256].rearrange("p (q n) -> p q n", q=2)[:, :, 0:n]
                evs.append(op("scalar", "fa", lambda e, o=o, v=v: e.copy(o, v), last, h1t.get((g - 1, "m")), ft0))
            h1t[(g, "f")] = evs[-1]
            C = 256 * len(ws)
            mm = []
            for k_, (c0, m_) in enumerate(((0, 128), (128, 128), (256, 64))):
                mm.append(op("tensor", "h1", lambda e, k_=k_, c0=c0, m_=m_: e.matmul(BK[4 + k_][0:m_, 0:C], W0[0:4, c0:c0 + m_], FT[0:4, 0:C], start=True, stop=True),
                             evs, wt, h2t.get((g - 1, k_))))
            h1t[(g, "m")] = mm[-1]
            r = []
            for k_, m_ in enumerate((128, 128, 64)):
                r.append(op("scalar", "fa", lambda e, k_=k_, m_=m_: e.activation(h1[k_][0:m_, 0:C], BK[4 + k_][0:m_, 0:C], ACT.Relu, bias=b01[0:m_, k_:k_ + 1]),
                            mm[k_], h2t.get((g - 1, "mm"))))
            m2 = []
            for k_, terms in enumerate((((W1a[:, 0:128], 0, 128), (W1b[0:64, 0:128], 2, 64)),
                                        ((W1s[:, 0:128], 1, 128), (W1b[0:64, 128:256], 2, 64)),
                                        ((W1a[:, 128:192], 0, 128), (W1s[:, 128:192], 1, 128), (W1b[0:64, 256:320], 2, 64)))):
                m_ = 64 if k_ == 2 else 128
                for i, (lw, hi_, kk) in enumerate(terms):
                    t_ = op("tensor", "h2", lambda e, k_=k_, lw=lw, hi_=hi_, kk=kk, i=i, m_=m_, nt=len(terms): e.matmul(
                        BK[4 + k_][0:m_, 0:C], lw, h1[hi_][0:kk, 0:C], start=(i == 0), stop=(i == nt - 1)), r)
                m2.append(t_)
            h2t[(g, "mm")] = m2[-1]
            for k_, m_ in enumerate((128, 128, 64)):
                h2t[(g, k_)] = op("scalar", "fa", lambda e, k_=k_, m_=m_: e.activation(h2[k_][0:m_, 0:C], BK[4 + k_][0:m_, 0:C], ACT.Relu, bias=b01[0:m_, 3 + k_:4 + k_]),
                                  m2[k_], l3.get(g - 1))
            for i, w in enumerate(ws):
                n = rows_of[w]
                for q in range(2):
                    c0 = 256 * i + 128 * q
                    for k_, kk in enumerate((128, 128, 64)):
                        t_ = op("tensor", "h3", lambda e, k_=k_, kk=kk, c0=c0, n=n, i=i, q=q: e.matmul(BK[7][0:n, 8 * i + 4 * q:8 * i + 4 * q + 4], h2[k_][0:kk, c0:c0 + n],
                                W2t[0:kk, 4 * k_:4 * k_ + 4], start=(k_ == 0), stop=(k_ == 2)), h2t[(g, 2)], h2t[(g, 0)], h2t[(g, 1)], wt,
                                res.get(2 * g - 1), res.get(2 * g - 2))
            l3[g] = t_
            for i, w in enumerate(ws):
                n, s = rows_of[w], sc[w % 4]
                xx = xr[w % 4]
                um = f_masks(w)
                r4 = s[0:n, 124:132].rearrange("p (q c) -> p q c", q=2)
                u = op("vector", "fz", lambda e, i=i, n=n, r4=r4: e.tensor_tensor(r4, BK[7][0:n, 8 * i:8 * i + 8].rearrange("p (q c) -> p q c", q=2),
                       b2r[0:n, :].rearrange("p (a c) -> p a c", a=1).broadcast_to([n, 2, 4]), ALU.add), l3[g], wt, um)
                psf = u
                u = op("vector", "fz", lambda e, r4=r4, s=s, n=n: e.tensor_scalar(r4[:, :, 2:4], r4[:, :, 2:4], s[0:n, 116:117], None, ALU.mult), u)
                u = op("vector", "fz", lambda e, r4=r4, s=s, n=n: e.scalar_tensor_tensor(r4[:, :, 0:2], r4[:, :, 0:2], s[0:n, 115:116], r4[:, :, 2:4], ALU.mult, ALU.add), u)
                u = op("vector", "fz", lambda e, r4=r4: e.tensor_scalar(r4[:, :, 0:2], r4[:, :, 0:2], 0.0, 15.0, ALU.max, ALU.min), u)
                u = op("vector", "fz", lambda e, r4=r4: e.tensor_scalar(r4[:, :, 0:2], r4[:, :, 0:2], 12582912.0, 12582912.0, ALU.add, ALU.subtract), u)
                vs = []
                for q in range(2):
                    vs.append(op("vector", "fz", lambda e, q=q, r4=r4, s=s, n=n: e.tensor_scalar(s[0:n, 16 * q:16 * q + 16], iotaF[0:n, 0:16], r4[:, q, 0:1], s[0:n, 118:119],
                              ALU.is_equal, ALU.mult), u, ynt[w]))
                vs.append(op("vector", "fz", lambda e, r4=r4, s=s, n=n: e.tensor_scalar(s[0:n, 32:33], r4[:, 1, 1:2], 0.5, s[0:n, 117:118], ALU.is_gt, ALU.mult), u))
                res[w] = op("vector", "fz", lambda e, xx=xx, s=s, n=n: e.tensor_tensor(xx[0:n, 128:161], xx[0:n, 128:161], s[0:n, 0:33], ALU.add), vs, xnt[(w, "s")])
                outt[w] = dma("sync", f"o{w % 4}", lambda e, w=w, n=n, xx=xx: e.dma_start(out[128 * w:128 * w + n, :], xx[0:n, :]), res[w], xnt[(w, "s")])
                o_all.append(outt[w])

        for w in range(4):
            f_load(w)
        G = (W + 1) // 2
        for g in range(G):
            for w in (2 * g, 2 * g + 1):
                if w < W:
                    f_y(w)
            for w in (2 * g, 2 * g + 1):
                if w < W:
                    f_ln(w)
            f_ffn(g)
            for w in (2 * g + 4, 2 * g + 5):
                if w < W:
                    f_load(w)
        P.plain("sync", None, o_all)

        block = ctx.enter_context(nc.Block())

        @block.sync
        def _(e):
            P.emit("sync", e)

        @block.gpsimd
        def _(e):
            P.emit("gpsimd", e)

        @block.scalar
        def _(e):
            P.emit("scalar", e)

        @block.vector
        def _(e):
            P.emit("vector", e)

        @block.tensor
        def _(e):
            P.emit("tensor", e)


_INS = ['x', 'src', 'dst', 'edge_attr_8', 'L0_gnn_Wq', 'L0_gnn_bq', 'L0_gnn_Wk', 'L0_gnn_bk', 'L0_gnn_Wv', 'L0_gnn_bv',
        'L0_gnn_Wo', 'L0_gnn_bo', 'L0_ffn_Wa', 'L0_ffn_ba', 'L0_ffn_Ws', 'L0_ffn_bs']
_OUTS = [((6250, 512), 'float32')]


def kernel(**inputs):
    import numpy as _np
    import concourse.bacc as _bacc
    from concourse import mybir as _mybir
    from concourse.bass_utils import run_bass_kernel_spmd as _run

    nc = _bacc.Bacc("TRN2", target_bir_lowering=False, num_devices=1)
    arrays, args = {}, []
    for name in _INS:
        a = _np.asarray(inputs[name])
        if name in ('L0_ffn_Wa', 'L0_ffn_Ws'):
            a = a.transpose(0, 2, 1)
        a = _np.ascontiguousarray(a)
        arrays[f"in_{name}_dram"] = a
        args.append(nc.dram_tensor(f"in_{name}_dram", a.shape, _mybir.dt.from_np(a.dtype), kind="ExternalInput").ap())
    for i, (shape, dtype) in enumerate(_OUTS):
        args.append(nc.dram_tensor(f"out_{i}_dram", shape, _mybir.dt.from_np(_np.dtype(dtype)), kind="ExternalOutput").ap())
    build(nc, *args)
    r = _run(nc, [arrays], core_ids=[0])
    return r.results[0]["out_0_dram"]
```

```python
import concourse.bass as bass
from concourse import mybir
from contextlib import ExitStack


class Program:

    def __init__(self, nc, ctx):
        self.nc, self.ctx = nc, ctx
        self.queues = {e: [] for e in ("sync", "gpsimd", "scalar", "vector", "tensor")}
        self.sems, self.counts = {}, {}

    def token(self, stream, n):
        if stream not in self.sems:
            self.sems[stream] = self.ctx.enter_context(self.nc.semaphore("s_" + stream))
            self.counts[stream] = 0
        self.counts[stream] += n
        return (stream, self.counts[stream])

    def op(self, eng, stream, fn, *waits):
        tok = self.token(stream, 1)
        self.queues[eng].append((fn, waits, stream, 1))
        return tok

    def dma(self, eng, stream, fn, *waits):
        tok = self.token(stream, 16)
        self.queues[eng].append((fn, waits, stream, 16))
        return tok

    def plain(self, eng, fn, *waits):
        self.queues[eng].append((fn, waits, None, 0))

    def emit(self, name, eng):
        seen = {}

        def flat(ws):
            for w in ws:
                if isinstance(w, list):
                    yield from flat(w)
                elif w is not None:
                    yield w

        for fn, waits, stream, n in self.queues[name]:
            need = {}
            for s, v in flat(waits):
                need[s] = max(need.get(s, 0), v)
            for s, v in need.items():
                if seen.get(s, 0) < v:
                    eng.wait_ge(self.sems[s], v)
                    seen[s] = v
            if fn is None:
                continue
            ins = fn(eng)
            if stream is not None:
                ins.then_inc(self.sems[stream], n)


def build(nc, x, src, dst, attr, wq, bq, wk, bk, wv, bv, wo, bo, waT, ba, wsT, bs, out):
    f32, i32 = mybir.dt.float32, mybir.dt.int32
    bf16, u16 = mybir.dt.bfloat16, mybir.dt.uint16
    ALU, ACT, AX = mybir.AluOpType, mybir.ActivationFunctionType, mybir.AxisListType
    N, E, D, H = 6250, 100000, 512, 8
    W = 49
    TS = 782
    T = 832
    NB = T // 16
    REC = 10
    YW = 520
    BIG = 1.0e30
    rows_of = [min(128, N - 128 * w) for w in range(W)]

    ctx = ExitStack()
    with ctx:
        P = Program(nc, ctx)
        op, dma = P.op, P.dma

        def sb(name, shape, dt):
            return ctx.enter_context(nc.sbuf_tensor(name, shape, dt))

        def dram(name, shape, dt):
            return nc.dram_tensor(name, shape, dt, kind="Internal").ap()

        Qd = dram("q_scratch", (W * 128, D), f32)
        Kd = dram("k_scratch", (N, D), f32)
        Vd = dram("v_scratch", (N, D), f32)
        recd = dram("rec_scratch", (128 * T, REC), f32)
        loTd = dram("lo_rows", (TS * 128,), bf16)
        srcTd = dram("src_rows", (TS * 128,), u16)
        loSd = dram("lo_sorted", (T * 128,), bf16)
        sfd = dram("seg_flags", (T * 128,), bf16)
        widd = dram("tile_window", (896,), i32)

        R1 = sb("R1", [128, W * YW], f32)
        R2 = sb("R2", [128, T * REC], f32)
        R3 = sb("R3", [128, TS * REC], f32)
        rowR = sb("rowR", [128, 2, 2048], bf16)
        ident = sb("ident", [128, 128], f32)
        iotaF = sb("iotaF", [128, 128], f32)
        pidx = sb("pidx", [128, 1], f32)
        loS = sb("loS", [128, T], f32)
        dstS = sb("dstS", [128, T], i32)
        loEnd = sb("loEnd", [128, T], f32)
        widr = sb("widr", [1, T], i32)
        Mall = sb("Mall", [128, W, 8], f32)
        small = sb("small", [128, 3100], f32)
        ones = sb("ones", [3, 128], bf16)
        npidx = sb("npidx", [128, 1], f32)
        one1 = sb("one1", [128, 1], f32)
        PS = ctx.enter_context(nc.psum_tensor("banks", [128, 8 * 512], f32))
        BK = [PS[:, 512 * i:512 * i + 512] for i in range(8)]

        def carve(base, start=0):
            at = [start]

            def take(n, dt=f32):
                words = n if dt in (f32, i32) else (n + 1) // 2
                v = base[:, at[0]:at[0] + words]
                at[0] += words
                assert at[0] <= base.shape[1], (base.name, at[0])
                return v if dt == f32 else v.bitcast(dt)
            return take

        a = carve(R1)
        iotaI = a(128).bitcast(i32)
        pI = a(1).bitcast(i32)
        a(3)
        low = a(128)
        upp = a(128)
        onesf = a(128)
        W3 = [a(2048).rearrange("p (c n) -> p c n", c=4) for _ in range(3)]
        Bs = a(1536, bf16)
        ar = carve(R2)
        Bt = ar(3 * 1536, bf16).rearrange("p (r n) -> p r n", r=3)
        Bf = ar(1536)
        Br = Bf
        k1 = op("gpsimd", "cst", lambda e: e.iota(iotaI, pattern=[[1, 128]], base=0, channel_multiplier=0))
        k2 = op("gpsimd", "cst", lambda e: e.iota(pI, pattern=[[0, 1]], base=0, channel_multiplier=1))
        c_iota = op("vector", "cv", lambda e: e.tensor_copy(iotaF[:, :], iotaI), k1)
        c_pidx = op("vector", "cv", lambda e: e.tensor_copy(pidx[:, :], pI), k2)
        c_id = op("vector", "cv", lambda e: e.tensor_scalar(ident[:, :], iotaF[:, :], pidx[:, 0:1], None, ALU.is_equal), c_pidx)
        c_low = op("vector", "cv", lambda e: e.tensor_scalar(low, iotaF[:, :], pidx[:, 0:1], None, ALU.is_lt))
        c_upp = op("vector", "cv", lambda e: e.tensor_scalar(upp, iotaF[:, :], pidx[:, 0:1], None, ALU.is_gt))
        c_onesf = op("vector", "cv", lambda e: e.memset(onesf, 1.0))
        c_ones = op("vector", "cv", lambda e: e.memset(ones[:, :], 1.0))
        c_np = op("vector", "cv", lambda e: e.tensor_scalar(npidx[:, :], pidx[:, 0:1], -1.0, None, ALU.mult), c_pidx)
        c_one1 = op("vector", "cv", lambda e: e.memset(one1[:, :], 1.0))

        def split_bias(tag, parts, bf, br, bt, dst3, wait):
            n = 512 * len(parts)
            ld = [dma("sync", tag + "l", lambda e, i=i, b_=b_: e.dma_start(bf[0:1, 512 * i:512 * i + 512], b_.rearrange("(a n) -> a n", a=1)), wait)
                  for i, b_ in enumerate(parts)]
            u = op("vector", tag, lambda e: e.tensor_copy(bt[0:1, 0, 0:n], bf[0:1, 0:n]), ld)
            u = op("vector", tag, lambda e: e.tensor_tensor(br[0:1, 0:n], bf[0:1, 0:n], bt[0:1, 0, 0:n], ALU.subtract), u)
            u = op("vector", tag, lambda e: e.tensor_copy(bt[0:1, 1, 0:n], br[0:1, 0:n]), u)
            u = op("vector", tag, lambda e: e.tensor_tensor(bf[0:1, 0:n], br[0:1, 0:n], bt[0:1, 1, 0:n], ALU.subtract), u)
            u = op("vector", tag, lambda e: e.tensor_copy(bt[0:1, 2, 0:n], bf[0:1, 0:n]), u)
            return [dma("sync", tag + "s", lambda e, i=i: e.dma_start(dst3[i:i + 1, 0:n], bt[0:1, i, 0:n]), u) for i in range(3)]

        wl = [dma("sync", f"w{n}", lambda e, n=n, w_=w_: e.dma_start(W3[n], w_.rearrange("(c p) n -> p c n", p=128)))
              for n, w_ in enumerate((wq, wk, wv))]
        srcI = a(TS).bitcast(i32)
        dstI = a(TS).bitcast(i32)
        tI = a(TS).bitcast(i32)
        srcF = a(TS)
        hiF = a(TS)
        inv = a(TS)
        rec = R3[:, :].rearrange("p (t r) -> p t r", r=REC)
        FULL = 127 * TS
        TAIL = E - FULL
        def2 = R2[:, :].rearrange("p (t r) -> p t r", r=REC)
        z1 = op("vector", "v", lambda e: e.memset(srcI[:, TAIL:TS], 8191))
        z2 = op("vector", "v", lambda e: e.memset(dstI[:, TAIL:TS], 0))
        d1 = op("gpsimd", "g", lambda e: e.memset(R2[:, :], 0.0))
        d2 = op("gpsimd", "g", lambda e: e.memset(def2[:, :, 8:9], -1.0), d1)
        t_def = dma("sync", "def", lambda e: e.dma_start(recd.rearrange("(p t) r -> p (t r)", p=128), R2[:, :]), d2)
        ls = []
        for name, t_, v_ in (("ls", srcI, src), ("ld", dstI, dst)):
            zt = z1 if name == "ls" else z2
            ls.append([dma("sync", name, lambda e, t_=t_, v_=v_: e.dma_start(t_[0:127, :], v_[0:FULL].rearrange("(p t) -> p t", t=TS)), zt),
                       dma("sync", name, lambda e, t_=t_, v_=v_: e.dma_start(t_[127:128, 0:TAIL], v_[FULL:E].rearrange("(p t) -> p t", p=1)), zt)])
        at8 = R2[:, 0:TS * 8]
        d3 = op("gpsimd", "g", lambda e: e.memset(R2[:, TAIL * 8:TS * 8], 0.0), t_def)
        la = [dma("sync", "la", lambda e: e.dma_start(at8[0:127, :], attr[0:FULL, :].rearrange("(p t) h -> p (t h)", t=TS)), d3, t_def),
              dma("sync", "la", lambda e: e.dma_start(at8[127:128, 0:TAIL * 8], attr[FULL:E, :].rearrange("(p t) h -> p (t h)", p=1)), d3, t_def)]
        r1 = op("scalar", "a", lambda e: e.copy(rec[:, :, 0:8], at8.rearrange("p (t h) -> p t h", h=8)), la)
        r2 = op("vector", "v", lambda e: e.tensor_copy(rec[:, :, 9:10].bitcast(i32), dstI.rearrange("p (t a) -> p t a", a=1)), ls[1])
        r3 = op("vector", "v", lambda e: e.tensor_copy(srcF, srcI), ls[0])
        r4 = op("vector", "v", lambda e: e.tensor_scalar(tI, srcI, 7, None, ALU.logical_shift_right))
        r5 = op("vector", "v", lambda e: e.tensor_copy(hiF, tI), r4)
        r6 = op("vector", "v", lambda e: e.scalar_tensor_tensor(rec[:, :, 8:9].rearrange("p t a -> p (t a)"), hiF, -128.0, srcF, ALU.mult, ALU.add), r5)
        r7 = op("vector", "v", lambda e: e.tensor_scalar(inv, hiF, 48.5, 1048576.0, ALU.is_gt, ALU.mult), r5)
        loF = rec[:, :, 8]

        tr = []
        stl = a(7 * 128, bf16).rearrange("p (c n) -> p c n", c=7)
        stu = a(7 * 128, u16).rearrange("p (c n) -> p c n", c=7)
        for c in range(7):
            n = min(128, TS - 128 * c)
            m1 = op("tensor", "tr", lambda e, c=c, n=n: e.transpose(BK[c % 2][0:n, 0:128], loF[:, 128 * c:128 * c + n], ident[:, :]), r6, c_id,
                    tr[-2] if c >= 2 else None)
            m2 = op("tensor", "tr", lambda e, c=c, n=n: e.transpose(BK[c % 2][0:n, 128:256], srcF[:, 128 * c:128 * c + n], ident[:, :]), r3)
            v1 = op("vector", "v", lambda e, c=c, n=n: e.tensor_copy(stl[0:n, c, :], BK[c % 2][0:n, 0:128]), m1, m2)
            v2 = op("vector", "v", lambda e, c=c, n=n: e.tensor_copy(stu[0:n, c, :], BK[c % 2][0:n, 128:256]), m2)
            tr.append(v2)
        t_rows = []
        for st, dd in ((stl, loTd), (stu, srcTd)):
            t_rows.append(dma("sync", "rw", lambda e, st=st, dd=dd: e.dma_start(dd[0:768 * 128].rearrange("(c p n) -> p c n", p=128, n=128), st[:, 0:6, :]), tr[-1]))
            t_rows.append(dma("sync", "rw", lambda e, st=st, dd=dd: e.dma_start(dd[768 * 128:TS * 128].rearrange("(p n) -> p n", n=128), st[0:14, 6, :]), tr[-1]))

        a2 = carve(R1, 6144 + 4 + 512 + 768 + 6 * TS + 2 * 448)
        Abf = [a2(8 * 128, bf16).rearrange("p (t n) -> p t n", n=128) for _ in range(2)]
        Bbf = [a2(8 * W, bf16).rearrange("p (t n) -> p t n", n=W) for _ in range(3)]
        AT = [a2(8 * 128).rearrange("p (t n) -> p t n", n=128) for _ in range(2)]
        Cs = [a2(W * 9).rearrange("p (n t) -> p n t", t=9) for _ in range(3)]
        keep9 = a2(W * 9).rearrange("p (n t) -> p n t", t=9)
        GB = a2(8 * W).rearrange("p (t n) -> p t n", n=W)
        rank = a2(2 * 8).rearrange("p (a t) -> p a t", a=2)
        psel = a2(2 * 8).rearrange("p (a t) -> p a t", a=2)
        sm = [a2(8) for _ in range(6)]
        ridx = a2(4 * 8).bitcast(i32).rearrange("p (a t) -> p a t", a=4)
        scr = [a2(128) for _ in range(2)]
        xin = [ar(512) for _ in range(3)]
        xT = [a2(512).rearrange("p (c n) -> p c n", c=4) for _ in range(2)]
        stg = [a2(512) for _ in range(3)]
        rowsS = [ar(1024, u16) for _ in range(3)]
        rowsL = [rowR[:, 0, 0:1024], rowR[:, 0, 1024:2048], rowR[:, 1, 0:1024]]
        NCH = (TS + 7) // 8
        chn = [min(8, TS - 8 * c) for c in range(NCH)]

        def bcast_last(ap, n, m):
            return ap.rearrange("p (t a) -> p t a", a=1).broadcast_to([128, n, m])

        def build_AB(c, slot_wait, b_on_pool=False):
            n = chn[c]
            lo_c = rec[:, 8 * c:8 * c + n, 8:9].broadcast_to([128, n, 128])
            io = iotaF[:, :].rearrange("p (a n) -> p a n", a=1).broadcast_to([128, n, 128])
            ta = op("vector", "ab", lambda e: e.tensor_tensor(Abf[c % 2][:, 0:n, :], lo_c, io, ALU.is_equal), r6, c_iota, slot_wait)
            if b_on_pool:
                for j in range(n):
                    tb = op("gpsimd", "bp", lambda e, j=j: e.tensor_scalar(Bbf[c % 3][:, j, :], iotaF[:, 0:W], hiF[:, 8 * c + j:8 * c + j + 1], None, ALU.is_equal),
                            r5, c_iota, slot_wait)
                return [ta, tb]
            hi_c = bcast_last(hiF[:, 8 * c:8 * c + n], n, W)
            io2 = iotaF[:, 0:W].rearrange("p (a n) -> p a n", a=1).broadcast_to([128, n, W])
            tb = op("vector", "ab", lambda e: e.tensor_tensor(Bbf[c % 3][:, 0:n, :], hi_c, io2, ALU.is_equal), r5)
            return [ta, tb]

        c_b3 = split_bias("b3", (bq, bk, bv), Bf, Br, Bt, Bs, r1)
        st6 = small[:, 0:12].rearrange("p (a n) -> p a n", a=2)
        mv = small[:, 12:16].rearrange("p (a n) -> p a n", a=2)
        rs = small[:, 16:20].rearrange("p (a n) -> p a n", a=2)
        xl, xTt, pj, stv, lnd = {}, {}, {}, {}, {}
        stored = {}
        OUTS = (Qd, Kd, Vd)

        def load_x(w):
            n = rows_of[w]
            xl[w] = dma("sync", f"x{w % 3}", lambda e: e.dma_start(xin[w % 3][0:n, :], x[128 * w:128 * w + n, :]), xTt.get((w - 3, "T")), r1)

        def ln_stats(w, xt, n, wait, tag, slot):
            b1 = op("vector", tag, lambda e: e.bn_stats(st6[0:n, slot, :], xt), wait)
            b2 = op("vector", tag, lambda e: e.bn_aggr(mv[0:n, slot, :], st6[0:n, slot, :]), b1)
            b3 = op("vector", tag, lambda e: e.tensor_scalar(rs[0:n, slot, 0:1], mv[0:n, slot, 1:2], 1e-5, None, ALU.add), b2)
            b4 = op("scalar", tag + "a", lambda e: e.activation(rs[0:n, slot, 1:2], rs[0:n, slot, 0:1], ACT.Sqrt), b3)
            b5 = op("vector", tag, lambda e: e.reciprocal(rs[0:n, slot, 0:1], rs[0:n, slot, 1:2]), b4)
            return b5

        def proj_ln(w):
            n, xt = rows_of[w], xin[w % 3]
            b5 = ln_stats(w, xt[0:n, :], n, xl[w], "ln", w % 2)
            lnd[w] = op("vector", "ln", lambda e: e.tensor_scalar(xt[0:n, :], xt[0:n, :], mv[0:n, w % 2, 0:1], rs[0:n, w % 2, 0:1],
                        ALU.subtract, ALU.mult), b5)

        def proj_T(w):
            n, xt = rows_of[w], xin[w % 3]
            for c in range(4):
                last = op("tensor", "pt", lambda e, c=c: e.transpose(BK[3][:, 128 * c:128 * c + n], xt[0:n, 128 * c:128 * c + 128],
                          ident[0:n, 0:n]), lnd[w], xTt.get(w - 1))
            xTt[(w, "T")] = last
            xTt[w] = op("scalar", "px", lambda e: e.copy(xT[w % 2][:, :, 0:n], BK[3][:, :].rearrange("p (c n) -> p c n", c=4)[:, :, 0:n]),
                        last, pj.get((w - 2, 2)))

        def proj_M(w, m):
            n = rows_of[w]
            i = 3 * w + m
            bank = BK[4 + i % 3]
            for c in range(4):
                op("tensor", "pj", lambda e, c=c: e.matmul(bank[0:n, :], xT[w % 2][:, c, 0:n], W3[m][:, c, :], start=(c == 0), stop=False),
                   xTt[w], wl[m], stv.get(i - 3))
            pj[(w, m)] = op("tensor", "pj", lambda e: e.matmul(bank[0:n, :], ones[0:3, 0:n], Bs[0:3, 512 * m:512 * m + 512], start=False, stop=True),
                            c_ones, c_b3)
            stv[i] = op("scalar", "ps", lambda e: e.activation(stg[i % 3][0:n, :], bank[0:n, :], ACT.Copy, scale=0.125 if m == 0 else 1.0),
                        pj[(w, m)], stored.get(i - 3))
            stored[i] = dma("sync", f"st{i % 3}", lambda e: e.dma_start(OUTS[m][128 * w:128 * w + n, :], stg[i % 3][0:n, :]), stv[i])

        proj = []
        for w in range(W):
            proj += [lambda w=w: (proj_T(w), proj_ln(w + 1) if w + 1 < W else None, load_x(w + 3) if w + 3 < W else None),
                     lambda w=w: proj_M(w, 0), lambda w=w: proj_M(w, 1), lambda w=w: proj_M(w, 2)]
        at_unit = [0]

        def next_unit():
            if at_unit[0] < len(proj):
                proj[at_unit[0]]()
                at_unit[0] += 1

        for w in range(3):
            load_x(w)
        proj_ln(0)
        hist = []
        for c in range(NCH):
            t_ab = build_AB(c, hist[c - 2] if c >= 2 else None, True)
            for j in range(chn[c]):
                last = op("tensor", "hi", lambda e, c=c, j=j: e.matmul(BK[0][:, 0:W], Abf[c % 2][:, j, :], Bbf[c % 3][:, j, :],
                          start=(c == 0 and j == 0), stop=(c == NCH - 1 and j == chn[c] - 1)), t_ab, tr[-1])
            hist.append(last)
            if c % 3 == 2:
                next_unit()
        sHt = a2(W)
        sC = a2(W)
        sTi = a2(W).bitcast(i32)
        sTf = a2(W)
        sInc = a2(W)
        z0 = a2(W)
        q1 = op("vector", "v", lambda e: e.tensor_copy(sHt, BK[0][:, 0:W]), hist[-1])
        q0 = op("vector", "v", lambda e: e.memset(z0, 0.0))
        m1 = op("tensor", "hb", lambda e: e.matmul(BK[1][:, 0:W], upp, sHt, start=True, stop=True), q1, c_upp)
        m2 = op("tensor", "hb", lambda e: e.matmul(BK[1][:, 64:64 + W], onesf, sHt, start=True, stop=True), q1, c_onesf)
        q2 = op("vector", "v", lambda e: e.tensor_scalar(sC, BK[1][:, 64:64 + W], 127.0, None, ALU.add), m2)
        q3 = op("vector", "v", lambda e: e.tensor_copy(sTi, sC), q2)
        q4 = op("vector", "v", lambda e: e.tensor_scalar(sTi, sTi, 7, None, ALU.logical_shift_right), q3)
        q5 = op("vector", "v", lambda e: e.tensor_copy(sTf, sTi), q4)
        q6 = op("vector", "v", lambda e: e.tensor_tensor_scan(sInc, z0, sTf, 0.0, ALU.add, ALU.add), q5, q0)
        q7 = op("vector", "v", lambda e: e.tensor_tensor(sC, sInc, sTf, ALU.subtract), q6)
        t_base = op("vector", "v", lambda e: e.scalar_tensor_tensor(Cs[2][:, :, 8], sC, 128.0, BK[1][:, 0:W], ALU.mult, ALU.add), q7, m1)
        k9 = op("vector", "v", lambda e: e.memset(keep9, 1.0))
        k9 = op("vector", "v", lambda e: e.memset(keep9[:, :, 0:1], 0.0), k9)
        wI = a2(7).bitcast(i32)
        wF = a2(7)
        wC = a2(7 * W).rearrange("p (c n) -> p c n", n=W)
        g1 = op("gpsimd", "g", lambda e: e.iota(wI, pattern=[[128, 7]], base=0, channel_multiplier=1))
        q8 = op("vector", "v", lambda e: e.tensor_copy(wF, wI), g1)
        q9 = op("vector", "v", lambda e: e.tensor_tensor(wC, sInc.rearrange("p (a n) -> p a n", a=1).broadcast_to([128, 7, W]),
                bcast_last(wF, 7, W), ALU.is_le), q8, q6)
        q10 = op("vector", "v", lambda e: e.tensor_reduce(wF, wC, AX.X, ALU.add), q9)
        q11 = op("vector", "v", lambda e: e.tensor_scalar(wI, wF, 48.0, None, ALU.min), q10)
        t_wd = dma("sync", "wid", lambda e: e.dma_start(widd.rearrange("(c p) -> p c", p=128), wI, allow_slow_non_contiguous=True), q11)
        t_wid = dma("sync", "wid", lambda e: e.dma_start(widr[:, :], widd[0:T].rearrange("(a t) -> a t", a=1)), t_wd)

        rowt, gsum, rk, scat, ATt, Gt, Ht, Cst = {}, {}, {}, {}, {}, {}, {}, {}
        abt = {}
        HB = (0, 7)

        def s_rows(c):
            n = chn[c]
            rowt[c] = [dma("sync", f"rl{c % 3}", lambda e: e.dma_start(rowsL[c % 3][:, 0:128 * n], loTd[1024 * c:1024 * c + 128 * n]
                           .rearrange("(a n) -> a n", a=1).broadcast_to([128, 128 * n])), t_rows, ATt.get(c - 3)),
                       dma("sync", f"rs{c % 3}", lambda e: e.dma_start(rowsS[c % 3][:, 0:128 * n], srcTd[1024 * c:1024 * c + 128 * n]
                           .rearrange("(a n) -> a n", a=1).broadcast_to([128, 128 * n])), t_rows, rk.get(c - 3), r1)]

        def s_ab(c):
            n = chn[c]
            abt[c] = build_AB(c, [Ht.get(c - 2), hist[-1], gsum.get(c - 3)])
            for j in range(n):
                last = op("tensor", "sh", lambda e, j=j: e.matmul(BK[HB[c % 2]][:, 0:W * 9].rearrange("p (n t) -> p n t", t=9)[:, :, j + 1],
                          Abf[c % 2][:, j, :], Bbf[c % 3][:, j, :], start=True, stop=True), abt[c], q1, Cst.get(c - 2))
            Ht[c] = last

        def s_at(c):
            n = chn[c]
            v = op("scalar", "at", lambda e: e.activation(AT[c % 2][:, 0:n, :], rowsL[c % 3][:, 0:128 * n].rearrange("p (t n) -> p t n", n=128),
                   ACT.Abs, bias=npidx[:, 0:1]), rowt[c][0], Gt.get(c - 2), c_np)
            ATt[c] = op("scalar", "at", lambda e: e.activation(AT[c % 2][:, 0:n, :], AT[c % 2][:, 0:n, :], ACT.Relu, bias=one1[:, 0:1], scale=-1.0), v, c_one1)

        def s_scan(c):
            n = chn[c]
            bank = BK[HB[c % 2]][:, 0:W * 9]
            v = op("vector", "cs", lambda e: e.tensor_copy(bank.rearrange("p (n t) -> p n t", t=9)[:, :, 0], Cs[(c - 1) % 3][:, :, 8]),
                   Ht[c], Cst.get(c - 1), t_base)
            if n < 8:
                v = op("vector", "cs", lambda e: e.memset(bank.rearrange("p (n t) -> p n t", t=9)[:, :, n + 1:9], 0.0), v)
            Cst[c] = op("vector", "cs", lambda e: e.tensor_tensor_scan(Cs[c % 3].rearrange("p n t -> p (n t)"), keep9.rearrange("p n t -> p (n t)"), bank, 0.0,
                        ALU.mult, ALU.add), v, k9, Gt.get(c - 3))

        def s_g(c):
            for j in range(chn[c]):
                Gt[c] = op("tensor", "sg", lambda e, j=j: e.matmul(BK[1 + c % 2][:, j * W:(j + 1) * W], AT[c % 2][:, j, :], Cs[c % 3][:, :, j], start=True, stop=True),
                           ATt[c], Cst[c], gsum.get(c - 2), q11)

        scr_free = [None, None]

        def s_rank(c, j):
            t = 8 * c + j
            rk[c] = scr_free[j % 2] = op("vector", "rk", lambda e: e.scalar_tensor_tensor(scr[j % 2], rowsS[c % 3][:, 128 * j:128 * j + 128], srcF[:, t:t + 1], low,
                       ALU.is_equal, ALU.mult, accum_out=rank[:, c % 2, j:j + 1]), rowt[c][1], c_low, gsum.get((c - 2, "u")), scr_free[j % 2])

        def s_place(c):
            n, k = chn[c], c % 2
            pf, pi, af, bf_, av = sm[0][:, 0:n], sm[1].bitcast(i32)[:, 0:n], sm[2][:, 0:n], sm[3][:, 0:n], sm[4][:, 0:n]
            last = lambda: gsum[(c, "z")]

            def step(fn, *w):
                def f():
                    gsum[(c, "z")] = op("vector", "sv", fn, gsum.get((c, "z")), *w)
                return f

            def gb():
                gsum[(c, "z")] = op("vector", "sv", lambda e: e.tensor_tensor(GB[:, 0:n, :], BK[1 + k][:, 0:n * W].rearrange("p (t n) -> p t n", n=W),
                                    Bbf[c % 3][:, 0:n, :], ALU.mult), Gt[c], gsum.get(c - 1))

            def red():
                gsum[c] = gsum[(c, "z")] = op("vector", "sv", lambda e: e.tensor_reduce(psel[:, k, 0:n], GB[:, 0:n, :], AX.X, ALU.add), gsum[(c, "z")])

            def u1():
                gsum[(c, "u")] = gsum[(c, "z")] = op("vector", "sv", lambda e: e.tensor_tensor(pf, psel[:, k, 0:n], rank[:, k, 0:n], ALU.add), gsum[c], rk[c])

            def fin():
                u7 = op("vector", "sv", lambda e: e.scalar_tensor_tensor(ridx[:, c % 4, 0:n], bf_, float(T), av, ALU.mult, ALU.add), gsum[(c, "z")], scat.get(c - 4))
                for j in range(n):
                    t = 8 * c + j
                    scat[c] = dma("gpsimd", f"sc{c % 4}", lambda e, t=t, j=j: e.indirect_dma_start(
                        recd, bass.IndirectOffsetOnAxis(ap=ridx[:, c % 4, j:j + 1], axis=0), rec[:, t, :], None,
                        bounds_check=128 * T - 1, oob_is_err=False), u7, r1, r2, r6, t_def)
            return [gb, red, u1, step(lambda e: e.tensor_copy(pi, pf)),
                    step(lambda e: e.tensor_scalar(pi, pi, 7, None, ALU.logical_shift_right)),
                    step(lambda e: e.tensor_copy(af, pi)),
                    step(lambda e: e.scalar_tensor_tensor(bf_, af, -128.0, pf, ALU.mult, ALU.add)),
                    step(lambda e: e.tensor_tensor(av, af, inv[:, 8 * c:8 * c + n], ALU.add), r7), fin]

        s_rows(0)
        s_rows(1)
        s_ab(0)
        s_at(0)
        s_ab(1)
        for j in range(chn[0]):
            s_rank(0, j)
        s_scan(0)
        s_g(0)
        for c in range(NCH):
            if c + 2 < NCH:
                s_rows(c + 2)
                s_ab(c + 2)
            if c + 1 < NCH:
                s_at(c + 1)
                s_scan(c + 1)
            next_unit()
            if c + 1 < NCH:
                s_g(c + 1)
            steps = s_place(c)
            for j in range(max(len(steps), 8)):
                if j < len(steps):
                    steps[j]()
                if c + 1 < NCH and j < chn[c + 1]:
                    s_rank(c + 1, j)
            if c % 4 < 3:
                next_unit()
        while at_unit[0] < len(proj):
            next_unit()
        scat_all = [scat[c] for c in range(NCH - 4, NCH)]
        proj_all = [stored[i] for i in range(3 * W - 3, 3 * W)]
        phaseA = [pj[(W - 1, 2)], stv[3 * W - 1], gsum[NCH - 1], rk[NCH - 1]]

        Qall = R1[:, 0:W * 512].rearrange("p (w n) -> p w n", n=512)
        t_q = dma("sync", "q", lambda e: e.dma_start(Qall[:, 0:W - 1, :], Qd[0:(W - 1) * 128, :].rearrange("(w p) n -> p w n", p=128)),
                  phaseA, proj_all, scat_all)
        z3 = op("vector", "v", lambda e: e.memset(Qall[:, W - 1, :], 0.0), phaseA, proj_all, scat_all)
        t_q2 = dma("sync", "q", lambda e: e.dma_start(Qall[0:106, W - 1, :], Qd[(W - 1) * 128:N, :]), z3, phaseA, proj_all)
        t_rec = dma("sync", "rec", lambda e: e.dma_start(R2[:, :], recd.rearrange("(p t) r -> p (t r)", p=128)), scat_all, phaseA)
        L = R3[:, 0:T * 8].rearrange("p (b h t) -> p b h t", h=8, t=16)
        recS = R2[:, :].rearrange("p (b t r) -> p b t r", t=16, r=REC)
        s1 = op("vector", "v", lambda e: e.tensor_copy(loS[:, :], R2[:, :].rearrange("p (t r) -> p t r", r=REC)[:, :, 8]), t_rec)
        s2 = op("vector", "v", lambda e: e.tensor_copy(dstS[:, :], R2[:, :].rearrange("p (t r) -> p t r", r=REC)[:, :, 9].bitcast(i32)))
        s3 = op("scalar", "a", lambda e: e.copy(L.rearrange("p b h t -> p b t h"), recS[:, :, :, 0:8]), t_rec, scat_all)
        s4 = op("vector", "v", lambda e: e.memset(Mall[:, :, :], -BIG))
        loT = R3[:, T * 8:T * 8 + 896].rearrange("p (c n) -> p c n", n=128)
        loTb = small[:, 0:448].bitcast(bf16).rearrange("p (c n) -> p c n", n=128)
        sfb = small[:, 448:896].bitcast(bf16).rearrange("p (c n) -> p c n", n=128)
        en = small[:, 896:1024]
        te = []
        for c in range(7):
            n = min(128, T - 128 * c)
            m1 = op("tensor", "u", lambda e, c=c, n=n: e.transpose(BK[c % 2][0:n, 0:128], loS[:, 128 * c:128 * c + n], ident[:, :]), s1, te[c - 2] if c >= 2 else None,
                    phaseA)
            v1 = op("vector", "u2", lambda e, c=c, n=n: e.tensor_copy(loT[0:n, c, :], BK[c % 2][0:n, 0:128]), m1, s3)
            v2 = op("vector", "u2", lambda e, c=c, n=n: e.tensor_copy(loTb[0:n, c, :], loT[0:n, c, :]), v1)
            v3 = op("vector", "u2", lambda e, c=c, n=n: e.tensor_tensor(sfb[0:n, c, 1:128], loT[0:n, c, 1:128], loT[0:n, c, 0:127], ALU.is_equal), v1)
            v4 = op("vector", "u2", lambda e, c=c, n=n: e.memset(sfb[0:n, c, 0:1], 0.0))
            v5 = op("vector", "u2", lambda e, c=c, n=n: e.tensor_scalar(en[0:n, 0:127], sfb[0:n, c, 1:128], -1.0, 1.0, ALU.mult, ALU.add), v3, te[-1] if te else None)
            v6 = op("vector", "u2", lambda e, c=c, n=n: e.memset(en[0:n, 127:128], 1.0))
            v7 = op("vector", "u2", lambda e, c=c, n=n: e.scalar_tensor_tensor(en[0:n, :], loT[0:n, c, :], 1.0, en[0:n, :], ALU.add, ALU.mult), v5, v6)
            v8 = op("vector", "u2", lambda e, c=c, n=n: e.tensor_scalar(en[0:n, :], en[0:n, :], -1.0, None, ALU.add), v7)
            v9 = op("vector", "u2", lambda e, c=c, n=n: e.tensor_scalar(sfb[0:n, c, :], sfb[0:n, c, :], -1.0, BIG, ALU.add, ALU.mult), v5, v4)
            m2 = op("tensor", "u", lambda e, c=c, n=n: e.transpose(BK[c % 2][:, 128:128 + n], en[0:n, :], ident[0:n, 0:n]), v8)
            te.append(op("vector", "u2", lambda e, c=c, n=n: e.tensor_scalar(loEnd[:, 128 * c:128 * c + n], BK[c % 2][:, 128:128 + n], -1.0, None, ALU.mult), m2))
        nlo = op("vector", "u2", lambda e: e.tensor_scalar(loS[:, :], loS[:, :], -1.0, None, ALU.mult), te[-1])
        t_ss = []
        for st, dd in ((loTb, loSd), (sfb, sfd)):
            t_ss.append(dma("sync", "rx", lambda e, st=st, dd=dd: e.dma_start(dd[0:768 * 128].rearrange("(c p n) -> p c n", p=128, n=128), st[:, 0:6, :]), te[-1]))
            t_ss.append(dma("sync", "rx", lambda e, st=st, dd=dd: e.dma_start(dd[768 * 128:T * 128].rearrange("(p n) -> p n", n=128), st[0:64, 6, :]), te[-1]))

        b = carve(R2)
        KR = 8
        Kr = [b(512) for _ in range(KR)]
        prod = [b(512) for _ in range(3)]
        ohT = [b(8 * 128).rearrange("p (t n) -> p t n", n=128) for _ in range(2)]
        c3 = carve(small)
        oh = [c3(8 * 128).rearrange("p (t n) -> p t n", n=128) for _ in range(2)]
        sfr = [c3(128, bf16) for _ in range(2)]
        Lr = [c3(128).rearrange("p (h t) -> p h t", h=8) for _ in range(2)]
        Fs = [c3(128) for _ in range(2)]
        Fe = [c3(9 * 16).rearrange("p (h t) -> p h t", h=9) for _ in range(2)]
        pen = [c3(16) for _ in range(2)]
        fe2 = [op("vector", "v", lambda e, k=k: e.memset(Fe[k][:, 8, :], 1.0), t_ss) for k in range(2)]
        rt, oht, kt, qt, prt, redt, sft, lb = {}, {}, {}, {}, {}, {}, {}, {}
        clr = [s1, s2, s3]
        QB = (0, 1, 2, 6, 7)

        def regs(eng_name, tag):
            return {"r": None, "tag": tag, "eng": eng_name}

        def load_regs(st, b_):
            def f(e):
                if st["r"] is None:
                    st["r"] = [e.alloc_register(f"{st['tag']}{j}") for j in range(16)]
                return e.reg_load(st["r"], widr[0:1, 16 * b_:16 * b_ + 16])
            P.plain(st["eng"], f, t_wid)

        def win(e, st, t):
            return e.snap(st["r"][t % 16], min_val=0, max_val=W - 1)

        def in_slots(jobs):
            for _, _, f in sorted(((s_, n_, f) for n_, (s_, f) in enumerate(jobs)), key=lambda z: z[:2]):
                f()

        def rows2(b_, store, tag, wait):
            store[b_] = dma("sync", f"{tag}{b_ % 2}", lambda e: e.dma_start(rowR[:, b_ % 2, :], loSd[2048 * b_:2048 * b_ + 2048]
                            .rearrange("(a n) -> a n", a=1).broadcast_to([128, 2048])), wait)

        def one_hot_T(h_, rtok, store, free):
            b_ = h_ // 2
            o = ohT[h_ % 2]
            v = op("scalar", "oh", lambda e: e.activation(o, rowR[:, b_ % 2, 1024 * (h_ % 2):1024 * (h_ % 2) + 1024].rearrange("p (t n) -> p t n", n=128),
                   ACT.Abs, bias=npidx[:, 0:1]), rtok[b_], free)
            store[h_] = op("scalar", "oh", lambda e: e.activation(o, o, ACT.Relu, bias=one1[:, 0:1], scale=-1.0), v)

        def one_hot(h_, j, neg, store, free):
            t = 8 * h_ + j
            o = oh[h_ % 2]
            store[(h_, "a")] = op("scalar", "eo", lambda e: e.activation(o[:, j, :], iotaF[:, :], ACT.Abs, bias=neg[:, t:t + 1]), free)
            if j == 7:
                store[h_] = op("scalar", "eo", lambda e: e.activation(o, o, ACT.Relu, bias=one1[:, 0:1], scale=-1.0), store[(h_, "a")])

        def gather_k(t):
            kt[t] = dma("gpsimd", f"k{t % KR}", lambda e: e.indirect_dma_start(Kr[t % KR], None, Kd, bass.IndirectOffsetOnAxis(ap=dstS[:, t:t + 1], axis=0),
                        bounds_check=N - 1, oob_is_err=False), prt.get(t - KR), clr, proj_all, phaseA)

        pe1 = regs("tensor", "pw")
        dv1 = regs("vector", "dw")

        def p1_q(t):
            if t % 16 == 0:
                load_regs(pe1, t // 16)
            qt[t] = op("tensor", "q1", lambda e: e.matmul(BK[QB[t % 5]], ohT[(t // 8) % 2][:, t % 8, :], Qall[:, bass.ds(win(e, pe1, t), 1), :],
                       start=True, stop=True), oht[t // 8], prt.get(t - 5), t_q, t_q2, te[-1])

        def p1_pr(t):
            prt[t] = op("vector", "pr", lambda e: e.tensor_tensor(prod[t % 3], BK[QB[t % 5]], Kr[t % KR], ALU.mult), qt[t], kt[t], redt.get(t - 3))

        def p1_rd(t):
            b_, k = t // 16, t // 16 % 2
            redt[t] = op("vector", "rd", lambda e: e.tensor_reduce(Lr[k][:, :, t % 16], prod[t % 3].rearrange("p (h d) -> p h d", h=8), AX.X, ALU.add),
                         prt[t], lb.get(b_ - 2), t_ss)

        fet, eot, mt, mu, pent = {}, {}, {}, {}, {}

        def p1_lb(b_):
            lb[b_] = op("vector", "lb", lambda e: e.tensor_tensor(L[:, b_, :, :], L[:, b_, :, :], Lr[b_ % 2], ALU.add), redt[16 * b_ + 15], s3)

        def p1_sf(b_):
            sft[b_] = dma("sync", f"sf{b_ % 2}", lambda e: e.dma_start(sfr[b_ % 2], sfd[2048 * b_:2048 * b_ + 2048].rearrange("(a t n) -> a t n", a=1, n=128)
                          .broadcast_to([8, 16, 128])), t_ss, fet.get((b_ - 2, "s")))

        def p1_t1(b_):
            fet[(b_, "t")] = op("tensor", "lt", lambda e: e.transpose(BK[3][:, 0:128], L[:, b_, :, :].rearrange("p h t -> p (h t)"), ident[:, :]), lb[b_],
                                fet.get(b_ - 1))

        def p1_scan(b_):
            fet[(b_, "s")] = op("vector", "sc", lambda e: e.tensor_tensor_scan(Fs[b_ % 2], sfr[b_ % 2], BK[3][:, 0:128], -BIG, ALU.add, ALU.max),
                                fet[(b_, "t")], sft[b_], fet.get((b_ - 2, "p")))

        def p1_t2(b_):
            k = b_ % 2
            m2 = fet[(b_, "p")] = op("tensor", "lt", lambda e: e.transpose(BK[3][:, 128:256], Fs[k], ident[:, :]), fet[(b_, "s")])
            fet[b_] = op("scalar", "fe", lambda e: e.copy(Fe[k][:, 0:8, :], BK[3][:, 128:256].rearrange("p (h t) -> p h t", h=8)), m2, mt.get(16 * (b_ - 2) + 15), fe2)

        def p1_mt(t):
            b_, k, j = t // 16, t // 16 % 2, t % 16
            mt[t] = op("tensor", "mt", lambda e: e.matmul(BK[4 + k][:, 16 * j:16 * j + 9], oh[(t // 8) % 2][:, t % 8, :], Fe[k][:, :, j], start=True, stop=True),
                       eot[t // 8], fet[b_], mu.get(16 * (b_ - 2) + 15), te[-1])

        def p1_pen(b_):
            k = b_ % 2
            load_regs(dv1, b_)
            pent[b_] = op("vector", "mu", lambda e: e.tensor_scalar(pen[k], BK[4 + k][:, 0:256].rearrange("p (t n) -> p t n", n=16)[:, :, 8], -1.0, BIG,
                          ALU.add, ALU.mult), mt[16 * b_ + 15], mu.get(16 * b_ - 17))

        def p1_mu(t):
            b_, k, j = t // 16, t // 16 % 2, t % 16

            def f(e):
                mw = Mall[:, bass.ds(win(e, dv1, t), 1), :].rearrange("p a n -> p (a n)")
                return e.scalar_tensor_tensor(mw, BK[4 + k][:, 16 * j:16 * j + 8], pen[k][:, j:j + 1], mw, ALU.add, ALU.max)
            mu[t] = op("vector", "mu", f, pent[b_], mu.get(t - 1), s4)

        rows2(0, rt, "r", [t_ss, ATt[NCH - 1]])
        rows2(1, rt, "r", [t_ss, ATt[NCH - 1]])
        one_hot_T(0, rt, oht, [clr, c_np])
        one_hot_T(1, rt, oht, [clr, c_np])
        for t in range(KR):
            gather_k(t)
        jobs = []
        job = lambda s_, f: jobs.append((s_, f))
        for b_ in range(NB):
            s_ = 16 * b_
            if b_ >= 2:
                job(s_ - 16 - 6.5, lambda b_=b_: rows2(b_, rt, "r", [t_ss, oht[2 * b_ - 3]]))
            job(s_ + 2, lambda b_=b_: p1_sf(b_))
            job(s_ + 18.6, lambda b_=b_: p1_lb(b_))
            job(s_ + 20.6, lambda b_=b_: p1_t1(b_))
            job(s_ + 22.6, lambda b_=b_: p1_scan(b_))
            job(s_ + 24.6, lambda b_=b_: p1_t2(b_))
            for i in range(2):
                for j in range(8):
                    job(s_ + 18.7 + 8 * i + j, lambda b_=b_, i=i, j=j: one_hot(2 * b_ + i, j, loEnd, eot, [mt.get(8 * (2 * b_ + i) - 9), te[-1], t_ss]))
            for j in range(16):
                job(s_ + 27.2 + j, lambda t=16 * b_ + j: p1_mt(t))
            job(s_ + 45.2, lambda b_=b_: p1_pen(b_))
            for j in range(16):
                job(s_ + 46.4 + 0.5 * j - (0.2 if j % 2 else 0), lambda t=16 * b_ + j: p1_mu(t))
        for h_ in range(2, 2 * NB):
            job(8 * h_ - 6.4, lambda h_=h_: one_hot_T(h_, rt, oht, [qt[8 * h_ - 9]]))
        for t in range(T):
            job(t, lambda t=t: p1_q(t))
            job(t + 1.3, lambda t=t: p1_pr(t))
            job(t + 2.5, lambda t=t: p1_rd(t))
            if t + KR < T:
                job(t + 1.35, lambda t=t: gather_k(t + KR))
        in_slots(jobs)
        mx_all = mu[T - 1]
        pass1 = [mu[T - 1], qt[T - 1], redt[T - 1], lb[NB - 1], mt[T - 1]]

        Yall = R1[:, :].rearrange("p (w n) -> p w n", n=YW)
        Vr, pv = Kr, prod
        YB = [PS[:, 0:1024], PS[:, 1024:2048], PS[:, 3072:4096]]
        rt2, oht2, vt, mgt, pt, pvt, yt, ya, oh2, lst = {}, {}, {}, {}, {}, {}, {}, {}, {}, {}

        def gather_v(t):
            vt[t] = dma("gpsimd", f"k{t % KR}", lambda e: e.indirect_dma_start(Vr[t % KR], None, Vd, bass.IndirectOffsetOnAxis(ap=dstS[:, t:t + 1], axis=0),
                        bounds_check=N - 1, oob_is_err=False), prt[T - KR + t % KR] if t < KR else pvt[t - KR])

        def p2_mg(t):
            b_, k, j = t // 16, t // 16 % 2, t % 16
            if j == 0:
                load_regs(pe1, b_)
            mgt[t] = op("tensor", "mg", lambda e: e.matmul(BK[4 + k][:, 8 * j:8 * j + 8], ohT[(t // 8) % 2][:, t % 8, :],
                        Mall[:, bass.ds(win(e, pe1, t), 1), :], start=True, stop=True), oht2[t // 8], lst.get(b_ - 2), mx_all)

        def p2_p(b_):
            k = b_ % 2
            lst[b_] = op("vector", "lp", lambda e: e.tensor_tensor(L[:, b_, :, :], L[:, b_, :, :], BK[4 + k][:, 0:128].rearrange("p (t h) -> p h t", h=8), ALU.subtract),
                         mgt[16 * b_ + 15], mx_all)
            pt[b_] = op("scalar", "ex", lambda e: e.activation(L[:, b_, :, :], L[:, b_, :, :], ACT.Exp), lst[b_])

        def p2_pv(t):
            ph = L[:, t // 16, :, t % 16]
            pvt[t] = op("vector", "pv", lambda e: e.tensor_tensor(pv[t % 3].rearrange("p (h d) -> p h d", h=8), Vr[t % KR].rearrange("p (h d) -> p h d", h=8),
                        ph.rearrange("p (h a) -> p h a", a=1).broadcast_to([128, 8, 64]), ALU.mult), vt[t], pt[t // 16], yt.get(t - 3), pass1)
            o = oh[(t // 8) % 2][:, t % 8, :]
            op("tensor", "yt", lambda e: e.matmul(YB[t % 3][:, 512:520], o, ph, start=True, stop=True), pt[t // 16], oh2[t // 8], ya.get(t - 3), pass1)
            yt[t] = op("tensor", "yt", lambda e: e.matmul(YB[t % 3][:, 0:512], o, pv[t % 3], start=True, stop=True), pvt[t])

        def p2_ya(t):
            if t % 16 == 0:
                load_regs(dv1, t // 16)

            def f(e):
                yw = Yall[:, bass.ds(win(e, dv1, t), 1), :].rearrange("p a n -> p (a n)")
                return e.tensor_tensor(yw, yw, YB[t % 3][:, 0:520], ALU.add)
            ya[t] = op("vector", "ya", f, yt[t], ya.get(t - 1), y0, y1)

        rows2(0, rt2, "r", [oht[2 * NB - 1]])
        rows2(1, rt2, "r", [oht[2 * NB - 1]])
        one_hot_T(0, rt2, oht2, qt[T - 1])
        one_hot_T(1, rt2, oht2, qt[T - 1])
        for t in range(KR):
            gather_v(t)
        HW_ = (W * YW) // 2
        y0 = op("vector", "v", lambda e: e.memset(R1[:, 0:HW_], 0.0), pass1)
        y1 = op("gpsimd", "g", lambda e: e.memset(R1[:, HW_:W * YW], 0.0), pass1)
        jobs.clear()
        for b_ in range(NB):
            s_ = 16 * b_
            if b_ >= 2:
                job(s_ - 28, lambda b_=b_: rows2(b_, rt2, "r", [oht2[2 * b_ - 3]]))
            for j in range(16):
                job(s_ - 14.9 + 0.5 * j, lambda t=16 * b_ + j: p2_mg(t))
            job(s_ - 4.6, lambda b_=b_: p2_p(b_))
            for i in range(2):
                for j in range(8):
                    job(s_ + 8 * i + j - 8.7, lambda b_=b_, i=i, j=j: one_hot(2 * b_ + i, j, loS, oh2, [yt.get(8 * (2 * b_ + i) - 9), nlo, pass1]))
        for h_ in range(2, 2 * NB):
            job(8 * h_ - 20 if h_ % 2 == 0 else 8 * h_ - 25, lambda h_=h_: one_hot_T(h_, rt2, oht2, [mgt[8 * h_ - 9]]))
        for t in range(T):
            job(t, lambda t=t: p2_pv(t))
            job(t + 2.3, lambda t=t: p2_ya(t))
            if t + KR < T:
                job(t + 0.1, lambda t=t: gather_v(t + KR))
        in_slots(jobs)
        pass2 = [ya[T - 1], yt[T - 1], pvt[T - 1]]

        d = carve(R2)
        e_ = carve(R3)
        WoS = d(2048).rearrange("p (c n) -> p c n", c=4)
        xr = [d(512) for _ in range(4)]
        yn = [d(512) for _ in range(2)]
        yT = [d(512).rearrange("p (c n) -> p c n", c=4) for _ in range(2)]
        xn = [d(512) for _ in range(4)]
        h1 = [e_(512) for _ in range(3)]
        h2 = [e_(512) for _ in range(3)]
        FT = e_(512)
        W0 = e_(320)
        W1a = e_(192)
        W1s = e_(192)
        W1b = e_(320)
        W2t = e_(12)
        b01 = e_(6)
        b2r = e_(4)
        boT = e_(3 * 512, bf16).rearrange("p (r n) -> p r n", r=3)
        boF = e_(512)
        boS = e_(512, bf16)
        DF = 6
        sc = [e_(160) for _ in range(4)]
        ini = [op("vector", "w", lambda e, t_=t_: e.memset(t_, 0.0), pass2) for t_ in (W1a, W1s, W1b, W2t, b01, b2r)]
        ft0 = op("vector", "w", lambda e: e.memset(FT, 0.0))
        wt = []

        def wload(dst_, src_):
            wt.append(dma("sync", "wt", lambda e: e.dma_start(dst_, src_, allow_slow_non_contiguous=True), ini, pass2))

        wload(WoS, wo.rearrange("(c p) n -> p c n", p=128))
        wt += split_bias("b4", (bo,), boF, boF, boT, boS, pass2)
        for pi_, (wT, bb) in enumerate(((waT, ba), (wsT, bs))):
            o = 160 * pi_
            for k_, r_ in enumerate((0, 1, 35, 36)):
                wload(W0[k_:k_ + 1, 128 * pi_:128 * pi_ + 128], wT[0, r_:r_ + 1, 0:128])
                wload(W0[k_:k_ + 1, 256 + 32 * pi_:288 + 32 * pi_], wT[0, r_:r_ + 1, 128:160])
            W1 = (W1a, W1s)[pi_]
            wload(W1[:, 0:128], wT[1, 0:128, 0:128])
            wload(W1[:, 128 + 32 * pi_:160 + 32 * pi_], wT[1, 0:128, 128:160])
            wload(W1b[32 * pi_:32 * pi_ + 32, 128 * pi_:128 * pi_ + 128], wT[1, 128:160, 0:128])
            wload(W1b[32 * pi_:32 * pi_ + 32, 256 + 32 * pi_:288 + 32 * pi_], wT[1, 128:160, 128:160])
            wload(W2t[:, 4 * pi_ + 2 * pi_:4 * pi_ + 2 * pi_ + 2], wT[2, 0:128, 100:102])
            wload(W2t[32 * pi_:32 * pi_ + 32, 8 + 2 * pi_:10 + 2 * pi_], wT[2, 128:160, 100:102])
            for l in range(2):
                wload(b01[:, 3 * l + pi_:3 * l + pi_ + 1], bb[l, 0:128].rearrange("(p a) -> p a", a=1))
                wload(b01[32 * pi_:32 * pi_ + 32, 3 * l + 2:3 * l + 3], bb[l, 128:160].rearrange("(p a) -> p a", a=1))
            wload(b2r[:, 2 * pi_:2 * pi_ + 2], bb[2:3, 100:102].broadcast_to([128, 2]))
        w16 = small[:, 1024:1088].rearrange("p (a n) -> p a n", a=4)
        iw = op("vector", "w", lambda e: e.tensor_scalar(w16, iotaF[:, 0:16].rearrange("p (a n) -> p a n", a=1).broadcast_to([128, 4, 16]), -1.0, 16.0, ALU.mult, ALU.add))

        xt3, ynt, yTt, ot, x1t, xnt, outt, pst = {}, {}, {}, {}, {}, {}, {}, {}
        o_all = []
        res = {}

        def f_load(w):
            n = rows_of[w]
            xt3[w] = dma("sync", f"x{w % 4}" if w % 4 < 3 else "x3", lambda e: e.dma_start(xr[w % 4][0:n, :], x[128 * w:128 * w + n, :]), outt.get(w - 4), pass2)

        def f_y(w):
            n, k = rows_of[w], w % 2
            s = sc[w % 4]
            y = Yall[0:n, w, 0:512]
            u = op("vector", "fy", lambda e: e.tensor_scalar(s[0:n, 0:8], Yall[0:n, w, 512:520], 1e-30, None, ALU.max), pass2, res.get(w - 4))
            u = op("vector", "fy", lambda e: e.reciprocal(s[0:n, 8:16], s[0:n, 0:8]), u)
            ynt[w] = op("vector", "fy", lambda e: e.tensor_tensor(yn[k][0:n, :].rearrange("p (h d) -> p h d", h=8), y.rearrange("p (h d) -> p h d", h=8),
                        s[0:n, 8:16].rearrange("p (h a) -> p h a", a=1).broadcast_to([n, 8, 64]), ALU.mult), u, yTt.get((w - 2, "T")))
            for c in range(4):
                last = op("tensor", "ft", lambda e, c=c: e.transpose(BK[0][:, 128 * c:128 * c + n], yn[k][0:n, 128 * c:128 * c + 128], ident[0:n, 0:n]),
                          ynt[w], yTt.get(w - 1), pass2)
            yTt[(w, "T")] = last
            yTt[w] = op("scalar", "fa", lambda e: e.copy(yT[k][:, :, 0:n], BK[0][:, :].rearrange("p (c n) -> p c n", c=4)[:, :, 0:n]), last, ot.get(w - 2))
            for c in range(4):
                op("tensor", "fo", lambda e, c=c: e.matmul(BK[1 + k][0:n, :], yT[k][:, c, 0:n], WoS[:, c, :], start=(c == 0), stop=False), yTt[w], wt, x1t.get(w - 2))
            ot[w] = op("tensor", "fo", lambda e: e.matmul(BK[1 + k][0:n, :], ones[0:3, 0:n], boS[0:3, :], start=False, stop=True))

        def f_ln(w):
            n, k = rows_of[w], w % 2
            xx, xo, s = xr[w % 4], xn[w % 4], sc[w % 4]
            x1t[w] = op("vector", "fl", lambda e: e.tensor_tensor(xx[0:n, :], xx[0:n, :], BK[1 + k][0:n, :], ALU.add), ot[w], xt3[w])
            b5 = ln_stats(w, xx[0:n, :], n, x1t[w], "l2", w % 2)
            v = op("vector", "fl", lambda e: e.tensor_scalar(xo[0:n, :], xx[0:n, :], mv[0:n, k, 0:1], rs[0:n, k, 0:1], ALU.subtract, ALU.mult), b5, res.get(w - 4))
            xs = op("gpsimd", "fg", lambda e: e.tensor_tensor(xx[0:n, :], xx[0:n, :], xo[0:n, :], ALU.add), v)
            xnt[(w, "s")] = xs
            v1 = op("vector", "fl", lambda e: e.scalar_tensor_tensor(s[0:n, 32:96].rearrange("p (a n) -> p a n", a=4), xo[0:n, 16:80].rearrange("p (a n) -> p a n", a=4), 0.5,
                    w16[0:n, :, :], ALU.is_gt, ALU.mult), v, iw)
            v2 = op("vector", "fl", lambda e: e.tensor_reduce(s[0:n, 96:100], s[0:n, 32:96].rearrange("p (a n) -> p a n", a=4), AX.X, ALU.max), v1)
            v3 = op("vector", "fl", lambda e: e.tensor_scalar(s[0:n, 100:104], s[0:n, 96:100], -1.0, 16.0, ALU.mult, ALU.add), v2)
            fv = s[0:n, 104:112].rearrange("p (q f) -> p q f", q=2)
            v4 = op("vector", "fl", lambda e: e.scalar_tensor_tensor(fv[:, :, 0:2].rearrange("p q f -> p f q"), s[0:n, 96:100].rearrange("p (f q) -> p f q", f=2), 0.0,
                    s[0:n, 100:104].rearrange("p (f q) -> p f q", f=2), ALU.is_gt, ALU.mult), v3)
            v5 = op("vector", "fl", lambda e: e.tensor_copy(fv[:, :, 2:4], xo[0:n, 105:107].rearrange("p (a f) -> p a f", a=1).broadcast_to([n, 2, 2])), v)
            v6 = op("vector", "fl", lambda e: e.tensor_scalar(s[0:n, 112:115], xo[0:n, 0:3], 0.5, None, ALU.is_gt), v)
            xnt[w] = [v4, v5, v6]

        def f_masks(w):
            n, s = rows_of[w], sc[w % 4]
            mk, ad, su = s[0:n, 112:113], s[0:n, 113:114], s[0:n, 114:115]
            u1 = op("vector", "fm", lambda e: e.tensor_tensor(s[0:n, 115:116], mk, ad, ALU.mult), xnt[w])
            u2 = op("vector", "fm", lambda e: e.tensor_tensor(s[0:n, 116:117], mk, su, ALU.mult), u1)
            u3 = op("vector", "fm", lambda e: e.tensor_scalar(s[0:n, 119:120], ad, -1.0, 1.0, ALU.mult, ALU.add), u1)
            u4 = op("vector", "fm", lambda e: e.tensor_tensor(s[0:n, 116:117], s[0:n, 116:117], s[0:n, 119:120], ALU.mult), u3, u2)
            u5 = op("vector", "fm", lambda e: e.tensor_tensor(s[0:n, 117:118], s[0:n, 115:116], s[0:n, 116:117], ALU.add), u4)
            u6 = op("vector", "fm", lambda e: e.tensor_scalar(s[0:n, 118:119], s[0:n, 117:118], 2.0, None, ALU.mult), u5)
            return u6

        ftt, h1t, h2t, l3 = {}, {}, {}, {}

        def f_ffn(g):
            ws = [w for w in (2 * g, 2 * g + 1) if w < W]
            last = None
            for i, w in enumerate(ws):
                n, s = rows_of[w], sc[w % 4]
                for q in range(2):
                    last = op("tensor", "fq", lambda e, i=i, q=q, n=n, s=s: e.transpose(BK[3][0:4, 256 * i + 128 * q:256 * i + 128 * q + n], s[0:n, 104 + 4 * q:108 + 4 * q],
                              ident[0:n, 0:n]), xnt[w], h1t.get((g - 1, "f")))
            evs = []
            for i, w in enumerate(ws):
                n = rows_of[w]
                v = BK[3][0:4, 256 * i:256 * i + 256].rearrange("p (q n) -> p q n", q=2)[:, :, 0:n]
                o = FT[0:4, 256 * i:256 * i + 256].rearrange("p (q n) -> p q n", q=2)[:, :, 0:n]
                evs.append(op("scalar", "fa", lambda e, o=o, v=v: e.copy(o, v), last, h1t.get((g - 1, "m")), ft0))
            h1t[(g, "f")] = evs[-1]
            h1t[(g, "e")] = evs

        def f_h1(g):
            ws = [w for w in (2 * g, 2 * g + 1) if w < W]
            evs = h1t[(g, "e")]
            C = 256 * len(ws)
            mm = []
            for k_, (c0, m_) in enumerate(((0, 128), (128, 128), (256, 64))):
                mm.append(op("tensor", "h1", lambda e, k_=k_, c0=c0, m_=m_: e.matmul(BK[4 + k_][0:m_, 0:C], W0[0:4, c0:c0 + m_], FT[0:4, 0:C], start=True, stop=True),
                             evs, wt, h2t.get((g - 1, k_))))
            h1t[(g, "m")] = mm[-1]
            r = []
            for k_, m_ in enumerate((128, 128, 64)):
                r.append(op("scalar", "fa", lambda e, k_=k_, m_=m_: e.activation(h1[k_][0:m_, 0:C], BK[4 + k_][0:m_, 0:C], ACT.Relu, bias=b01[0:m_, k_:k_ + 1]),
                            mm[k_], h2t.get((g - 1, "mm"))))
            h1t[(g, "r")] = r

        def f_h2(g):
            ws = [w for w in (2 * g, 2 * g + 1) if w < W]
            r = h1t[(g, "r")]
            C = 256 * len(ws)
            m2 = []
            for k_, terms in enumerate((((W1a[:, 0:128], 0, 128), (W1b[0:64, 0:128], 2, 64)),
                                        ((W1s[:, 0:128], 1, 128), (W1b[0:64, 128:256], 2, 64)),
                                        ((W1a[:, 128:192], 0, 128), (W1s[:, 128:192], 1, 128), (W1b[0:64, 256:320], 2, 64)))):
                m_ = 64 if k_ == 2 else 128
                for i, (lw, hi_, kk) in enumerate(terms):
                    t_ = op("tensor", "h2", lambda e, k_=k_, lw=lw, hi_=hi_, kk=kk, i=i, m_=m_, nt=len(terms): e.matmul(
                        BK[4 + k_][0:m_, 0:C], lw, h1[hi_][0:kk, 0:C], start=(i == 0), stop=(i == nt - 1)), r)
                m2.append(t_)
            h2t[(g, "mm")] = m2[-1]
            for k_, m_ in enumerate((128, 128, 64)):
                h2t[(g, k_)] = op("scalar", "fa", lambda e, k_=k_, m_=m_: e.activation(h2[k_][0:m_, 0:C], BK[4 + k_][0:m_, 0:C], ACT.Relu, bias=b01[0:m_, 3 + k_:4 + k_]),
                                  m2[k_], l3.get(g - 1))

        def f_out(g):
            ws = [w for w in (2 * g, 2 * g + 1) if w < W]
            for i, w in enumerate(ws):
                n = rows_of[w]
                for q in range(2):
                    c0 = 256 * i + 128 * q
                    for k_, kk in enumerate((128, 128, 64)):
                        t_ = op("tensor", "h3", lambda e, k_=k_, kk=kk, c0=c0, n=n, i=i, q=q: e.matmul(BK[7][0:n, 8 * i + 4 * q:8 * i + 4 * q + 4], h2[k_][0:kk, c0:c0 + n],
                                W2t[0:kk, 4 * k_:4 * k_ + 4], start=(k_ == 0), stop=(k_ == 2)), h2t[(g, 2)], h2t[(g, 0)], h2t[(g, 1)], wt,
                                res.get(2 * g - 1), res.get(2 * g - 2))
            l3[g] = t_
            for i, w in enumerate(ws):
                n, s = rows_of[w], sc[w % 4]
                xx = xr[w % 4]
                um = f_masks(w)
                r4 = s[0:n, 124:132].rearrange("p (q c) -> p q c", q=2)
                u = op("vector", "fz", lambda e, i=i, n=n, r4=r4: e.tensor_tensor(r4, BK[7][0:n, 8 * i:8 * i + 8].rearrange("p (q c) -> p q c", q=2),
                       b2r[0:n, :].rearrange("p (a c) -> p a c", a=1).broadcast_to([n, 2, 4]), ALU.add), l3[g], wt, um)
                psf = u
                u = op("vector", "fz", lambda e, r4=r4, s=s, n=n: e.tensor_scalar(r4[:, :, 2:4], r4[:, :, 2:4], s[0:n, 116:117], None, ALU.mult), u)
                u = op("vector", "fz", lambda e, r4=r4, s=s, n=n: e.scalar_tensor_tensor(r4[:, :, 0:2], r4[:, :, 0:2], s[0:n, 115:116], r4[:, :, 2:4], ALU.mult, ALU.add), u)
                u = op("vector", "fz", lambda e, r4=r4: e.tensor_scalar(r4[:, :, 0:2], r4[:, :, 0:2], 0.0, 15.0, ALU.max, ALU.min), u)
                u = op("vector", "fz", lambda e, r4=r4: e.tensor_scalar(r4[:, :, 0:2], r4[:, :, 0:2], 12582912.0, 12582912.0, ALU.add, ALU.subtract), u)
                vs = []
                for q in range(2):
                    vs.append(op("vector", "fz", lambda e, q=q, r4=r4, s=s, n=n: e.tensor_scalar(s[0:n, 16 * q:16 * q + 16], iotaF[0:n, 0:16], r4[:, q, 0:1], s[0:n, 118:119],
                              ALU.is_equal, ALU.mult), u, ynt[w]))
                vs.append(op("vector", "fz", lambda e, r4=r4, s=s, n=n: e.tensor_scalar(s[0:n, 32:33], r4[:, 1, 1:2], 0.5, s[0:n, 117:118], ALU.is_gt, ALU.mult), u))
                res[w] = op("vector", "fz", lambda e, xx=xx, s=s, n=n: e.tensor_tensor(xx[0:n, 128:161], xx[0:n, 128:161], s[0:n, 0:33], ALU.add), vs, xnt[(w, "s")])
                outt[w] = dma("sync", f"o{w % 4}", lambda e, w=w, n=n, xx=xx: e.dma_start(out[128 * w:128 * w + n, :], xx[0:n, :]), res[w], xnt[(w, "s")])
                o_all.append(outt[w])

        for w in range(4):
            f_load(w)
        G = (W + 1) // 2

        def f_win(w, f):
            if w < W:
                f(w)

        for w in (0, 1):
            f_y(w)
            f_ln(w)
        for g in range(G):
            f_ffn(g)
            f_win(2 * g + 2, f_y)
            f_h1(g)
            f_win(2 * g + 3, f_y)
            f_h2(g)
            f_win(2 * g + 2, f_ln)
            f_out(g)
            f_win(2 * g + 3, f_ln)
            for w in (2 * g + 4, 2 * g + 5):
                f_win(w, f_load)
        P.plain("sync", None, o_all)

        block = ctx.enter_context(nc.Block())

        @block.sync
        def _(e):
            P.emit("sync", e)

        @block.gpsimd
        def _(e):
            P.emit("gpsimd", e)

        @block.scalar
        def _(e):
            P.emit("scalar", e)

        @block.vector
        def _(e):
            P.emit("vector", e)

        @block.tensor
        def _(e):
            P.emit("tensor", e)


_INS = ['x', 'src', 'dst', 'edge_attr_8', 'L0_gnn_Wq', 'L0_gnn_bq', 'L0_gnn_Wk', 'L0_gnn_bk', 'L0_gnn_Wv', 'L0_gnn_bv',
        'L0_gnn_Wo', 'L0_gnn_bo', 'L0_ffn_Wa', 'L0_ffn_ba', 'L0_ffn_Ws', 'L0_ffn_bs']
_OUTS = [((6250, 512), 'float32')]


def kernel(**inputs):
    import numpy as _np
    import concourse.bacc as _bacc
    from concourse import mybir as _mybir
    from concourse.bass_utils import run_bass_kernel_spmd as _run

    nc = _bacc.Bacc("TRN2", target_bir_lowering=False, num_devices=1)
    arrays, args = {}, []
    for name in _INS:
        a = _np.asarray(inputs[name])
        if name in ('L0_ffn_Wa', 'L0_ffn_Ws'):
            a = a.transpose(0, 2, 1)
        a = _np.ascontiguousarray(a)
        arrays[f"in_{name}_dram"] = a
        args.append(nc.dram_tensor(f"in_{name}_dram", a.shape, _mybir.dt.from_np(a.dtype), kind="ExternalInput").ap())
    for i, (shape, dtype) in enumerate(_OUTS):
        args.append(nc.dram_tensor(f"out_{i}_dram", shape, _mybir.dt.from_np(_np.dtype(dtype)), kind="ExternalOutput").ap())
    build(nc, *args)
    r = _run(nc, [arrays], core_ids=[0])
    return r.results[0]["out_0_dram"]
```

```python
import concourse.bass as bass
from concourse import mybir
from contextlib import ExitStack


class Program:

    def __init__(self, nc, ctx):
        self.nc, self.ctx = nc, ctx
        self.queues = {e: [] for e in ("sync", "gpsimd", "scalar", "vector", "tensor")}
        self.sems, self.counts = {}, {}

    def token(self, stream, n):
        if stream not in self.sems:
            self.sems[stream] = self.ctx.enter_context(self.nc.semaphore("s_" + stream))
            self.counts[stream] = 0
        self.counts[stream] += n
        return (stream, self.counts[stream])

    def op(self, eng, stream, fn, *waits):
        tok = self.token(stream, 1)
        self.queues[eng].append((fn, waits, stream, 1))
        return tok

    def dma(self, eng, stream, fn, *waits):
        tok = self.token(stream, 16)
        self.queues[eng].append((fn, waits, stream, 16))
        return tok

    def plain(self, eng, fn, *waits):
        self.queues[eng].append((fn, waits, None, 0))

    def emit(self, name, eng):
        seen = {}

        def flat(ws):
            for w in ws:
                if isinstance(w, list):
                    yield from flat(w)
                elif w is not None:
                    yield w

        for fn, waits, stream, n in self.queues[name]:
            need = {}
            for s, v in flat(waits):
                need[s] = max(need.get(s, 0), v)
            for s, v in need.items():
                if seen.get(s, 0) < v:
                    eng.wait_ge(self.sems[s], v)
                    seen[s] = v
            if fn is None:
                continue
            ins = fn(eng)
            if stream is not None:
                ins.then_inc(self.sems[stream], n)


def build(nc, x, src, dst, attr, wq, bq, wk, bk, wv, bv, wo, bo, waT, ba, wsT, bs, out):
    f32, i32 = mybir.dt.float32, mybir.dt.int32
    bf16, u16 = mybir.dt.bfloat16, mybir.dt.uint16
    ALU, ACT, AX = mybir.AluOpType, mybir.ActivationFunctionType, mybir.AxisListType
    N, E, D = 6250, 100000, 512
    W = 49
    TS = 782
    T = 832
    NB = T // 16
    REC = 10
    YW = 520
    BIG = 1.0e30
    rows_of = [min(128, N - 128 * w) for w in range(W)]

    ctx = ExitStack()
    with ctx:
        P = Program(nc, ctx)
        op, dma = P.op, P.dma

        def sb(name, shape, dt):
            return ctx.enter_context(nc.sbuf_tensor(name, shape, dt))

        def dram(name, shape, dt):
            return nc.dram_tensor(name, shape, dt, kind="Internal").ap()

        Qd = dram("q_scratch", (W * 128, D), f32)
        Kd = dram("k_scratch", (N, D), f32)
        Vd = dram("v_scratch", (N, YW), f32)
        recd = dram("rec_scratch", (128 * T, REC), f32)
        loTd = dram("lo_rows", (TS * 128,), bf16)
        srcTd = dram("src_rows", (TS * 128,), u16)
        loSd = dram("lo_sorted", (T * 128,), bf16)
        sfd = dram("seg_flags", (T * 128,), bf16)
        widd = dram("tile_window", (896,), i32)

        R1 = sb("R1", [128, W * YW], f32)
        R2 = sb("R2", [128, T * REC], f32)
        R3 = sb("R3", [128, TS * REC], f32)
        rowR = sb("rowR", [128, 2, 2048], bf16)
        ident = sb("ident", [128, 128], f32)
        iotaF = sb("iotaF", [128, 128], f32)
        pidx = sb("pidx", [128, 1], f32)
        loS = sb("loS", [128, T], f32)
        dstS = sb("dstS", [128, T], i32)
        endP = sb("endP", [128, T], f32)
        widr = sb("widr", [1, T], i32)
        Mall = sb("Mall", [128, W, 8], f32)
        small = sb("small", [128, 3200], f32)
        ones = sb("ones", [3, 128], bf16)
        npidx = sb("npidx", [128, 1], f32)
        fw = sb("fw", [128, 1048 + 256], f32)
        one1 = sb("one1", [128, 1], f32)
        PS = ctx.enter_context(nc.psum_tensor("banks", [128, 8 * 512], f32))
        BK = [PS[:, 512 * i:512 * i + 512] for i in range(8)]

        def carve(base, start=0):
            at = [start]

            def take(n, dt=f32):
                words = n if dt in (f32, i32) else (n + 1) // 2
                v = base[:, at[0]:at[0] + words]
                at[0] += words
                assert at[0] <= base.shape[1], (base.name, at[0])
                return v if dt == f32 else v.bitcast(dt)
            return take

        a = carve(R1)
        iotaI = a(128).bitcast(i32)
        pI = a(1).bitcast(i32)
        a(3)
        low = a(128)
        upp = a(128)
        onesf = a(128)
        W3 = [a(2048).rearrange("p (c n) -> p c n", c=4) for _ in range(3)]
        Bs = a(1536, bf16)
        ar = carve(R2)
        Bt = [ar(3 * 48, bf16).rearrange("p (r n) -> p r n", r=3) for _ in range(2)]
        Bf = [ar(48) for _ in range(2)]
        Br = [ar(48) for _ in range(2)]
        k1 = op("gpsimd", "cst", lambda e: e.iota(iotaI, pattern=[[1, 128]], base=0, channel_multiplier=0))
        k2 = op("gpsimd", "cst", lambda e: e.iota(pI, pattern=[[0, 1]], base=0, channel_multiplier=1))
        c_iota = op("vector", "cv", lambda e: e.tensor_copy(iotaF[:, :], iotaI), k1)
        c_pidx = op("vector", "cv", lambda e: e.tensor_copy(pidx[:, :], pI), k2)
        c_id = op("vector", "cv", lambda e: e.tensor_scalar(ident[:, :], iotaF[:, :], pidx[:, 0:1], None, ALU.is_equal), c_pidx)
        c_low = op("vector", "cv", lambda e: e.tensor_scalar(low, iotaF[:, :], pidx[:, 0:1], None, ALU.is_lt))
        c_upp = op("vector", "cv", lambda e: e.tensor_scalar(upp, iotaF[:, :], pidx[:, 0:1], None, ALU.is_gt))
        c_onesf = op("vector", "cv", lambda e: e.memset(onesf, 1.0))
        c_ones = op("vector", "cv", lambda e: e.memset(ones[:, :], 1.0))
        c_np = op("vector", "cv", lambda e: e.tensor_scalar(npidx[:, :], pidx[:, 0:1], -1.0, None, ALU.mult), c_pidx)
        c_one1 = op("vector", "cv", lambda e: e.memset(one1[:, :], 1.0))

        def load_bias(tag, parts, bf, wait):
            return [dma("sync", tag + "l", lambda e, i=i, b_=b_: e.dma_start(bf[0:32, 16 * i:16 * i + 16], b_.rearrange("(p n) -> p n", n=16)), wait)
                    for i, b_ in enumerate(parts)]

        def split_bias(tag, parts, bf, br, bt, dst3, ld):
            n = 16 * len(parts)
            u = op("vector", tag, lambda e: e.tensor_copy(bt[0:32, 0, 0:n], bf[0:32, 0:n]), ld)
            u = op("vector", tag, lambda e: e.tensor_tensor(br[0:32, 0:n], bf[0:32, 0:n], bt[0:32, 0, 0:n], ALU.subtract), u)
            u = op("vector", tag, lambda e: e.tensor_copy(bt[0:32, 1, 0:n], br[0:32, 0:n]), u)
            u = op("vector", tag, lambda e: e.tensor_tensor(bt[0:32, 2, 0:n], br[0:32, 0:n], bt[0:32, 1, 0:n], ALU.subtract), u)
            return [dma("sync", tag + "s", lambda e, i=i, j=j: e.dma_start(dst3[i:i + 1, 512 * j:512 * j + 512].rearrange("a (p n) -> a p n", n=16),
                        bt[0:32, i, 16 * j:16 * j + 16]), u) for i in range(3) for j in range(len(parts))]

        srcI = a(TS).bitcast(i32)
        dstI = a(TS).bitcast(i32)
        tI = a(TS).bitcast(i32)
        srcF = a(TS)
        hiF = a(TS)
        inv = a(TS)
        nlo0 = loS[:, 0:TS]
        rec = R3[:, :].rearrange("p (t r) -> p t r", r=REC)
        FULL = 127 * TS
        TAIL = E - FULL
        def2 = R2[:, :].rearrange("p (t r) -> p t r", r=REC)
        z1 = op("vector", "v", lambda e: e.memset(srcI[:, TAIL:TS], 8191))
        z2 = op("vector", "v", lambda e: e.memset(dstI[:, TAIL:TS], 0))
        d1 = op("gpsimd", "g", lambda e: e.memset(R2[:, :], 0.0))
        d2 = op("gpsimd", "g", lambda e: e.memset(def2[:, :, 8:9], -1.0), d1)
        ls = []
        for name, t_, v_ in (("ls", srcI, src), ("ld", dstI, dst)):
            zt = z1 if name == "ls" else z2
            ls.append([dma("sync", name, lambda e, t_=t_, v_=v_: e.dma_start(t_[0:127, :], v_[0:FULL].rearrange("(p t) -> p t", t=TS)), zt),
                       dma("sync", name, lambda e, t_=t_, v_=v_: e.dma_start(t_[127:128, 0:TAIL], v_[FULL:E].rearrange("(p t) -> p t", p=1)), zt)])
        t_def = dma("sync", "def", lambda e: e.dma_start(recd.rearrange("(p t) r -> p (t r)", p=128), R2[:, :]), d2)
        at8 = R2[:, 0:TS * 8]
        d3 = op("gpsimd", "g", lambda e: e.memset(R2[:, TAIL * 8:TS * 8], 0.0), t_def)
        la = [dma("sync", "la", lambda e: e.dma_start(at8[0:127, :], attr[0:FULL, :].rearrange("(p t) h -> p (t h)", t=TS)), d3, t_def),
              dma("sync", "la", lambda e: e.dma_start(at8[127:128, 0:TAIL * 8], attr[FULL:E, :].rearrange("(p t) h -> p (t h)", p=1)), d3, t_def)]
        wl = [dma("sync", f"w{n}", lambda e, n=n, w_=w_: e.dma_start(W3[n], w_.rearrange("(c p) n -> p c n", p=128)))
              for n, w_ in enumerate((wq, wk, wv))]
        r2 = op("vector", "v", lambda e: e.tensor_copy(rec[:, :, 9:10].bitcast(i32), dstI.rearrange("p (t a) -> p t a", a=1)), ls[1])
        r3 = op("vector", "v", lambda e: e.tensor_copy(srcF, srcI), ls[0])
        r4 = op("vector", "v", lambda e: e.tensor_scalar(tI, srcI, 7, None, ALU.logical_shift_right))
        r5 = op("vector", "v", lambda e: e.tensor_copy(hiF, tI), r4)
        r6 = op("vector", "v", lambda e: e.scalar_tensor_tensor(rec[:, :, 8:9].rearrange("p t a -> p (t a)"), hiF, -128.0, srcF, ALU.mult, ALU.add), r5)
        r7 = op("vector", "v", lambda e: e.tensor_scalar(inv, hiF, 48.5, 1048576.0, ALU.is_gt, ALU.mult), r5)
        r8 = op("vector", "v", lambda e: e.tensor_scalar(nlo0, rec[:, :, 8:9].rearrange("p t a -> p (t a)"), -1.0, None, ALU.mult), r6)
        loF = rec[:, :, 8]

        tr = []
        stl = a(7 * 128, bf16).rearrange("p (c n) -> p c n", c=7)
        stu = a(7 * 128, u16).rearrange("p (c n) -> p c n", c=7)
        for c in range(7):
            n = min(128, TS - 128 * c)
            m1 = op("tensor", "tr", lambda e, c=c, n=n: e.transpose(BK[c % 2][0:n, 0:128], loF[:, 128 * c:128 * c + n], ident[:, :]), r6, c_id,
                    tr[-2] if c >= 2 else None)
            m2 = op("tensor", "tr", lambda e, c=c, n=n: e.transpose(BK[c % 2][0:n, 128:256], srcF[:, 128 * c:128 * c + n], ident[:, :]), r3)
            v1 = op("vector", "v", lambda e, c=c, n=n: e.tensor_copy(stl[0:n, c, :], BK[c % 2][0:n, 0:128]), m1, m2)
            v2 = op("vector", "v", lambda e, c=c, n=n: e.tensor_copy(stu[0:n, c, :], BK[c % 2][0:n, 128:256]), m2)
            tr.append(v2)
        t_rows = []
        for st, dd in ((stl, loTd), (stu, srcTd)):
            t_rows.append(dma("sync", "rw", lambda e, st=st, dd=dd: e.dma_start(dd[0:768 * 128].rearrange("(c p n) -> p c n", p=128, n=128), st[:, 0:6, :]), tr[-1]))
            t_rows.append(dma("sync", "rw", lambda e, st=st, dd=dd: e.dma_start(dd[768 * 128:TS * 128].rearrange("(p n) -> p n", n=128), st[0:14, 6, :]), tr[-1]))

        f_ = carve(fw)
        W0 = f_(320)
        W0b = W0.bitcast(bf16)[:, 0:320]
        W1a = f_(192)
        W1s = f_(192)
        W1b = f_(320)
        W2t = f_(12)
        b01 = f_(6)
        b2r = f_(4)
        boS = f_(512, bf16)
        ini = [op("vector", "w", lambda e, t_=t_: e.memset(t_, 0.0)) for t_ in (W1a, W1s, W1b, W2t, b01, b2r)]
        wt = []

        def wload(dst_, src_):
            wt.append(dma("sync", "wt", lambda e: e.dma_start(dst_, src_, allow_slow_non_contiguous=True), ini))

        for pi_, (wT, bb) in enumerate(((waT, ba), (wsT, bs))):
            for k_, r_ in enumerate((0, 1, 35, 36)):
                wload(W0[k_:k_ + 1, 128 * pi_:128 * pi_ + 128], wT[0, r_:r_ + 1, 0:128])
                wload(W0[k_:k_ + 1, 256 + 32 * pi_:288 + 32 * pi_], wT[0, r_:r_ + 1, 128:160])
            W1 = (W1a, W1s)[pi_]
            wload(W1[:, 0:128], wT[1, 0:128, 0:128])
            wload(W1[:, 128 + 32 * pi_:160 + 32 * pi_], wT[1, 0:128, 128:160])
            wload(W1b[32 * pi_:32 * pi_ + 32, 128 * pi_:128 * pi_ + 128], wT[1, 128:160, 0:128])
            wload(W1b[32 * pi_:32 * pi_ + 32, 256 + 32 * pi_:288 + 32 * pi_], wT[1, 128:160, 128:160])
            wload(W2t[:, 4 * pi_ + 2 * pi_:4 * pi_ + 2 * pi_ + 2], wT[2, 0:128, 100:102])
            wload(W2t[32 * pi_:32 * pi_ + 32, 8 + 2 * pi_:10 + 2 * pi_], wT[2, 128:160, 100:102])
            for l in range(2):
                wload(b01[:, 3 * l + pi_:3 * l + pi_ + 1], bb[l, 0:128].rearrange("(p a) -> p a", a=1))
                wload(b01[32 * pi_:32 * pi_ + 32, 3 * l + 2:3 * l + 3], bb[l, 128:160].rearrange("(p a) -> p a", a=1))
            wload(b2r[:, 2 * pi_:2 * pi_ + 2], bb[2:3, 100:102].broadcast_to([128, 2]))

        a2 = carve(R1, 6144 + 4 + 512 + 768 + 6 * TS + 2 * 448)
        NR = 6
        AHEAD = 4
        Abf = [a2(8 * 128, bf16).rearrange("p (t n) -> p t n", n=128) for _ in range(NR)]
        Bbf = [a2(8 * W, bf16).rearrange("p (t n) -> p t n", n=W) for _ in range(NR)]
        AT = [a2(8 * 128).rearrange("p (t n) -> p t n", n=128) for _ in range(2)]
        Cs = [a2(W * 9).rearrange("p (n t) -> p n t", t=9) for _ in range(3)]
        keep9 = a2(W * 9).rearrange("p (n t) -> p n t", t=9)
        GB = a2(8 * W).rearrange("p (t n) -> p t n", n=W)
        rank = a2(2 * 8).rearrange("p (a t) -> p a t", a=2)
        psel = a2(2 * 8).rearrange("p (a t) -> p a t", a=2)
        sm = [a2(8) for _ in range(6)]
        ridx = small[:, 64:96].bitcast(i32).rearrange("p (a t) -> p a t", a=4)
        scr = [a2(128) for _ in range(2)]
        xin = [ar(512) for _ in range(3)]
        xT = [a2(512).rearrange("p (c n) -> p c n", c=4) for _ in range(2)]
        stg = [a2(512), a2(512), a2(YW)]
        stV = stg[2].rearrange("p (h d) -> p h d", d=65)
        rowsS = [ar(1024, u16) for _ in range(3)]
        rowsL = [rowR[:, 0, 0:1024], rowR[:, 0, 1024:2048], rowR[:, 1, 0:1024]]
        NCH = (TS + 7) // 8
        chn = [min(8, TS - 8 * c) for c in range(NCH)]

        def bcast_last(ap, n, m):
            return ap.rearrange("p (t a) -> p t a", a=1).broadcast_to([128, n, m])

        def build_AB(c, slot_wait, b_on_pool=False, a_on_act=False):
            n = chn[c]
            if a_on_act:
                for j in range(n):
                    ta = op("scalar", "aa", lambda e, j=j: e.activation(Abf[c % NR][:, j, :], iotaF[:, :], ACT.Abs, bias=nlo0[:, 8 * c + j:8 * c + j + 1]),
                            r8, c_iota, slot_wait)
                ta = op("scalar", "aa", lambda e: e.activation(Abf[c % NR][:, 0:n, :], Abf[c % NR][:, 0:n, :], ACT.Relu, bias=one1[:, 0:1], scale=-1.0), ta, c_one1)
            lo_c = rec[:, 8 * c:8 * c + n, 8:9].broadcast_to([128, n, 128])
            io = iotaF[:, :].rearrange("p (a n) -> p a n", a=1).broadcast_to([128, n, 128])
            if not a_on_act:
                ta = op("vector", "ab", lambda e: e.tensor_tensor(Abf[c % NR][:, 0:n, :], lo_c, io, ALU.is_equal), r6, c_iota, slot_wait)
            if b_on_pool:
                tb = None
                for j in range(n):
                    tb = op("gpsimd", "bp", lambda e, j=j: e.tensor_scalar(Bbf[c % NR][:, j, :], iotaF[:, 0:W], hiF[:, 8 * c + j:8 * c + j + 1], None, ALU.is_equal),
                            r5, c_iota, slot_wait)
                return [ta, tb]
            hi_c = bcast_last(hiF[:, 8 * c:8 * c + n], n, W)
            io2 = iotaF[:, 0:W].rearrange("p (a n) -> p a n", a=1).broadcast_to([128, n, W])
            tb = op("vector", "ab", lambda e: e.tensor_tensor(Bbf[c % NR][:, 0:n, :], hi_c, io2, ALU.is_equal), r5, slot_wait)
            return [ta, tb]

        st6 = small[:, 0:12].rearrange("p (a n) -> p a n", a=2)
        mv = small[:, 12:16].rearrange("p (a n) -> p a n", a=2)
        rs = small[:, 16:20].rearrange("p (a n) -> p a n", a=2)
        xl, xTt, pj, stv, lnd = {}, {}, {}, {}, {}
        stored = {}
        OUTS = (Qd, Kd, Vd)

        def load_x(w):
            n = rows_of[w]
            xl[w] = dma("sync", f"x{w % 3}", lambda e: e.dma_start(xin[w % 3][0:n, :], x[128 * w:128 * w + n, :]), xTt.get((w - 3, "T")), r1)

        def ln_stats(w):
            n, xt, k = rows_of[w], xin[w % 3], w % 2
            b1 = op("vector", "ln", lambda e: e.bn_stats(st6[0:n, k, :], xt[0:n, :]), xl[w])
            b2 = op("vector", "ln", lambda e: e.bn_aggr(mv[0:n, k, :], st6[0:n, k, :]), b1)
            b3 = op("vector", "ln", lambda e: e.tensor_scalar(rs[0:n, k, 0:1], mv[0:n, k, 1:2], 1e-5, None, ALU.add), b2)
            lnd[(w, "s")] = op("scalar", "lna", lambda e: e.activation(rs[0:n, k, 1:2], rs[0:n, k, 0:1], ACT.Sqrt), b3)

        def ln_out(w):
            n, xt, k = rows_of[w], xin[w % 3], w % 2
            b5 = op("vector", "ln", lambda e: e.reciprocal(rs[0:n, k, 0:1], rs[0:n, k, 1:2]), lnd[(w, "s")])
            lnd[w] = op("vector", "ln", lambda e: e.tensor_scalar(xt[0:n, :], xt[0:n, :], mv[0:n, k, 0:1], rs[0:n, k, 0:1],
                        ALU.subtract, ALU.mult), b5)

        def proj_T(w):
            n, xt = rows_of[w], xin[w % 3]
            for c in range(4):
                last = op("tensor", "pt", lambda e, c=c: e.transpose(BK[3][:, 128 * c:128 * c + n], xt[0:n, 128 * c:128 * c + 128],
                          ident[0:n, 0:n]), lnd[w], xTt.get(w - 1))
            xTt[(w, "T")] = last
            xTt[w] = op("scalar", "px", lambda e: e.copy(xT[w % 2][:, :, 0:n], BK[3][:, :].rearrange("p (c n) -> p c n", c=4)[:, :, 0:n]),
                        last, pj.get((w - 2, 2)))

        def proj_M(w, m):
            n = rows_of[w]
            i = 3 * w + m
            bank = BK[4 + i % 3]
            for c in range(4):
                op("tensor", "pj", lambda e, c=c: e.matmul(bank[0:n, :], xT[w % 2][:, c, 0:n], W3[m][:, c, :], start=(c == 0), stop=False),
                   xTt[w], wl[m], stv.get(i - 3))
            pj[(w, m)] = op("tensor", "pj", lambda e: e.matmul(bank[0:n, :], ones[0:3, 0:n], Bs[0:3, 512 * m:512 * m + 512], start=False, stop=True),
                            c_ones, c_b3)
            to, of = stg[m][0:n, :], bank[0:n, :]
            if m == 2:
                to, of = stV[0:n, :, 0:64], of.rearrange("p (h d) -> p h d", d=64)
            stv[i] = op("scalar", "ps", lambda e: e.activation(to, of, ACT.Copy, scale=0.125 if m == 0 else 1.0),
                        pj[(w, m)], stored.get(i - 3))
            stored[i] = dma("sync", f"st{i % 3}", lambda e: e.dma_start(OUTS[m][128 * w:128 * w + n, :], stg[m][0:n, :]), stv[i], c_stV)

        proj = []
        for w in range(W):
            proj += [lambda w=w: (ln_stats(w + 1) if w + 1 < W else None, proj_T(w), load_x(w + 3) if w + 3 < W else None),
                     lambda w=w: (proj_M(w, 0), ln_out(w + 1) if w + 1 < W else None), lambda w=w: proj_M(w, 1), lambda w=w: proj_M(w, 2)]
        at_unit = [0]

        def next_unit():
            if at_unit[0] < len(proj):
                proj[at_unit[0]]()
                at_unit[0] += 1

        c_stV = op("vector", "cv", lambda e: e.memset(stV[:, :, 64:65], 1.0))
        hist = []
        tab = {}
        for c in range(NCH + AHEAD):
            if c == 9:
                r1 = op("scalar", "a", lambda e: e.copy(rec[:, :, 0:8], at8.rearrange("p (t h) -> p t h", h=8)), la)
            if c == 10:
                for w in range(3):
                    load_x(w)
                bl3 = load_bias("b3", (bq, bk, bv), Bf[0], r1)
                bl4 = load_bias("b4", (bo,), Bf[1], r1)
            if c == 20:
                ln_stats(0)
                ln_out(0)
                c_b3 = split_bias("b3", (bq, bk, bv), Bf[0], Br[0], Bt[0], Bs, bl3)
                c_bo = split_bias("b4", (bo,), Bf[1], Br[1], Bt[1], boS, bl4)
            if c < NCH:
                tab[c] = build_AB(c, hist[c - NR] if c >= NR else None, c % 3 == 1, c % 3 == 2)
            k_ = c - AHEAD
            if k_ >= 0:
                for j in range(chn[k_]):
                    last = op("tensor", "hi", lambda e, k_=k_, j=j: e.matmul(BK[0][:, 0:W], Abf[k_ % NR][:, j, :], Bbf[k_ % NR][:, j, :],
                              start=(k_ == 0 and j == 0), stop=(k_ == NCH - 1 and j == chn[k_] - 1)), tab[k_], tr[-1])
                hist.append(last)
                if k_ >= 17 and k_ % 4 == 2:
                    next_unit()
        sHt = a2(W)
        sC = a2(W)
        sTi = a2(W).bitcast(i32)
        sTf = a2(W)
        sInc = a2(W)
        z0 = a2(W)
        q1 = op("vector", "v", lambda e: e.tensor_copy(sHt, BK[0][:, 0:W]), hist[-1])
        q0 = op("vector", "v", lambda e: e.memset(z0, 0.0))
        m1 = op("tensor", "hb", lambda e: e.matmul(BK[1][:, 0:W], upp, sHt, start=True, stop=True), q1, c_upp)
        m2 = op("tensor", "hb", lambda e: e.matmul(BK[1][:, 64:64 + W], onesf, sHt, start=True, stop=True), q1, c_onesf)
        q2 = op("vector", "v", lambda e: e.tensor_scalar(sC, BK[1][:, 64:64 + W], 127.0, None, ALU.add), m2)
        q3 = op("vector", "v", lambda e: e.tensor_copy(sTi, sC), q2)
        q4 = op("vector", "v", lambda e: e.tensor_scalar(sTi, sTi, 7, None, ALU.logical_shift_right), q3)
        q5 = op("vector", "v", lambda e: e.tensor_copy(sTf, sTi), q4)
        q6 = op("vector", "v", lambda e: e.tensor_tensor_scan(sInc, z0, sTf, 0.0, ALU.add, ALU.add), q5, q0)
        q7 = op("vector", "v", lambda e: e.tensor_tensor(sC, sInc, sTf, ALU.subtract), q6)
        t_base = op("vector", "v", lambda e: e.scalar_tensor_tensor(Cs[2][:, :, 8], sC, 128.0, BK[1][:, 0:W], ALU.mult, ALU.add), q7, m1)
        k9 = op("vector", "v", lambda e: e.memset(keep9, 1.0))
        k9 = op("vector", "v", lambda e: e.memset(keep9[:, :, 0:1], 0.0), k9)
        wI = a2(7).bitcast(i32)
        wF = a2(7)
        wC = a2(7 * W).rearrange("p (c n) -> p c n", n=W)
        g1 = op("gpsimd", "g", lambda e: e.iota(wI, pattern=[[128, 7]], base=0, channel_multiplier=1))
        q8 = op("vector", "v", lambda e: e.tensor_copy(wF, wI), g1)
        q9 = op("vector", "v", lambda e: e.tensor_tensor(wC, sInc.rearrange("p (a n) -> p a n", a=1).broadcast_to([128, 7, W]),
                bcast_last(wF, 7, W), ALU.is_le), q8, q6)
        q10 = op("vector", "v", lambda e: e.tensor_reduce(wF, wC, AX.X, ALU.add), q9)
        q11 = op("vector", "v", lambda e: e.tensor_scalar(wI, wF, 48.0, None, ALU.min), q10)
        t_wd = dma("sync", "wid", lambda e: e.dma_start(widd.rearrange("(c p) -> p c", p=128), wI, allow_slow_non_contiguous=True), q11)
        t_wid = dma("sync", "wid", lambda e: e.dma_start(widr[:, :], widd[0:T].rearrange("(a t) -> a t", a=1)), t_wd)

        rowt, gsum, rk, scat, ATt, Gt, Ht, Cst = {}, {}, {}, {}, {}, {}, {}, {}
        abt = {}
        HB = (0, 7)

        def s_rows(c):
            n = chn[c]
            rowt[c] = [dma("sync", f"rl{c % 3}", lambda e: e.dma_start(rowsL[c % 3][:, 0:128 * n], loTd[1024 * c:1024 * c + 128 * n]
                           .rearrange("(a n) -> a n", a=1).broadcast_to([128, 128 * n])), t_rows, ATt.get(c - 3)),
                       dma("sync", f"rs{c % 3}", lambda e: e.dma_start(rowsS[c % 3][:, 0:128 * n], srcTd[1024 * c:1024 * c + 128 * n]
                           .rearrange("(a n) -> a n", a=1).broadcast_to([128, 128 * n])), t_rows, rk.get(c - 3), r1)]

        def s_ab(c):
            n = chn[c]
            abt[c] = build_AB(c, [Ht.get(c - NR), hist[-1], gsum.get(c - NR)])
            for j in range(n):
                last = op("tensor", "sh", lambda e, j=j: e.matmul(BK[HB[c % 2]][:, 0:W * 9].rearrange("p (n t) -> p n t", t=9)[:, :, j + 1],
                          Abf[c % NR][:, j, :], Bbf[c % NR][:, j, :], start=True, stop=True), abt[c], q1, Cst.get(c - 2))
            Ht[c] = last

        def s_at(c):
            n = chn[c]
            v = op("scalar", "at", lambda e: e.activation(AT[c % 2][:, 0:n, :], rowsL[c % 3][:, 0:128 * n].rearrange("p (t n) -> p t n", n=128),
                   ACT.Abs, bias=npidx[:, 0:1]), rowt[c][0], Gt.get(c - 2), c_np)
            ATt[c] = op("scalar", "at", lambda e: e.activation(AT[c % 2][:, 0:n, :], AT[c % 2][:, 0:n, :], ACT.Relu, bias=one1[:, 0:1], scale=-1.0), v, c_one1)

        def s_scan(c):
            n = chn[c]
            bank = BK[HB[c % 2]][:, 0:W * 9]
            v = op("vector", "cs", lambda e: e.tensor_copy(bank.rearrange("p (n t) -> p n t", t=9)[:, :, 0], Cs[(c - 1) % 3][:, :, 8]),
                   Ht[c], Cst.get(c - 1), t_base)
            if n < 8:
                v = op("vector", "cs", lambda e: e.memset(bank.rearrange("p (n t) -> p n t", t=9)[:, :, n + 1:9], 0.0), v)
            Cst[c] = op("vector", "cs", lambda e: e.tensor_tensor_scan(Cs[c % 3].rearrange("p n t -> p (n t)"), keep9.rearrange("p n t -> p (n t)"), bank, 0.0,
                        ALU.mult, ALU.add), v, k9, Gt.get(c - 3))

        def s_g(c):
            for j in range(chn[c]):
                Gt[c] = op("tensor", "sg", lambda e, j=j: e.matmul(BK[1 + c % 2][:, j * W:(j + 1) * W], AT[c % 2][:, j, :], Cs[c % 3][:, :, j], start=True, stop=True),
                           ATt[c], Cst[c], gsum.get(c - 2), q11)

        scr_free = [None, None]

        def s_rank(c, j):
            t = 8 * c + j
            rk[c] = scr_free[j % 2] = op("vector", "rk", lambda e: e.scalar_tensor_tensor(scr[j % 2], rowsS[c % 3][:, 128 * j:128 * j + 128], srcF[:, t:t + 1], low,
                       ALU.is_equal, ALU.mult, accum_out=rank[:, c % 2, j:j + 1]), rowt[c][1], c_low, gsum.get((c - 2, "u")), scr_free[j % 2])

        def s_place(c):
            n, k = chn[c], c % 2
            pf, pi, af, bf_, av = sm[0][:, 0:n], sm[1].bitcast(i32)[:, 0:n], sm[2][:, 0:n], sm[3][:, 0:n], sm[4][:, 0:n]

            def step(fn, *w):
                def f():
                    gsum[(c, "z")] = op("vector", "sv", fn, gsum.get((c, "z")), *w)
                return f

            def gb():
                gsum[(c, "z")] = op("vector", "sv", lambda e: e.tensor_tensor(GB[:, 0:n, :], BK[1 + k][:, 0:n * W].rearrange("p (t n) -> p t n", n=W),
                                    Bbf[c % NR][:, 0:n, :], ALU.mult), Gt[c], gsum.get(c - 1))

            def red():
                gsum[c] = gsum[(c, "z")] = op("vector", "sv", lambda e: e.tensor_reduce(psel[:, k, 0:n], GB[:, 0:n, :], AX.X, ALU.add), gsum[(c, "z")])

            def u1():
                gsum[(c, "u")] = gsum[(c, "z")] = op("vector", "sv", lambda e: e.tensor_tensor(pf, psel[:, k, 0:n], rank[:, k, 0:n], ALU.add), gsum[c], rk[c])

            def fin():
                u7 = gsum["fin"] = op("vector", "sv", lambda e: e.scalar_tensor_tensor(ridx[:, c % 4, 0:n], bf_, float(T), av, ALU.mult, ALU.add), gsum[(c, "z")], scat.get(c - 4))
                for j in range(n):
                    t = 8 * c + j
                    scat[c] = dma("gpsimd", f"sc{c % 4}", lambda e, t=t, j=j: e.indirect_dma_start(
                        recd, bass.IndirectOffsetOnAxis(ap=ridx[:, c % 4, j:j + 1], axis=0), rec[:, t, :], None,
                        bounds_check=128 * T - 1, oob_is_err=False), u7, r1, r2, r6, t_def)
            return [gb, red, u1, step(lambda e: e.tensor_copy(pi, pf)),
                    step(lambda e: e.tensor_scalar(pi, pi, 7, None, ALU.logical_shift_right)),
                    step(lambda e: e.tensor_copy(af, pi)),
                    step(lambda e: e.scalar_tensor_tensor(bf_, af, -128.0, pf, ALU.mult, ALU.add)),
                    step(lambda e: e.tensor_tensor(av, af, inv[:, 8 * c:8 * c + n], ALU.add), r7), fin]

        s_rows(0)
        s_rows(1)
        s_ab(0)
        s_at(0)
        s_ab(1)
        for j in range(chn[0]):
            s_rank(0, j)
        s_scan(0)
        s_g(0)
        for c in range(NCH):
            if c + 2 < NCH:
                s_rows(c + 2)
                s_ab(c + 2)
            if c + 1 < NCH:
                s_at(c + 1)
                s_scan(c + 1)
            next_unit()
            if c + 1 < NCH:
                s_g(c + 1)
            steps = s_place(c)
            for j in range(max(len(steps), 8)):
                if j < len(steps):
                    steps[j]()
                if c + 1 < NCH and j < chn[c + 1]:
                    s_rank(c + 1, j)
            if c % 8 < 7:
                next_unit()
        while at_unit[0] < len(proj):
            next_unit()
        scat_all = [scat[c] for c in range(NCH - 4, NCH)]
        proj_all = [stored[i] for i in range(3 * W - 3, 3 * W)]
        phaseA = [pj[(W - 1, 2)], stv[3 * W - 1], gsum[NCH - 1], rk[NCH - 1], gsum["fin"]]

        Qall = R1[:, 0:W * 512].rearrange("p (w n) -> p w n", n=512)
        t_rec = dma("sync", "rec", lambda e: e.dma_start(R2[:, :], recd.rearrange("(p t) r -> p (t r)", p=128)), scat_all, phaseA)
        z3 = op("vector", "v", lambda e: e.memset(Qall[:, W - 1, :], 0.0), phaseA, proj_all)
        t_q = []

        def load_q(w0, w1, *wait):
            t_q.append(dma("scalar", "q", lambda e: e.dma_start(Qall[:, w0:w1, :], Qd[w0 * 128:w1 * 128, :].rearrange("(w p) n -> p w n", p=128)),
                           phaseA, proj_all, *wait))

        for w0 in range(0, 32, 8):
            load_q(w0, w0 + 8)
        L = R3[:, 0:T * 8].rearrange("p (b h t) -> p b h t", h=8, t=16)
        recS = R2[:, :].rearrange("p (b t r) -> p b t r", t=16, r=REC)
        cw = carve(small, 1792)
        Wp = [cw(320, bf16) for _ in range(3)]
        Wr = cw(320)
        sel = [cw(36, bf16).rearrange("p (i j f) -> p i j f", i=3, j=3) for _ in range(3)]
        u = op("vector", "wb", lambda e: e.tensor_copy(Wp[0][0:4, :], W0[0:4, :]), wt, phaseA)
        u = op("vector", "wb", lambda e: e.tensor_tensor(Wr[0:4, :], W0[0:4, :], Wp[0][0:4, :], ALU.subtract), u)
        u = op("vector", "wb", lambda e: e.tensor_copy(Wp[1][0:4, :], Wr[0:4, :]), u)
        u = op("vector", "wb", lambda e: e.tensor_tensor(Wp[2][0:4, :], Wr[0:4, :], Wp[1][0:4, :], ALU.subtract), u)
        for i in range(3):
            z = op("vector", "wb", lambda e, i=i: e.memset(sel[i][0:4, :, :, :], 0.0))
            z = op("vector", "wb", lambda e, i=i: e.tensor_copy(sel[i][0:4, i, :, :], ident[0:4, 0:4].rearrange("p (a f) -> p a f", a=1).broadcast_to([4, 3, 4])), z)
            m = op("tensor", "wm", lambda e, i=i: e.matmul(BK[7][0:36, 0:320], sel[i][0:4, :, :, :].rearrange("p i j f -> p (i j f)"), Wp[i][0:4, :],
                   start=(i == 0), stop=(i == 2)), z, u, phaseA)
        w0b = op("vector", "wb", lambda e: e.tensor_copy(W0b[0:36, :], BK[7][0:36, 0:320]), m)
        s1 = op("vector", "v", lambda e: e.tensor_copy(loS[:, :], R2[:, :].rearrange("p (t r) -> p t r", r=REC)[:, :, 8]), t_rec)
        s2 = op("vector", "v", lambda e: e.tensor_copy(dstS[:, :], R2[:, :].rearrange("p (t r) -> p t r", r=REC)[:, :, 9].bitcast(i32)))
        s3 = op("scalar", "a", lambda e: e.copy(L.rearrange("p b h t -> p b t h"), recS[:, :, :, 0:8]), t_rec, scat_all)
        s4 = op("vector", "v", lambda e: e.memset(Mall[:, :, :], -BIG))
        loT = R3[:, T * 8:T * 8 + 896].rearrange("p (c n) -> p c n", n=128)
        loTb = small[:, 0:448].bitcast(bf16).rearrange("p (c n) -> p c n", n=128)
        sfb = small[:, 448:896].bitcast(bf16).rearrange("p (c n) -> p c n", n=128)
        ens = small[:, 896:1792].rearrange("p (c n) -> p c n", n=128)
        te, tm, tv = [], [], []
        tn = [min(128, T - 128 * c) for c in range(7)]
        for c, n in enumerate(tn):
            tm.append(op("tensor", "u", lambda e, c=c, n=n: e.transpose(BK[c][0:n, 0:128], loS[:, 128 * c:128 * c + n], ident[:, :]), s1, phaseA))
        for c, n in enumerate(tn):
            en = ens[:, c, :]
            v1 = op("vector", "u2", lambda e, c=c, n=n: e.tensor_copy(loT[0:n, c, :], BK[c][0:n, 0:128]), tm[c], scat_all)
            v2 = op("vector", "u2", lambda e, c=c, n=n: e.tensor_copy(loTb[0:n, c, :], loT[0:n, c, :]), v1)
            v3 = op("vector", "u2", lambda e, c=c, n=n: e.tensor_tensor(sfb[0:n, c, 1:128], loT[0:n, c, 1:128], loT[0:n, c, 0:127], ALU.is_equal), v1)
            v4 = op("vector", "u2", lambda e, c=c, n=n: e.memset(sfb[0:n, c, 0:1], 0.0))
            v5 = op("vector", "u2", lambda e, c=c, n=n, en=en: e.tensor_scalar(en[0:n, 0:127], sfb[0:n, c, 1:128], -1.0, 1.0, ALU.mult, ALU.add), v3)
            v6 = op("vector", "u2", lambda e, c=c, n=n, en=en: e.memset(en[0:n, 127:128], 1.0))
            v9 = op("vector", "u2", lambda e, c=c, n=n: e.tensor_scalar(sfb[0:n, c, :], sfb[0:n, c, :], -1.0, BIG, ALU.add, ALU.mult), v5, v4)
            m2 = op("tensor", "u", lambda e, c=c, n=n, en=en: e.transpose(BK[c][:, 128:128 + n], en[0:n, :], ident[0:n, 0:n]), v5, v6)
            tv.append((m2, v9))
        for c, n in enumerate(tn):
            te.append(op("vector", "u2", lambda e, c=c, n=n: e.tensor_copy(endP[:, 128 * c:128 * c + n], BK[c][:, 128:128 + n]), tv[c][0]))
        t_ss = []
        for st, dd in ((loTb, loSd), (sfb, sfd)):
            t_ss.append(dma("sync", "rx", lambda e, st=st, dd=dd: e.dma_start(dd[0:768 * 128].rearrange("(c p n) -> p c n", p=128, n=128), st[:, 0:6, :]), tv[-1][1]))
            t_ss.append(dma("sync", "rx", lambda e, st=st, dd=dd: e.dma_start(dd[768 * 128:T * 128].rearrange("(p n) -> p n", n=128), st[0:64, 6, :]), tv[-1][1]))

        load_q(32, 40, t_rec)
        load_q(40, W - 1, t_rec)
        t_q.append(dma("scalar", "q", lambda e: e.dma_start(Qall[0:106, W - 1, :], Qd[(W - 1) * 128:N, :]), z3, phaseA, proj_all))

        b = carve(R2)
        KR = 8
        PR = 4
        HA = 5
        Kr = [b(512) for _ in range(KR)]
        prod = [b(512) for _ in range(PR)]
        ohT = [b(8 * 128).rearrange("p (t n) -> p t n", n=128) for _ in range(2)]
        c3 = carve(small)
        ohb = [c3(8 * 128, bf16).rearrange("p (t n) -> p t n", n=128) for _ in range(5)]
        sfr = [c3(128, bf16) for _ in range(2)]
        FeP = [[c3(9 * 16, bf16).rearrange("p (h t) -> p h t", h=9) for _ in range(3)] for _ in range(2)]
        pen = [c3(16) for _ in range(2)]
        c5 = carve(R3, T * 8)
        Lr = [c5(128).rearrange("p (h t) -> p h t", h=8) for _ in range(2)]
        Fs = [c5(128) for _ in range(2)]
        Fm = [c5(9 * 16).rearrange("p (h t) -> p h t", h=9) for _ in range(2)]
        rt, oht, kt, qt, prt, redt, sft, lb = {}, {}, {}, {}, {}, {}, {}, {}
        clr = [s1, s2, s3, w0b]
        QB = (0, 1, 2)
        TB = (6, 7)

        def regs(eng_name, tag):
            return {"r": None, "tag": tag, "eng": eng_name}

        def load_regs(st, b_):
            def f(e):
                if st["r"] is None:
                    st["r"] = [e.alloc_register(f"{st['tag']}{j}") for j in range(16)]
                return e.reg_load(st["r"], widr[0:1, 16 * b_:16 * b_ + 16])
            P.plain(st["eng"], f, t_wid)

        def win(e, st, t):
            return e.snap(st["r"][t % 16], min_val=0, max_val=W - 1)

        def in_slots(jobs):
            for _, _, f in sorted(((s_, n_, f) for n_, (s_, f) in enumerate(jobs)), key=lambda z: z[:2]):
                f()

        def rows2(b_, store, tag, wait):
            store[b_] = dma("sync", f"{tag}{b_ % 2}", lambda e: e.dma_start(rowR[:, b_ % 2, :], loSd[2048 * b_:2048 * b_ + 2048]
                            .rearrange("(a n) -> a n", a=1).broadcast_to([128, 2048])), wait)

        def one_hot_T(h_, rtok, store, free):
            b_ = h_ // 2
            o = ohT[h_ % 2]
            v = op("scalar", "oh", lambda e: e.activation(o, rowR[:, b_ % 2, 1024 * (h_ % 2):1024 * (h_ % 2) + 1024].rearrange("p (t n) -> p t n", n=128),
                   ACT.Abs, bias=npidx[:, 0:1]), rtok[b_], free)
            store[(h_, "abs")] = v

        def one_hot_T2(h_, store):
            o = ohT[h_ % 2]
            store[h_] = op("scalar", "oh", lambda e: e.activation(o, o, ACT.Relu, bias=one1[:, 0:1], scale=-1.0), store[(h_, "abs")])

        def turn(h_, q, stream, dst_, need, store, free):
            i_ = (2 * h_ + q) % 2
            bank = BK[TB[i_]]
            for j in range(4):
                m = op("tensor", stream, lambda e, j=j: e.transpose(bank[:, 128 * j:128 * j + 128], ohT[h_ % 2][:, 4 * q + j, :], ident[:, :]),
                       need[h_], tfree[i_])
            store[(h_, "m")] = m
            store[h_] = tfree[i_] = op("scalar", stream + "e", lambda e: e.copy(dst_[:, 4 * q:4 * q + 4, :], bank.rearrange("p (t n) -> p t n", n=128)), m, free)

        tfree = [None, None]

        def gather_k(t):
            kt[t] = dma("gpsimd", f"k{t % KR}", lambda e: e.indirect_dma_start(Kr[t % KR], None, Kd, bass.IndirectOffsetOnAxis(ap=dstS[:, t:t + 1], axis=0),
                        bounds_check=N - 1, oob_is_err=False), prt.get(t - KR), clr, proj_all, phaseA)

        pe1 = regs("tensor", "pw")
        dv1 = regs("vector", "dw")

        def p1_q(t):
            if t % 16 == 0:
                load_regs(pe1, t // 16)
            qt[t] = op("tensor", "q1", lambda e: e.matmul(BK[QB[t % 3]], ohT[(t // 8) % 2][:, t % 8, :], Qall[:, bass.ds(win(e, pe1, t), 1), :],
                       start=True, stop=True), oht[t // 8], prt.get(t - 3), t_q, te[-1])

        def p1_pr(t):
            prt[t] = op("vector", "pr", lambda e: e.tensor_tensor(prod[t % PR], BK[QB[t % 3]], Kr[t % KR], ALU.mult), qt[t], kt[t], redt.get(t - PR))

        def p1_rd(t):
            b_, k = t // 16, t // 16 % 2
            r = [op("vector", "rd", lambda e: e.tensor_reduce(Lr[k][:, 0:HA, t % 16], prod[t % PR][:, 0:64 * HA].rearrange("p (h d) -> p h d", d=64), AX.X, ALU.add),
                    prt[t], lb.get(b_ - 2), t_ss)]
            for h in range(HA, 8):
                r.append(op("scalar", "ra", lambda e, h=h: e.activation(prod[t % PR][:, 64 * h:64 * h + 64], prod[t % PR][:, 64 * h:64 * h + 64], ACT.Copy,
                            accum_out=Lr[k][:, h, t % 16:t % 16 + 1]), prt[t], lb.get(b_ - 2), t_ss))
            redt[t] = [r[0], r[-1]]

        fet, eot, mt, mu, pent = {}, {}, {}, {}, {}

        def p1_lb(b_):
            lb[b_] = op("vector", "lb", lambda e: e.tensor_tensor(L[:, b_, :, :], L[:, b_, :, :], Lr[b_ % 2], ALU.add), redt[16 * b_ + 15], s3)

        def p1_sf(b_):
            sft[b_] = dma("sync", f"sf{b_ % 2}", lambda e: e.dma_start(sfr[b_ % 2], sfd[2048 * b_:2048 * b_ + 2048].rearrange("(a t n) -> a t n", a=1, n=128)
                          .broadcast_to([8, 16, 128])), t_ss, fet.get((b_ - 2, "s")))

        def p1_t1(b_):
            fet[(b_, "t")] = op("tensor", "lt", lambda e: e.transpose(BK[3][:, 0:128], L[:, b_, :, :].rearrange("p h t -> p (h t)"), ident[:, :]), lb[b_],
                                fet.get(b_ - 1))

        def p1_scan(b_):
            fet[(b_, "s")] = op("vector", "sc", lambda e: e.tensor_tensor_scan(Fs[b_ % 2], sfr[b_ % 2], BK[3][:, 0:128], -BIG, ALU.add, ALU.max),
                                fet[(b_, "t")], sft[b_], fet.get((b_ - 2, "p")))

        def p1_t2(b_):
            k = b_ % 2
            m2 = fet[(b_, "p")] = op("tensor", "lt", lambda e: e.transpose(BK[3][:, 128:256], Fs[k], ident[:, :]), fet[(b_, "s")])

        def p1_fm(b_):
            k = b_ % 2
            ev = endP[:, 16 * b_:16 * b_ + 16].rearrange("p (a t) -> p a t", a=1)
            fr = fet.get((b_ - 2, "lo"))
            fet[(b_, "m8")] = op("vector", "fm1", lambda e: e.tensor_copy(Fm[k][:, 8:9, :], ev), fr, te[-1], t_ss)
            fet[b_] = fet[(b_, "m")] = op("vector", "fm1", lambda e: e.tensor_tensor(Fm[k][:, 0:8, :], BK[3][:, 128:256].rearrange("p (h t) -> p h t", h=8),
                                          ev.broadcast_to([128, 8, 16]), ALU.mult), fet[(b_, "p")])
            fet[(b_, "hi")] = op("scalar", "fe", lambda e: e.copy(FeP[k][0], Fm[k]), fet[b_], mt.get(16 * (b_ - 2) + 15), t_ss)

        def p1_f2(b_):
            k = b_ % 2
            fet[(b_, "r")] = op("vector", "fm1", lambda e: e.tensor_tensor(Fm[k], Fm[k], FeP[k][0], ALU.subtract), fet[(b_, "hi")])
            fet[(b_, "mid")] = op("scalar", "fe", lambda e: e.copy(FeP[k][1], Fm[k]), fet[(b_, "r")])

        def p1_f3(b_):
            k = b_ % 2
            fet[(b_, "lo")] = op("vector", "fm1", lambda e: e.tensor_tensor(FeP[k][2], Fm[k], FeP[k][1], ALU.subtract), fet[(b_, "mid")])

        def p1_mt(t):
            b_, k, j = t // 16, t // 16 % 2, t % 16
            for i in range(3):
                mt[t] = op("tensor", "mt", lambda e, i=i: e.matmul(BK[4 + k][:, 16 * j:16 * j + 9], ohb[(t // 8) % 5][:, t % 8, :], FeP[k][i][:, :, j],
                           start=(i == 0), stop=(i == 2)), eot[t // 8], fet[(b_, "lo")], fet[(b_, "mid")], mu.get(16 * (b_ - 2) + 15))

        def p1_pen(b_):
            k = b_ % 2
            load_regs(dv1, b_)
            pent[b_] = op("vector", "mu", lambda e: e.tensor_scalar(pen[k], BK[4 + k][:, 0:256].rearrange("p (t n) -> p t n", n=16)[:, :, 8], -1.0, BIG,
                          ALU.add, ALU.mult), mt[16 * b_ + 15], mu.get(16 * b_ - 17))

        def p1_mu(t):
            b_, k, j = t // 16, t // 16 % 2, t % 16

            def f(e):
                mw = Mall[:, bass.ds(win(e, dv1, t), 1), :].rearrange("p a n -> p (a n)")
                return e.scalar_tensor_tensor(mw, BK[4 + k][:, 16 * j:16 * j + 8], pen[k][:, j:j + 1], mw, ALU.add, ALU.max)
            mu[t] = op("vector", "mu", f, pent[b_], mu.get(t - 1), s4)

        rows2(0, rt, "r", [t_ss, ATt[NCH - 1]])
        rows2(1, rt, "r", [t_ss, ATt[NCH - 1]])
        for h_ in range(2):
            one_hot_T(h_, rt, oht, [clr, c_np])
            one_hot_T2(h_, oht)
        for t in range(KR):
            gather_k(t)
        b7 = carve(R2)
        Vr = [b7(YW) for _ in range(KR)]
        PV = 6
        pv = [b7(YW) for _ in range(PV)]
        ohTb = [b7(8 * 128, bf16).rearrange("p (t n) -> p t n", n=128) for _ in range(2)]
        vt, pvt = {}, {}

        def gather_v(t):
            vt[t] = dma("gpsimd", f"k{t % KR}", lambda e: e.indirect_dma_start(Vr[t % KR], None, Vd, bass.IndirectOffsetOnAxis(ap=dstS[:, t:t + 1], axis=0),
                        bounds_check=N - 1, oob_is_err=False), [prt[T - 1], redt[T - 1], redt[T - 2], redt[T - 3], redt[T - 4]] if t < KR else pvt[t - KR])

        jobs = []
        job = lambda s_, f: jobs.append((s_, f))
        for b_ in range(NB):
            s_ = 16 * b_
            if b_ >= 2:
                job(s_ - 16 - 6.5, lambda b_=b_: rows2(b_, rt, "r", [t_ss, oht[2 * b_ - 3]]))
            job(s_ + 2, lambda b_=b_: p1_sf(b_))
            job(s_ + 18.6, lambda b_=b_: p1_lb(b_))
            job(s_ + 20.6, lambda b_=b_: p1_t1(b_))
            job(s_ + 22.6, lambda b_=b_: p1_scan(b_))
            job(s_ + 24.6, lambda b_=b_: p1_t2(b_))
            job(s_ + 26.6, lambda b_=b_: p1_fm(b_))
            job(s_ + 27.6, lambda b_=b_: p1_f2(b_))
            job(s_ + 28.6, lambda b_=b_: p1_f3(b_))
            for j in range(16):
                job(s_ + 29.7 + j * 0.9, lambda t=16 * b_ + j: p1_mt(t))
            job(s_ + 45.2, lambda b_=b_: p1_pen(b_))
            for j in range(16):
                job(s_ + 46.4 + 0.5 * j - (0.2 if j % 2 else 0), lambda t=16 * b_ + j: p1_mu(t))
        for h_ in range(2, 2 * NB):
            job(8 * h_ - 4.4, lambda h_=h_: one_hot_T(h_, rt, oht, [qt[8 * h_ - 9], eot[(h_ - 2, "m")]]))
            job(8 * h_ - 3.4, lambda h_=h_: one_hot_T2(h_, oht))
        for h_ in range(2 * NB):
            for q in range(2):
                job(8 * h_ + 0.3 + 2 * q, lambda h_=h_, q=q: turn(h_, q, "tu", ohb[h_ % 5], oht, eot, [mt.get(8 * (h_ - 5) + 7), t_ss]))
        for t in range(T):
            job(t, lambda t=t: p1_q(t))
            job(t + 1.3, lambda t=t: p1_pr(t))
            job(t + 2.5, lambda t=t: p1_rd(t))
            if t + KR < T:
                job(t + 1.35, lambda t=t: gather_k(t + KR))
        HW_ = 15000
        y0_ = []

        def clear_some(i):
            a_, b_ = i * HW_ // 6, (i + 1) * HW_ // 6
            zz = iotaF[:, 0:125].rearrange("p (a n) -> p a n", a=1).broadcast_to([128, (b_ - a_) // 125, 125])
            y0_.append(op("scalar", "z", lambda e: e.activation(R1[:, a_:b_].rearrange("p (a n) -> p a n", n=125), zz, ACT.Copy, scale=0.0), qt[T - 1]))

        for i in range(6):
            job(T + (4.5 if i < 3 else 30), lambda i=i: clear_some(i))
        for t in range(KR):
            job(T + 4.6, lambda t=t: gather_v(t))
        job(T + 4.7, lambda: y0_.append(op("gpsimd", "g", lambda e: e.memset(R1[:, HW_:W * YW], 0.0), qt[T - 1])))
        in_slots(jobs)
        y0 = y0_
        mx_all = mu[T - 1]
        pass1 = [mu[T - 1], qt[T - 1], redt[T - 1], lb[NB - 1], mt[T - 1]]

        Yall = R1[:, :].rearrange("p (w n) -> p w n", n=YW)
        YB = [PS[:, 0:1024], PS[:, 1024:2048], PS[:, 2048:3072]]
        HA2 = 5
        c6 = carve(small)
        oh = [c6(8 * 128).rearrange("p (t n) -> p t n", n=128) for _ in range(2)]
        Mb = [c6(W * 8, bf16).rearrange("p (w n) -> p w n", n=8) for _ in range(3)]
        Mr = c6(W * 8).rearrange("p (w n) -> p w n", n=8)
        identb = c6(128, bf16)
        rt2, oht2, mgt, pt, yt, ya, oh2, lst = {}, {}, {}, {}, {}, {}, {}, {}

        def p2_ohT(h_):
            b_, q = h_ // 2, h_ % 2
            oht2[h_] = op("vector", "oT", lambda e: e.tensor_scalar(ohTb[q], rowR[:, b_ % 2, 1024 * q:1024 * q + 1024].rearrange("p (t n) -> p t n", n=128),
                          pidx[:, 0:1], None, ALU.is_equal), rt2[b_], prt[T - 1], redt[T - 1], redt[T - 2], redt[T - 3], redt[T - 4], qt[T - 1], eot[(2 * NB - 1, "m")], mgt.get(8 * h_ - 9), oh2.get((h_ - 2, "m")))

        def p2_mg(t):
            h_, j = t // 8, t % 8
            if t % 16 == 0:
                load_regs(pe1, t // 16)
            for i in range(3):
                mgt[t] = op("tensor", "mg", lambda e, i=i: e.matmul(BK[6][:, 8 * j:8 * j + 8], ohTb[h_ % 2][:, j, :],
                            Mb[i][:, bass.ds(win(e, pe1, t), 1), :], start=(i == 0), stop=(i == 2)), oht2[h_], lst.get(h_ - 1), mb, pass1)

        def p2_p(h_):
            lh = L[:, h_ // 2, :, 8 * (h_ % 2):8 * (h_ % 2) + 8]
            lst[h_] = op("vector", "lp", lambda e: e.tensor_tensor(lh, lh, BK[6][:, 0:64].rearrange("p (t h) -> p h t", h=8), ALU.subtract),
                         mgt[8 * h_ + 7], mx_all)

        def p2_ex(h_):
            lh = L[:, h_ // 2, :, 8 * (h_ % 2):8 * (h_ % 2) + 8]
            pt[h_] = op("scalar", "ex", lambda e: e.activation(lh, lh, ACT.Exp), lst[h_])

        def p2_oh(h_):
            bank = BK[7].bitcast(bf16)
            for j in range(8):
                m = op("tensor", "tv", lambda e, j=j: e.transpose(bank[:, 128 * j:128 * j + 128], ohTb[h_ % 2][:, j, :], identb), oht2[h_], oh2.get(h_ - 1), mb, pass1)
            oh2[(h_, "m")] = m

        def p2_ohe(h_, q):
            bank = BK[7].bitcast(bf16).rearrange("p (t n) -> p t n", n=128)
            oh2[h_] = op("scalar", "tve", lambda e: e.copy(oh[h_ % 2][:, 4 * q:4 * q + 4, :], bank[:, 4 * q:4 * q + 4, :]), oh2[(h_, "m")], yt.get(8 * h_ - 13 + 4 * q), pass1)

        def heads(v, h0, h1):
            return v[:, 65 * h0:65 * h1].rearrange("p (h d) -> p h d", d=65)

        def p2_pv(t):
            ph = L[:, t // 16, :, t % 16]
            w_ = [vt[t], pt[t // 8], yt.get(t - PV), pass1]
            pvt[t] = [op("vector", "pv", lambda e: e.tensor_tensor(heads(pv[t % PV], 0, HA2), heads(Vr[t % KR], 0, HA2),
                         ph[:, 0:HA2].rearrange("p (h a) -> p h a", a=1).broadcast_to([128, HA2, 65]), ALU.mult), w_)]
            for h in range(HA2, 8):
                m = op("scalar", "pa", lambda e, h=h: e.activation(heads(pv[t % PV], h, h + 1), heads(Vr[t % KR], h, h + 1), ACT.Copy,
                       scale=ph[:, h:h + 1]), w_)
            pvt[t].append(m)
            o = oh[(t // 8) % 2][:, t % 8, :]
            for q in range(2):
                yt[t] = op("tensor", "yt", lambda e, q=q: e.matmul(YB[t % 3][:, 512 * q:512 * q + 260], o, pv[t % PV][:, 260 * q:260 * q + 260],
                           start=True, stop=True), pvt[t], oh2[t // 8], ya.get(t - 3), pass1)

        def p2_ya(t):
            if t % 16 == 0:
                load_regs(dv1, t // 16)

            def f(e):
                yw = Yall[:, bass.ds(win(e, dv1, t), 1), :].rearrange("p a (q n) -> p (a q) n", q=2)
                return e.tensor_tensor(yw, yw, YB[t % 3].rearrange("p (q n) -> p q n", q=2)[:, :, 0:260], ALU.add)
            ya[t] = op("vector", "ya", f, yt[t], ya.get(t - 1), y0)

        m_ = op("vector", "mb", lambda e: e.tensor_copy(Mb[0], Mall[:, :, :]), pass1)
        m_ = op("vector", "mb", lambda e: e.tensor_tensor(Mr, Mall[:, :, :], Mb[0], ALU.subtract), m_)
        m_ = op("vector", "mb", lambda e: e.tensor_copy(Mb[1], Mr), m_)
        m_ = op("vector", "mb", lambda e: e.tensor_tensor(Mb[2], Mr, Mb[1], ALU.subtract), m_)
        mb = [m_, op("vector", "mb", lambda e: e.tensor_copy(identb, ident[:, :]), pass1)]
        for b_ in range(2):
            rows2(b_, rt2, "r", [oht[2 * NB - 1]])
        jobs.clear()
        for b_ in range(2, NB):
            job(16 * b_ - 22, lambda b_=b_: rows2(b_, rt2, "r", [oht2[2 * b_ - 3]]))
        for h_ in range(2 * NB):
            job(8 * h_ - 15.6, lambda h_=h_: p2_ohT(h_))
            for j in range(8):
                job(8 * h_ - 14.2 + 0.5 * j, lambda t=8 * h_ + j: p2_mg(t))
            job(8 * h_ - 9.1, lambda h_=h_: p2_p(h_))
            job(8 * h_ - 6.9, lambda h_=h_: p2_ex(h_))
            job(8 * h_ - 7.3, lambda h_=h_: p2_oh(h_))
            job(8 * h_ - 5.3, lambda h_=h_: p2_ohe(h_, 0))
            job(8 * h_ - 2.3, lambda h_=h_: p2_ohe(h_, 1))
        for t in range(T):
            job(t, lambda t=t: p2_pv(t))
            job(t + 2.3, lambda t=t: p2_ya(t))
            if t + KR < T:
                job(t + 0.1, lambda t=t: gather_v(t + KR))
        in_slots(jobs)
        pass2 = [ya[T - 1], yt[T - 1], pvt[T - 1], pt[2 * NB - 1], oh2[2 * NB - 1]]

        d = carve(R2)
        e_ = carve(R3)
        WoS = d(2048).rearrange("p (c n) -> p c n", c=4)
        XR = 8
        SR = 6
        xr = [d(512) for _ in range(XR)]
        yn = [d(512) for _ in range(2)]
        yT = [d_(512).rearrange("p (c n) -> p c n", c=4) for d_ in (d, d, e_, e_)]
        xn = [e_(512) for _ in range(4)]
        h1 = [e_(512) for _ in range(3)]
        h2 = [e_(512) for _ in range(3)]
        FT = e_(512, bf16)
        sc = [e_(192) for _ in range(SR)]
        yd = [e_(16) for _ in range(2)]
        w16 = e_(64).rearrange("p (a n) -> p a n", a=4)
        ft0 = op("vector", "w", lambda e: e.memset(FT, 0.0), pass2)
        wo_t = dma("sync", "wo", lambda e: e.dma_start(WoS, wo.rearrange("(c p) n -> p c n", p=128)), pass2)
        iw = op("vector", "w", lambda e: e.tensor_scalar(w16, iotaF[:, 0:16].rearrange("p (a n) -> p a n", a=1).broadcast_to([128, 4, 16]), -1.0, 16.0, ALU.mult, ALU.add), pass2)

        xt3, ynt, yTt, ot, x1t, xnt, outt = {}, {}, {}, {}, {}, {}, {}
        o_all = []
        res = {}

        def f_load(w):
            n = rows_of[w]
            xt3[w] = dma("sync", f"xt{w % XR}", lambda e: e.dma_start(xr[w % XR][0:n, :], x[128 * w:128 * w + n, :]), outt.get(w - XR), pass2)

        def f_y(w):
            n, k = rows_of[w], w % 2
            s = yd[k]
            y = Yall[0:n, w, :].rearrange("p (h d) -> p h d", d=65)
            u = op("vector", "fy", lambda e: e.tensor_scalar(s[0:n, 0:8], y[:, :, 64], 1e-30, None, ALU.max), pass2, ynt.get(w - 2))
            u = op("vector", "fy", lambda e: e.reciprocal(s[0:n, 8:16], s[0:n, 0:8]), u)
            ynt[w] = op("vector", "fy", lambda e: e.tensor_tensor(yn[k][0:n, :].rearrange("p (h d) -> p h d", h=8), y[:, :, 0:64],
                        s[0:n, 8:16].rearrange("p (h a) -> p h a", a=1).broadcast_to([n, 8, 64]), ALU.mult), u, yTt.get((w - 2, "T")))

        def f_yT(w):
            n, k = rows_of[w], w % 2
            for c in range(4):
                last = op("tensor", "ft", lambda e, c=c: e.transpose(BK[0][:, 128 * c:128 * c + n], yn[k][0:n, 128 * c:128 * c + 128], ident[0:n, 0:n]),
                          ynt[w], yTt.get(w - 1), pass2)
            yTt[(w, "T")] = last
            yTt[w] = op("scalar", "fa", lambda e: e.copy(yT[w % 4][:, :, 0:n], BK[0][:, :].rearrange("p (c n) -> p c n", c=4)[:, :, 0:n]), last, ot.get(w - 4))

        def f_wo(w):
            n, k = rows_of[w], w % 2
            for c in range(4):
                op("tensor", "fo", lambda e, c=c: e.matmul(BK[1 + k][0:n, :], yT[w % 4][:, c, 0:n], WoS[:, c, :], start=(c == 0), stop=False), yTt[w], wo_t, c_bo, x1t.get(w - 2))
            ot[w] = op("tensor", "fo", lambda e: e.matmul(BK[1 + k][0:n, :], ones[0:3, 0:n], boS[0:3, :], start=False, stop=True))

        def f_x1(w):
            n, k, xx = rows_of[w], w % 2, xr[w % XR]
            x1t[w] = op("vector", "fl", lambda e: e.tensor_tensor(xx[0:n, :], xx[0:n, :], BK[1 + k][0:n, :], ALU.add), ot[w], xt3[w])

        def chain(eng, stream, key, *first):
            at = {"t": list(first)}

            def step(fn, *more, eng=eng, stream=stream, keep=None, side=False):
                def f():
                    t_ = op(eng, stream, fn, at["t"], *more)
                    if not side:
                        at["t"] = t_
                    if keep is not None:
                        keep[0][keep[1]] = t_
                return f
            return step, at

        def zipped(*lists):
            for i_ in range(max(len(l_) for l_ in lists)):
                for l_ in lists:
                    if i_ < len(l_):
                        l_[i_]()

        def parts_of(w):
            return sc[w % SR][:, 144:180].bitcast(bf16)

        def f_ln(w):
            n, k = rows_of[w], w % 2
            xx, xo, s = xr[w % XR], xn[w % 4], sc[w % SR]
            st, _ = chain("vector", "fl", w, x1t[w])
            fv = s[0:n, 104:112].rearrange("p (q f) -> p q f", q=2)
            nt = {"w": iw}
            Gs = parts_of(w)[0:n].rearrange("p (q i j f) -> p q i j f", q=2, i=3, j=3)
            fr = s[0:n, 180:188].rearrange("p (q f) -> p q f", q=2)
            fb, frb = [v.rearrange("p q (a f) -> p q a f", a=1).broadcast_to([n, 2, 3, 4]) for v in (fv, fr)]
            mk, ad, su = s[0:n, 112:113], s[0:n, 113:114], s[0:n, 114:115]

            def after(fn, keys, keep):
                def f():
                    nt[keep] = op("vector", "fl", fn, [nt[q_] for q_ in keys])
                return f
            steps = [
                st(lambda e: e.bn_stats(st6[0:n, k, :], xx[0:n, :])),
                st(lambda e: e.bn_aggr(mv[0:n, k, :], st6[0:n, k, :])),
                st(lambda e: e.tensor_scalar(rs[0:n, k, 0:1], mv[0:n, k, 1:2], 1e-5, None, ALU.add)),
                st(lambda e: e.activation(rs[0:n, k, 1:2], rs[0:n, k, 0:1], ACT.Sqrt), eng="scalar", stream="l2a"),
                st(lambda e: e.reciprocal(rs[0:n, k, 0:1], rs[0:n, k, 1:2])),
                st(lambda e: e.tensor_scalar(xo[0:n, :], xx[0:n, :], mv[0:n, k, 0:1], rs[0:n, k, 0:1], ALU.subtract, ALU.mult), res.get(w - SR), xnt.get(w - 4), xnt.get((w - 4, "s")), keep=(nt, "x")),
                st(lambda e: e.tensor_tensor(xx[0:n, :], xx[0:n, :], xo[0:n, :], ALU.add), eng="gpsimd", stream="fg", side=True, keep=(xnt, (w, "s"))),
                after(lambda e: e.scalar_tensor_tensor(s[0:n, 32:96].rearrange("p (a n) -> p a n", a=4), xo[0:n, 16:80].rearrange("p (a n) -> p a n", a=4), 0.5,
                      w16[0:n, :, :], ALU.is_gt, ALU.mult), ("x", "w"), "m"),
                after(lambda e: e.tensor_scalar(s[0:n, 112:115], xo[0:n, 0:3], 0.5, None, ALU.is_gt), ("x",), "k"),
                after(lambda e: e.tensor_reduce(s[0:n, 96:100], s[0:n, 32:96].rearrange("p (a n) -> p a n", a=4), AX.X, ALU.max), ("m",), "r"),
                after(lambda e: e.tensor_copy(fv[:, :, 2:4], xo[0:n, 105:107].rearrange("p (a f) -> p a f", a=1).broadcast_to([n, 2, 2])), ("x",), "o"),
                after(lambda e: e.tensor_scalar(s[0:n, 100:104], s[0:n, 96:100], -1.0, 16.0, ALU.mult, ALU.add), ("r",), "i"),
                after(lambda e: e.tensor_tensor(s[0:n, 115:116], mk, ad, ALU.mult), ("k",), "a"),
                after(lambda e: e.scalar_tensor_tensor(fv[:, :, 0:2].rearrange("p q f -> p f q"), s[0:n, 96:100].rearrange("p (f q) -> p f q", f=2), 0.0,
                      s[0:n, 100:104].rearrange("p (f q) -> p f q", f=2), ALU.is_gt, ALU.mult), ("i",), "f"),
                after(lambda e: e.tensor_tensor(s[0:n, 119:120], mk, s[0:n, 115:116], ALU.subtract), ("a",), "b"),
                after(lambda e: e.tensor_tensor(s[0:n, 116:117], s[0:n, 119:120], su, ALU.mult), ("b",), "c"),
                after(lambda e: e.tensor_tensor(s[0:n, 117:118], s[0:n, 115:116], s[0:n, 116:117], ALU.add), ("c",), "d"),
                after(lambda e: e.tensor_scalar(s[0:n, 118:119], s[0:n, 117:118], 2.0, None, ALU.mult), ("d",), "e"),
                after(lambda e: e.tensor_copy(Gs[:, :, :, 0, :], fb), ("f", "o"), "g0"),
                after(lambda e: e.tensor_tensor(fr, fv, Gs[:, :, 0, 0, :], ALU.subtract), ("g0",), "g1"),
                after(lambda e: e.tensor_copy(Gs[:, :, :, 1, :], frb), ("g1",), "g2"),
                after(lambda e: e.tensor_tensor(Gs[:, :, :, 2, :], frb, Gs[:, :, :, 1, :], ALU.subtract), ("g2",), "g3"),
            ]

            def close():
                xnt[w] = [nt["g3"]]
                xnt[(w, "m")] = [nt["e"]]
            return steps + [close]

        h1t, h2t, l3 = {}, {}, {}

        def f_ffn(g):
            ws = [w for w in (2 * g, 2 * g + 1) if w < W]
            last = None
            FB = BK[3].bitcast(bf16)
            for i, w in enumerate(ws):
                n, s = rows_of[w], sc[w % SR]
                for q in range(2):
                    last = op("tensor", "fq", lambda e, i=i, q=q, n=n, w=w: e.transpose(FB[0:36, 256 * i + 128 * q:256 * i + 128 * q + n], parts_of(w)[0:n, 36 * q:36 * q + 36],
                              identb[0:n, 0:n]), xnt[w], h1t.get((g - 1, "f")))
            evs = []
            for i, w in enumerate(ws):
                n = rows_of[w]
                v = FB[0:36, 256 * i:256 * i + 256].rearrange("p (q n) -> p q n", q=2)[:, :, 0:n]
                o = FT[0:36, 256 * i:256 * i + 256].rearrange("p (q n) -> p q n", q=2)[:, :, 0:n]
                evs.append(op("scalar", "fa", lambda e, o=o, v=v: e.copy(o, v), last, h1t.get((g - 1, "m")), ft0))
            h1t[(g, "f")] = evs[-1]
            h1t[(g, "e")] = evs

        def f_h1(g):
            ws = [w for w in (2 * g, 2 * g + 1) if w < W]
            evs = h1t[(g, "e")]
            C = 256 * len(ws)
            mm = []
            for k_, (c0, m_) in enumerate(((0, 128), (128, 128), (256, 64))):
                mm.append(op("tensor", "h1", lambda e, k_=k_, c0=c0, m_=m_: e.matmul(BK[4 + k_][0:m_, 0:C], W0b[0:36, c0:c0 + m_], FT[0:36, 0:C], start=True, stop=True),
                             evs, wt, h2t.get((g - 1, k_))))
            h1t[(g, "m")] = mm[-1]
            r = []
            for k_, m_ in enumerate((128, 128, 64)):
                r.append(op("scalar", "fa", lambda e, k_=k_, m_=m_: e.activation(h1[k_][0:m_, 0:C], BK[4 + k_][0:m_, 0:C], ACT.Relu, bias=b01[0:m_, k_:k_ + 1]),
                            mm[k_], h2t.get((g - 1, "mm"))))
            h1t[(g, "r")] = r

        def f_h2(g, between):
            ws = [w for w in (2 * g, 2 * g + 1) if w < W]
            r = h1t[(g, "r")]
            C = 256 * len(ws)
            m2 = []
            for k_, terms in enumerate((((W1a[:, 0:128], 0, 128), (W1b[0:64, 0:128], 2, 64)),
                                        ((W1s[:, 0:128], 1, 128), (W1b[0:64, 128:256], 2, 64)),
                                        ((W1a[:, 128:192], 0, 128), (W1s[:, 128:192], 1, 128), (W1b[0:64, 256:320], 2, 64)))):
                m_ = 64 if k_ == 2 else 128
                for i, (lw, hi_, kk) in enumerate(terms):
                    t_ = op("tensor", "h2", lambda e, k_=k_, lw=lw, hi_=hi_, kk=kk, i=i, m_=m_, nt=len(terms): e.matmul(
                        BK[4 + k_][0:m_, 0:C], lw, h1[hi_][0:kk, 0:C], start=(i == 0), stop=(i == nt - 1)), r)
                m2.append(t_)
                h2t[(g, k_)] = op("scalar", "fa", lambda e, k_=k_, m_=m_: e.activation(h2[k_][0:m_, 0:C], BK[4 + k_][0:m_, 0:C], ACT.Relu, bias=b01[0:m_, 3 + k_:4 + k_]),
                                  m2[k_], l3.get(g - 1))
                if k_ == 1:
                    between()
            h2t[(g, "mm")] = m2[-1]

        def f_out(g):
            ws = [w for w in (2 * g, 2 * g + 1) if w < W]
            for i, w in enumerate(ws):
                n = rows_of[w]
                for q in range(2):
                    c0 = 256 * i + 128 * q
                    for k_, kk in enumerate((128, 128, 64)):
                        t_ = op("tensor", "h3", lambda e, k_=k_, kk=kk, c0=c0, n=n, i=i, q=q: e.matmul(BK[7][0:n, 8 * i + 4 * q:8 * i + 4 * q + 4], h2[k_][0:kk, c0:c0 + n],
                                W2t[0:kk, 4 * k_:4 * k_ + 4], start=(k_ == 0), stop=(k_ == 2)), h2t[(g, 2)], h2t[(g, 0)], h2t[(g, 1)], wt,
                                res.get(2 * g - 1), res.get(2 * g - 2))
            l3[g] = t_

        def f_posts(g):
            zipped(*[f_post(g, i, w) for i, w in enumerate(pair(g))])

        def f_post(g, i, w):
            n, s, xx = rows_of[w], sc[w % SR], xr[w % XR]
            r4 = s[0:n, 124:132].rearrange("p (q c) -> p q c", q=2)
            st, at = chain("vector", "fz", w, l3[g], xnt[(w, "m")])
            vs = {}
            steps = [
                st(lambda e: e.tensor_tensor(r4, BK[7][0:n, 8 * i:8 * i + 8].rearrange("p (q c) -> p q c", q=2),
                   b2r[0:n, :].rearrange("p (a c) -> p a c", a=1).broadcast_to([n, 2, 4]), ALU.add), wt),
                st(lambda e: e.tensor_scalar(r4[:, :, 2:4], r4[:, :, 2:4], s[0:n, 116:117], None, ALU.mult)),
                st(lambda e: e.scalar_tensor_tensor(r4[:, :, 0:2], r4[:, :, 0:2], s[0:n, 115:116], r4[:, :, 2:4], ALU.mult, ALU.add)),
                st(lambda e: e.tensor_scalar(r4[:, :, 0:2], r4[:, :, 0:2], 0.0, 15.0, ALU.max, ALU.min)),
                st(lambda e: e.tensor_scalar(r4[:, :, 0:2], r4[:, :, 0:2], 12582912.0, 12582912.0, ALU.add, ALU.subtract))]
            for q in range(2):
                steps.append(st(lambda e, q=q: e.tensor_scalar(s[0:n, 16 * q:16 * q + 16], iotaF[0:n, 0:16], r4[:, q, 0:1], s[0:n, 118:119],
                             ALU.is_equal, ALU.mult), side=True, keep=(vs, q)))
            steps.append(st(lambda e: e.tensor_scalar(s[0:n, 32:33], r4[:, 1, 1:2], 0.5, s[0:n, 117:118], ALU.is_gt, ALU.mult), side=True, keep=(vs, 2)))

            def fin():
                res[w] = op("vector", "fz", lambda e: e.tensor_tensor(xx[0:n, 128:161], xx[0:n, 128:161], s[0:n, 0:33], ALU.add), list(vs.values()), xnt[(w, "s")])
                outt[w] = dma("sync", f"o{w % XR}", lambda e: e.dma_start(out[128 * w:128 * w + n, :], xx[0:n, :]), res[w], xnt[(w, "s")])
                o_all.append(outt[w])
            return steps + [fin]

        for w in range(XR):
            f_load(w)
        G = (W + 1) // 2

        def pair(g):
            return [w for w in (2 * g, 2 * g + 1) if w < W]

        for w in pair(0):
            f_y(w)
        for w in pair(0):
            f_yT(w)
        for w in pair(1):
            f_y(w)
        for w in pair(0):
            f_wo(w)
        for w in pair(1):
            f_yT(w)
        for w in pair(2):
            f_y(w)
        for w in pair(0):
            f_x1(w)
        zipped(*[f_ln(w) for w in pair(0)])
        for w in pair(1):
            f_wo(w)
        for w in pair(2):
            f_yT(w)
        for w in pair(3):
            f_y(w)
        f_ffn(0)
        q_ = P.queues["tensor"]
        for g in range(G):
            n1, n2, n3 = pair(g + 1), pair(g + 2), pair(g + 3)
            for w in n1:
                f_x1(w)
            cut = [len(q_)]
            f_h1(g)
            cut.append(len(q_))
            lists = [f_ln(w) for w in n1]
            if n1:
                zipped(*[l_[0:4] for l_ in lists])
            if g:
                f_posts(g - 1)
            if n2:
                f_wo(n2[0])
                few, full = q_[cut[0]:cut[1]], q_[cut[1]:]
                q_[cut[0]:] = [few[0], full[0], few[1]] + full[1:3] + [few[2]] + full[3:]
            if n3:
                f_yT(n3[0])
            f_h2(g, lambda: f_yT(n3[1]) if len(n3) > 1 else None)
            cut = [len(q_)]
            if len(n2) > 1:
                f_wo(n2[1])
            if n1:
                zipped(*[l_[4:] for l_ in lists])
            cut.append(len(q_))
            if n1:
                f_ffn(g + 1)
            f_out(g)
            if len(n2) > 1:
                full, few = q_[cut[0]:cut[1]], q_[cut[1]:]
                q_[cut[0]:] = full[0:2] + few[0:6] + full[2:3] + few[6:10] + full[3:4] + few[10:13] + full[4:] + few[13:]
            for w in pair(g + 4):
                f_y(w)
            if g:
                for w in n3:
                    f_load(w)
        f_posts(G - 1)
        P.plain("sync", None, o_all)

        block = ctx.enter_context(nc.Block())

        @block.sync
        def _(e):
            P.emit("sync", e)

        @block.gpsimd
        def _(e):
            P.emit("gpsimd", e)

        @block.scalar
        def _(e):
            P.emit("scalar", e)

        @block.vector
        def _(e):
            P.emit("vector", e)

        @block.tensor
        def _(e):
            P.emit("tensor", e)


_INS = ['x', 'src', 'dst', 'edge_attr_8', 'L0_gnn_Wq', 'L0_gnn_bq', 'L0_gnn_Wk', 'L0_gnn_bk', 'L0_gnn_Wv', 'L0_gnn_bv',
        'L0_gnn_Wo', 'L0_gnn_bo', 'L0_ffn_Wa', 'L0_ffn_ba', 'L0_ffn_Ws', 'L0_ffn_bs']
_OUTS = [((6250, 512), 'float32')]


def kernel(**inputs):
    import numpy as _np
    import concourse.bacc as _bacc
    from concourse import mybir as _mybir
    from concourse.bass_utils import run_bass_kernel_spmd as _run

    nc = _bacc.Bacc("TRN2", target_bir_lowering=False, num_devices=1)
    arrays, args = {}, []
    for name in _INS:
        a = _np.asarray(inputs[name])
        if name in ('L0_ffn_Wa', 'L0_ffn_Ws'):
            a = a.transpose(0, 2, 1)
        a = _np.ascontiguousarray(a)
        arrays[f"in_{name}_dram"] = a
        args.append(nc.dram_tensor(f"in_{name}_dram", a.shape, _mybir.dt.from_np(a.dtype), kind="ExternalInput").ap())
    for i, (shape, dtype) in enumerate(_OUTS):
        args.append(nc.dram_tensor(f"out_{i}_dram", shape, _mybir.dt.from_np(_np.dtype(dtype)), kind="ExternalOutput").ap())
    build(nc, *args)
    r = _run(nc, [arrays], core_ids=[0])
    return r.results[0]["out_0_dram"]
```
